# Optimizing a Trainium2 kernel written in Bass

```python
import numpy as np
import jax
import jax.numpy as jnp

def _softmax(x, axis=-1):
    return jax.nn.softmax(x, axis=axis)

def _gelu(x):
    return jax.nn.gelu(x, approximate=True)

def _silu(x):
    return jax.nn.silu(x)

def _sigmoid(x):
    return jax.nn.sigmoid(x)

def _layernorm(x, axis=-1, eps=1e-05):
    m = jnp.mean(x, axis=axis, keepdims=True)
    v = jnp.var(x, axis=axis, keepdims=True)
    return (x - m) / jnp.sqrt(v + eps)

def _scatter_add(tgt, idx, src, axis=0):
    return tgt.at[idx].add(src)

def _segment_sum(src, seg, n):
    return jax.ops.segment_sum(src, seg, n)
kernel_name = 'mk_vit_tower_cls_d1_tok_img512_r4_7e84dc'

def setup_inputs(seed: int=0):
    np.random.seed(seed)
    _w = jnp.asarray

    def _rec_inputs():
        import jax
        import jax.numpy as jnp
        _rk = jax.random.key(seed)
        x = 7.57192e-06 + 1.00007 * jax.random.normal(jax.random.fold_in(_rk, 1), (16, 96, 96, 3), jnp.float32)
        cls_tok = 0.02 * jax.random.normal(jax.random.fold_in(_rk, 5), (1, 1, 128), jnp.float32)
        return (x, cls_tok)
    x, cls_tok = _rec_inputs()

    def _L0_tok_setup():
        import jax, jax.numpy as jnp
        import numpy as np
        B, H, W, C = (64, 224, 224, 3)
        P, D = (16, 128)
        LN_EPS = 0.001

        def _shift4(x):
            pad = lambda a, spec: jnp.pad(a, spec)
            right = pad(x[:, :, :-1, :], ((0, 0), (0, 0), (1, 0), (0, 0)))
            left = pad(x[:, :, 1:, :], ((0, 0), (0, 0), (0, 1), (0, 0)))
            down = pad(x[:, :-1, :, :], ((0, 0), (1, 0), (0, 0), (0, 0)))
            up = pad(x[:, 1:, :, :], ((0, 0), (0, 1), (0, 0), (0, 0)))
            return [right, left, down, up]
        key = jax.random.key(seed)
        k0, k1, k2 = jax.random.split(key, 3)
        x = jax.random.normal(k0, (B, H, W, C), jnp.float32)
        conv_w = jax.random.normal(k1, (P, P, 5 * C, D), jnp.float32) * 0.02
        conv_b = jnp.zeros((D,), jnp.float32)
        gamma = jnp.ones((D,), jnp.float32)
        beta = jnp.zeros((D,), jnp.float32)
        dense_w = jax.random.normal(k2, (D, D), jnp.float32) * 0.02
        dense_b = jnp.zeros((D,), jnp.float32)
        return {'x': x, 'conv_w': conv_w, 'conv_b': conv_b, 'gamma': gamma, 'beta': beta, 'dense_w': dense_w, 'dense_b': dense_b}
    _L0_tok_all = _L0_tok_setup()
    _L0_tok_in = {k: v for k, v in _L0_tok_all.items() if k in ('conv_w', 'conv_b', 'gamma', 'beta', 'dense_w', 'dense_b')}
    del _L0_tok_all

    def _L0_attn_setup():
        import jax, jax.numpy as jnp
        import numpy as np
        THRE = 4.0
        EPS = 1e-05

        @jax.custom_vjp
        def spike(x):
            return jnp.floor(jnp.clip(x, 0.0, THRE) + 0.5)

        def _spike_fwd(x):
            return (spike(x), x)

        def _spike_bwd(x, g):
            return (g * ((x > 0) & (x < THRE)).astype(g.dtype),)
        spike.defvjp(_spike_fwd, _spike_bwd)
        key = jax.random.key(seed)
        k0, k1, k2 = jax.random.split(key, 3)
        B, N, C = (4, 256, 128)
        x = jax.random.normal(k0, (B, N, C), jnp.float32)
        Wqkv = jax.random.normal(k1, (3 * C, C), jnp.float32) * C ** (-0.5)
        gamma = jnp.ones((3 * C,), jnp.float32)
        beta = jnp.zeros((3 * C,), jnp.float32)
        Wproj = jax.random.normal(k2, (C, C), jnp.float32) * C ** (-0.5)
        bproj = jnp.zeros((C,), jnp.float32)
        return {'x': x, 'Wqkv': Wqkv, 'gamma': gamma, 'beta': beta, 'Wproj': Wproj, 'bproj': bproj}
    _L0_attn_all = _L0_attn_setup()
    _L0_attn_in = {k: v for k, v in _L0_attn_all.items() if k in ('Wqkv', 'gamma', 'beta', 'Wproj', 'bproj')}
    del _L0_attn_all

    def _L0_ffn_setup():
        import jax, jax.numpy as jnp
        import numpy as np
        K = 2
        EPS = 1e-06

        def _layernorm(x, gamma, beta):
            mu = jnp.mean(x, axis=-1, keepdims=True)
            var = jnp.mean(jnp.square(x - mu), axis=-1, keepdims=True)
            return (x - mu) * jax.lax.rsqrt(var + EPS) * gamma + beta
        key = jax.random.key(seed)
        ks = jax.random.split(key, 5)
        B, S, D, F, E = (8, 512, 128, 512, 8)
        x = jax.random.normal(ks[0], (B, S, D), dtype=jnp.float32)
        router_w = jax.random.normal(ks[1], (D, E), dtype=jnp.float32) * 0.02
        w1 = jax.random.normal(ks[2], (E, D, F), dtype=jnp.float32) * 0.02
        b1 = jnp.zeros((E, F), dtype=jnp.float32)
        w2 = jax.random.normal(ks[3], (E, F, D), dtype=jnp.float32) * 0.02
        b2 = jnp.zeros((E, D), dtype=jnp.float32)
        gamma = jnp.ones((E, D), dtype=jnp.float32)
        beta = jnp.zeros((E, D), dtype=jnp.float32)
        return {'x': x, 'router_w': router_w, 'w1': w1, 'b1': b1, 'w2': w2, 'b2': b2, 'gamma': gamma, 'beta': beta}
    _L0_ffn_all = _L0_ffn_setup()
    _L0_ffn_in = {k: v for k, v in _L0_ffn_all.items() if k in ('router_w', 'w1', 'b1', 'w2', 'b2', 'gamma', 'beta')}
    del _L0_ffn_all
    return {'x': x, 'cls_tok': cls_tok, 'L0_tok_conv_w': _L0_tok_in['conv_w'], 'L0_tok_conv_b': _L0_tok_in['conv_b'], 'L0_tok_gamma': _L0_tok_in['gamma'], 'L0_tok_beta': _L0_tok_in['beta'], 'L0_tok_dense_w': _L0_tok_in['dense_w'], 'L0_tok_dense_b': _L0_tok_in['dense_b'], 'L0_attn_Wqkv': _L0_attn_in['Wqkv'], 'L0_attn_gamma': _L0_attn_in['gamma'], 'L0_attn_beta': _L0_attn_in['beta'], 'L0_attn_Wproj': _L0_attn_in['Wproj'], 'L0_attn_bproj': _L0_attn_in['bproj'], 'L0_ffn_router_w': _L0_ffn_in['router_w'], 'L0_ffn_w1': _L0_ffn_in['w1'], 'L0_ffn_b1': _L0_ffn_in['b1'], 'L0_ffn_w2': _L0_ffn_in['w2'], 'L0_ffn_b2': _L0_ffn_in['b2'], 'L0_ffn_gamma': _L0_ffn_in['gamma'], 'L0_ffn_beta': _L0_ffn_in['beta']}

def reference(x, cls_tok, L0_tok_conv_w, L0_tok_conv_b, L0_tok_gamma, L0_tok_beta, L0_tok_dense_w, L0_tok_dense_b, L0_attn_Wqkv, L0_attn_gamma, L0_attn_beta, L0_attn_Wproj, L0_attn_bproj, L0_ffn_router_w, L0_ffn_w1, L0_ffn_b1, L0_ffn_w2, L0_ffn_b2, L0_ffn_gamma, L0_ffn_beta):
    import jax
    import jax.numpy as jnp

    def _L0_tok_ref(x, conv_w, conv_b, gamma, beta, dense_w, dense_b):
        import jax, jax.numpy as jnp
        import numpy as np
        B, H, W, C = (64, 224, 224, 3)
        P, D = (16, 128)
        LN_EPS = 0.001

        def _shift4(x):
            pad = lambda a, spec: jnp.pad(a, spec)
            right = pad(x[:, :, :-1, :], ((0, 0), (0, 0), (1, 0), (0, 0)))
            left = pad(x[:, :, 1:, :], ((0, 0), (0, 0), (0, 1), (0, 0)))
            down = pad(x[:, :-1, :, :], ((0, 0), (1, 0), (0, 0), (0, 0)))
            up = pad(x[:, 1:, :, :], ((0, 0), (0, 1), (0, 0), (0, 0)))
            return [right, left, down, up]
        xs = jnp.concatenate([x, *_shift4(x)], axis=-1)
        y = jax.lax.conv_general_dilated(xs, conv_w, window_strides=(P, P), padding='VALID', dimension_numbers=('NHWC', 'HWIO', 'NHWC')) + conv_b
        y = y.reshape(y.shape[0], -1, D)
        mu = jnp.mean(y, axis=-1, keepdims=True)
        var = jnp.mean(jnp.square(y - mu), axis=-1, keepdims=True)
        y = (y - mu) * jax.lax.rsqrt(var + LN_EPS) * gamma + beta
        return y @ dense_w + dense_b

    def _L0_attn_ref(x, Wqkv, gamma, beta, Wproj, bproj):
        import jax, jax.numpy as jnp
        import numpy as np
        THRE = 4.0
        EPS = 1e-05

        @jax.custom_vjp
        def spike(x):
            return jnp.floor(jnp.clip(x, 0.0, THRE) + 0.5)

        def _spike_fwd(x):
            return (spike(x), x)

        def _spike_bwd(x, g):
            return (g * ((x > 0) & (x < THRE)).astype(g.dtype),)
        spike.defvjp(_spike_fwd, _spike_bwd)
        B, N, C = x.shape
        H = 8
        hd = C // H
        scale = hd ** (-0.5)
        xs = spike(x)
        qkv = jnp.einsum('bnc,dc->bnd', xs, Wqkv)
        mu = qkv.mean(axis=(0, 1))
        var = qkv.var(axis=(0, 1))
        qkv = (qkv - mu) * jax.lax.rsqrt(var + EPS) * gamma + beta
        qkv = qkv.reshape(B, N, 3, H, hd).transpose(2, 0, 3, 1, 4)
        q = spike(qkv[0])
        k = spike(qkv[1])
        v = spike(qkv[2])
        attn = jnp.einsum('bhnd,bhmd->bhnm', q, k)
        attn = spike(attn)
        out = jnp.einsum('bhnm,bhmd->bhnd', attn, v) * scale
        out = out.transpose(0, 2, 1, 3).reshape(B, N, C)
        out = spike(out)
        return jnp.einsum('bnc,dc->bnd', out, Wproj) + bproj

    def _L0_ffn_ref(x, router_w, w1, b1, w2, b2, gamma, beta):
        import jax, jax.numpy as jnp
        import numpy as np
        K = 2
        EPS = 1e-06

        def _layernorm(x, gamma, beta):
            mu = jnp.mean(x, axis=-1, keepdims=True)
            var = jnp.mean(jnp.square(x - mu), axis=-1, keepdims=True)
            return (x - mu) * jax.lax.rsqrt(var + EPS) * gamma + beta
        B, S, D = x.shape
        E = w1.shape[0]
        xf = x.reshape(-1, D)
        logits = xf @ router_w
        gate_vals, idx = jax.lax.top_k(logits, K)
        gates = jax.nn.softmax(gate_vals, axis=-1)
        out = jnp.zeros_like(xf)
        for e in range(E):
            h = jax.nn.relu(xf @ w1[e] + b1[e]) @ w2[e] + b2[e]
            y = _layernorm(xf + h, gamma[e], beta[e])
            w = jnp.sum(jnp.where(idx == e, gates, 0.0), axis=-1)
            out = out + w[:, None] * y
        return out.reshape(B, S, D)
    h = _L0_tok_ref(x, L0_tok_conv_w, L0_tok_conv_b, L0_tok_gamma, L0_tok_beta, L0_tok_dense_w, L0_tok_dense_b)
    h = jnp.concatenate([jnp.broadcast_to(cls_tok, (h.shape[0], 1, h.shape[2])), h], axis=1)
    h = h + _L0_attn_ref(_layernorm(h, axis=-1), L0_attn_Wqkv, L0_attn_gamma, L0_attn_beta, L0_attn_Wproj, L0_attn_bproj)
    h = h + _L0_ffn_ref(_layernorm(h, axis=-1), L0_ffn_router_w, L0_ffn_w1, L0_ffn_b1, L0_ffn_w2, L0_ffn_b2, L0_ffn_gamma, L0_ffn_beta)
    return h

_drawn_inputs = setup_inputs


def setup_inputs(seed=0):
    import zlib

    import numpy as np

    out = dict(_drawn_inputs(seed))
    spreads = {'L0_tok_conv_b': (0.0, 0.1),
     'L0_tok_gamma': (1.0, 0.2),
     'L0_tok_beta': (0.0, 0.1),
     'L0_tok_dense_b': (0.0, 0.1),
     'L0_attn_gamma': (1.0, 0.2),
     'L0_attn_beta': (0.0, 0.1),
     'L0_attn_bproj': (0.0, 0.28),
     'L0_ffn_b1': (0.0, 0.8),
     'L0_ffn_b2': (0.0, 0.523),
     'L0_ffn_gamma': (1.0, 0.2),
     'L0_ffn_beta': (0.0, 0.521)}
    factors = {'L0_ffn_w1': 5.932, 'L0_ffn_w2': 4.905}
    for name, (base, spread) in spreads.items():
        noise = np.random.default_rng([zlib.crc32(name.encode()), seed]).standard_normal(out[name].shape)
        drawn = base * np.exp(spread * noise) if base else spread * noise
        out[name] = jnp.asarray(drawn.astype(out[name].dtype))
    for name, factor in factors.items():
        out[name] = (out[name] * factor).astype(out[name].dtype)
    return out
```

```python
from contextlib import ExitStack

import numpy as np

import concourse.bass as bass
from concourse import mybir

F32 = mybir.dt.float32
BF16 = mybir.dt.bfloat16
ALU = mybir.AluOpType
ACT = mybir.ActivationFunctionType
AX = mybir.AxisListType

B, IMG, CH, PATCH, D = 16, 96, 3, 16, 128
SIDE = IMG // PATCH
NP = SIDE * SIDE
NT = NP + 1
TOK = B * NT
PTOK = B * NP
TILES = -(-TOK // 128)
PAD = TILES * 128
HEADS, HD = 8, 16
E, F = 8, 512
FT = F // 128
BANK = 512
CUTS = ((0, BANK), (BANK, TOK))
PCUTS = ((0, BANK), (BANK, PTOK))
XROW = (IMG + 2) * CH
RNE = float(2 ** 23)
TIE = float(2 ** -22)
CAP = 4.0

V_B1, V_B2, V_CONVB, V_TG, V_TB, V_DENSEB, V_AG, V_AB, V_BPROJ, V_CLS, NV = 0, 32, 40, 41, 42, 43, 44, 47, 50, 51, 52

C_ID, C_CENTRE, C_NOT_LAST, C_NOT_FIRST, C_EVEN, C_ODD, C_RANK, C_TOP, C_BOTTOM, C_EPS, C_KEEP, CN = \
    0, 128, 256, 257, 258, 259, 260, 268, 269, 270, 273, 275
EPS = (1e-3, 1e-5, 1e-6)


def constants():
    p = np.arange(128)
    c = np.zeros((128, CN), np.float32)
    c[:, C_ID:C_ID + 128] = np.eye(128)
    c[:, C_CENTRE:C_CENTRE + 128] = np.eye(128) - 1.0 / 128
    c[:, C_NOT_LAST] = p % PATCH != PATCH - 1
    c[:, C_NOT_FIRST] = p % PATCH != 0
    c[:, C_EVEN] = (p // HD) % 2 == 0
    c[:, C_ODD] = (p // HD) % 2 == 1
    c[:, C_RANK:C_RANK + E] = E - np.arange(E)
    c[:, C_TOP] = p % SIDE != 0
    c[:, C_BOTTOM] = p % SIDE != SIDE - 1
    c[:, C_EPS:C_EPS + 3] = EPS
    c[:, C_KEEP] = c[:, C_EVEN] * HD ** -0.5
    c[:, C_KEEP + 1] = c[:, C_ODD] * HD ** -0.5
    return c


class Steps:

    def __init__(self, eng, sem):
        self.eng, self.sem, self.n = eng, sem, 0

    def mark(self, ins):
        self.n += 1
        ins.then_inc(self.sem, 1)

    def wait(self):
        self.eng.wait_ge(self.sem, self.n)

    def then(self, ins):
        self.mark(ins)
        self.wait()


def vit_layer(nc, consts, x, cls_tok, conv_w, conv_b, tok_g, tok_b, dense_w, dense_b, wqkv, attn_g, attn_b,
              wproj, bproj, router_w, w1, b1, w2, b2, ffn_g, ffn_b, out):
    with ExitStack() as ctx:
        def sb(name, shape, dt=F32):
            return ctx.enter_context(nc.sbuf_tensor(name, shape, dt))

        def sem(name):
            return ctx.enter_context(nc.semaphore(name))

        cst = sb("cst", [128, CN])
        ident = cst[:, C_ID:C_ID + 128]
        centre = cst[:, C_CENTRE:C_CENTRE + 128]
        evens = cst[:, C_KEEP:C_KEEP + 2]
        identb = sb("identb", [128, 128], BF16)
        ones = sb("ones", [128, 1])
        twos = sb("twos", [128, 128])
        vec = sb("vec", [64, 128])
        vecT = sb("vecT", [128, NV])
        vecC = sb("vecC", [128, NV])

        xin = sb("xin", [96, PATCH + 2, XROW])
        halo = sb("halo", [96, SIDE, CH, 4, PATCH])
        own_px = sb("own_px", [96, 6, SIDE, 128])
        XT = sb("XT", [128, 8, PTOK])
        wsh = sb("wsh", [128, 5, 2, CH * D])
        wk = sb("wk", [128, 8, D])
        wkc = sb("wkc", [128, 8, D])
        mean8 = sb("mean8", [128, 8])
        nmean8 = sb("nmean8", [128, 8])

        dw = sb("dw", [128, D])
        dwg = sb("dwg", [128, 2, D])
        c0 = sb("c0", [128, 2])
        ysb = sb("ysb", [128, PTOK])
        sq = sb("sq", [128, PAD])
        r_s = sb("r_s", [128, TILES])
        r_v = sb("r_v", [128, TILES])
        r_a = sb("r_a", [128, TILES])
        r_b = sb("r_b", [128, TILES])
        r_c = sb("r_c", [128, TILES])
        r_h = sb("r_h", [128, TILES])
        diag = sb("diag", [128, TILES, 128])
        h0 = sb("h0", [128, 2, PTOK])
        h1 = sb("h1", [128, PTOK])
        H = sb("H", [128, B, NT])
        Hc = sb("Hc", [128, B, NT])

        wt = sb("wt", [128, 4, D])
        wtT = sb("wtT", [128, 5, D])
        wrem = sb("wrem", [128, 2, 5, D])
        wpart = sb("wpart", [128, 3, 5, D], BF16)
        spk = sb("spk", [128, TOK])
        spk2 = sb("spk2", [128, TOK])
        xs = sb("xs", [128, TOK], BF16)
        bnst = sb("bnst", [128, 3, 2, 6])
        bnmv = sb("bnmv", [128, 3, 2])
        bn_s = sb("bn_s", [128, 8, 3])
        bn_scale = sb("bn_scale", [128, 3])
        bn_shift = sb("bn_shift", [128, 3])
        xt_room = XT[:, :, :].rearrange("p k n -> p (k n)")
        wsh_room = wsh[:, :, :, :].rearrange("p s m n -> p (s m n)")
        pre = xt_room[:, 0:3 * TOK].rearrange("p (k n) -> p k n", k=3)
        pre2 = wsh_room[:, 0:3 * TOK].rearrange("p (k n) -> p k n", k=3)
        qe = sb("qe", [128, 2, TOK], BF16)
        kvs = sb("kvs", [128, 2, PAD], BF16)
        vtok = sb("vtok", [128, B // 2, D], BF16)
        A = sb("A", [128, 4, B // 2, 2 * NT], BF16)
        av0 = sb("av0", [128, 4, 4, NT])
        av = sb("av", [128, B, NT])
        av2 = sb("av2", [128, TOK])
        os_ = sb("os", [128, TOK], BF16)

        X3 = sb("X3", [128, PAD])
        rw = sb("rw", [128, E])
        L = sb("L", [128, TILES, E])
        g = [sb(f"g{i}", [128, TILES, E]) for i in range(7)]
        gs = sb("gs", [128, 6, TILES])
        W8 = sb("W8", [128, TILES, E])
        wT = sb("wT", [E, PAD])
        fb = sb("fb", [E, D])
        gbc = sb("gbc", [128, E, D])
        w1r = sb("w1r", [128, E, F])
        w2r = sb("w2r", [128, E, FT, D])
        w2m = sb("w2m", [128, E, FT])
        w1s = sb("w1s", [128, 2, F])
        w2s = sb("w2s", [128, 2, FT, D])
        hs = xt_room[:, 3 * TOK:3 * TOK + FT * TOK].rearrange("p (f n) -> p f n", f=FT)
        ysum = sb("ysum", [128, PAD])
        junk = sb("junk", [128, TILES, 128], BF16)
        b1s = sb("b1s", [128, 2, FT])
        ssq = sb("ssq", [128, TILES])
        f_s = sb("f_s", [128, 6, TILES])
        frw = sb("frw", [128, TILES])
        z = sb("z", [128, TILES, D])
        acc = sb("acc", [128, TILES, D])

        PS = ctx.enter_context(nc.psum_tensor("PS", [128, 8, BANK], F32))

        def wide(bank, cols):
            return PS[:, bank:bank + 2, :].rearrange("p b n -> p (b n)")[:, 0:cols]

        def tile5(bank, t, rows=128):
            return PS[0:rows, bank + t // 4, (t % 4) * 128:(t % 4) * 128 + 128]

        s_cst, s_x, s_vec = sem("s_cst"), [sem("s_x0"), sem("s_x1")], sem("s_vec")
        s_halo_rows = sem("s_halo_rows")
        s_w = [sem(f"s_shift{i}") for i in range(5)]
        s_whalo, s_wt, s_dw, s_rw, s_w1, s_w2, s_gb = (sem(n) for n in
                                                      ("s_whalo", "s_wt", "s_dw", "s_rw", "s_w1", "s_w2", "s_gb"))
        pads = sem("pads")
        wpads = sem("wpads")
        tails = sem("tails")
        halo_ok = sem("halo_ok")
        px_act, px_dve = sem("px_act"), sem("px_dve")
        xt_ps, xt_act, xt_dve = sem("xt_ps"), sem("xt_act"), sem("xt_dve")
        small_ps, small_sb = sem("small_ps"), sem("small_sb")
        wk_ok, conv_ps, y_ok, sq_ok = sem("wk_ok"), sem("conv_ps"), sem("y_ok"), sem("sq_ok")
        dense_ok = sem("dense_ok")
        var_ps, v_ok, root_ok, diag_ok, bc_ps = sem("var_ps"), sem("v_ok"), sem("root_ok"), sem("diag_ok"), sem("bc_ps")
        t_ps, t_sb = sem("t_ps"), sem("t_sb")
        h0_ok, h_ok = sem("h0_ok"), sem("h_ok")
        wparts_ok, xs_ok = sem("wparts_ok"), sem("xs_ok")
        qkv_ps, bn_var, bn_root, bn_ok, pre_ok, spike_ok = (sem(n) for n in
                                                            ("qkv_ps", "bn_var", "bn_root", "bn_ok", "pre_ok", "spike_ok"))
        vt_ps, vt_sb, sc_ps, sc_sb, av_ps, os_ok = (sem(n) for n in
                                                    ("vt_ps", "vt_sb", "sc_ps", "sc_sb", "av_ps", "os_ok"))
        proj_ps, h2_ok, x3_ok = sem("proj_ps"), sem("h2_ok"), sem("x3_ok")
        h2t_ps, lg_ps, lg_sb, gap, gexp, gate_ok, wT_ps, wT_sb = (sem(n) for n in (
            "h2t_ps", "lg_ps", "lg_sb", "gap", "gexp", "gate_ok", "wT_ps", "wT_sb"))
        w2m_ok, w1_slot, w2_slot, b1_slot, out_ok, z_last = sem("w2m_ok"), sem("b1_slot"), sem("z_last"), sem("w1_slot"), sem("w2_slot"), sem("out_ok")
        g_ps, relu_ok, mm2_done, ysum_ok, turn_ps, ssq_ok, froot, z_ok, acc_ok, fch, ffac = (sem(n) for n in (
            "g_ps", "relu_ok", "mm2_done", "ysum_ok", "turn_ps", "ssq_ok", "froot", "z_ok", "acc_ok", "fch", "ffac"))
        beta_ps, beta_sb, s_out = sem("beta_ps"), sem("beta_sb"), sem("s_out")
        dve_own, pool_own, act_own = sem("dve_own"), sem("pool_own"), sem("act_own")

        def gather(copy, k):
            m, c = k // 3, k % 3
            pix = xin[:, 1 + 8 * m:9 + 8 * m, CH:CH + IMG * CH].rearrange("p r (j w c) -> p j r w c", w=PATCH, c=CH)
            return copy(own_px[:, k, :, :].rearrange("p j (r w) -> p j r w", w=PATCH), pix[:, :, :, :, c])

        block = ctx.enter_context(nc.Block())

        @block.sync
        def _(sp):
            nc.sync.dma_start(cst[:, :], consts).then_inc(s_cst, 16)
            bands = x.rearrange("b (i r) w c -> (b i) r (w c)", r=PATCH)
            sp.wait_ge(pads, 3)
            for m in range(2):
                nc.sync.dma_start(xin[:, 1 + 8 * m:9 + 8 * m, CH:CH + IMG * CH],
                                  bands[:, 8 * m:8 * m + 8, :]).then_inc(s_x[m], 16)
            nc.sync.dma_start(xin[1:96, 0, CH:CH + IMG * CH], bands[0:95, PATCH - 1, :]).then_inc(s_halo_rows, 16)
            nc.sync.dma_start(xin[0:95, PATCH + 1, CH:CH + IMG * CH], bands[1:96, 0, :]).then_inc(s_halo_rows, 16)
            wq = conv_w.rearrange("i j c d -> (i j) (c d)")
            sp.wait_ge(wpads, 4)
            for s, step in ((0, 0), (1, 1), (2, -1), (3, PATCH), (4, -PATCH)):
                cols = slice(3 * s * D, (3 * s + 3) * D)
                if step == 0:
                    nc.sync.dma_start(wsh[:, 0, :, :], wq[:, cols].rearrange("(m q) n -> q m n", m=2)).then_inc(s_w[s], 16)
                    continue
                for m in range(2):
                    lo, hi = max(0, 128 * m + step), min(256, 128 * m + 128 + step)
                    nc.sync.dma_start(wsh[lo - step - 128 * m:hi - step - 128 * m, s, m, :],
                                      wq[lo:hi, cols]).then_inc(s_w[s], 16)
            nc.sync.dma_start(wt[:, 0:3, :], wqkv.rearrange("(k p) c -> p k c", p=128)).then_inc(s_wt, 16)
            nc.sync.dma_start(wt[:, 3, :], wproj).then_inc(s_wt, 16)
            nc.sync.dma_start(dw[:, :], dense_w).then_inc(s_dw, 16)
            nc.sync.dma_start(rw[:, :], router_w).then_inc(s_rw, 16)
            nc.sync.dma_start(w2r[:, :, :, :], w2.rearrange("e (f p) d -> p e f d", p=128)).then_inc(s_w2, 16)
            nc.sync.dma_start(w1r[:, :, :], w1.rearrange("e p f -> p e f")).then_inc(s_w1, 16)
            nc.sync.dma_start(gbc[:, :, :].rearrange("p e d -> p (e d)"),
                              ffn_g.rearrange("e d -> (e d)").partition_broadcast(128)).then_inc(s_gb, 16)
            nc.sync.dma_start(fb[:, :], ffn_b).then_inc(s_gb, 16)

            rows = out.rearrange("b n d -> (b n) d")
            for t in range(TILES):
                sp.wait_ge(out_ok, t + 1)
                n = min(128, TOK - 128 * t)
                nc.sync.dma_start(rows[128 * t:128 * t + n, :], acc[0:n, t, :]).then_inc(s_out, 16)
            sp.wait_ge(s_out, 16 * TILES)

        @block.gpsimd
        def _(pool):
            nc.gpsimd.memset(xin[:, 0, :], 0.0).then_inc(pads, 1)
            nc.gpsimd.memset(xin[:, PATCH + 1, :], 0.0).then_inc(pads, 1)
            nc.gpsimd.memset(xin[:, 1:PATCH + 1, :].rearrange("p r (w c) -> p r w c", c=CH)[:, :, 0:IMG + 2:IMG + 1, :],
                             0.0).then_inc(pads, 1)
            nc.gpsimd.memset(wsh[96:128, 1, 1, :], 0.0).then_inc(wpads, 1)
            nc.gpsimd.memset(wsh[0:32, 2, 0, :], 0.0).then_inc(wpads, 1)
            nc.gpsimd.memset(wsh[96:128, 3, 1, :], 0.0).then_inc(wpads, 1)
            nc.gpsimd.memset(wsh[0:32, 4, 0, :], 0.0).then_inc(wpads, 1)
            sides = (conv_w[:, 0, 3:6, :], conv_w[:, PATCH - 1, 6:9, :], conv_w[0, :, 9:12, :], conv_w[PATCH - 1, :, 12:15, :])
            for s, w in enumerate(sides):
                nc.gpsimd.dma_start(wk[16 * s:16 * s + 16, 6:8, :], w[:, 0:3:2, :]).then_inc(s_whalo, 16)
                nc.gpsimd.dma_start(wk[64 + 16 * s:80 + 16 * s, 6, :], w[:, 1, :]).then_inc(s_whalo, 16)
            for row, v in ((V_B1, b1.rearrange("e (f p) -> (e f) p", p=128)), (V_B2, b2),
                           (V_CONVB, conv_b.rearrange("(a d) -> a d", a=1)), (V_TG, tok_g.rearrange("(a d) -> a d", a=1)),
                           (V_TB, tok_b.rearrange("(a d) -> a d", a=1)), (V_DENSEB, dense_b.rearrange("(a d) -> a d", a=1)),
                           (V_AG, attn_g.rearrange("(k d) -> k d", d=D)), (V_AB, attn_b.rearrange("(k d) -> k d", d=D)),
                           (V_BPROJ, bproj.rearrange("(a d) -> a d", a=1)), (V_CLS, cls_tok.rearrange("a b d -> (a b) d"))):
                nc.gpsimd.dma_start(vec[row:row + v.shape[0], :], v).then_inc(s_vec, 16)
            xw = xin[:, :, :].rearrange("p r (w c) -> p r w c", c=CH)
            pool.wait_ge(wpads, 4)
            pool.wait_ge(s_cst, 16)
            pool.wait_ge(s_x[0], 16)
            pool.wait_ge(s_x[1], 16)
            for side, col in ((0, 0), (1, PATCH + 1)):
                for c in range(CH):
                    nc.gpsimd.tensor_copy(
                        halo[:, :, c, side, :],
                        xw[:, 1:PATCH + 1, col:col + PATCH * (SIDE - 1) + 1:PATCH, c].rearrange("p r j -> p j r")
                    ).then_inc(halo_ok, 1)
            pool.wait_ge(s_halo_rows, 32)
            for side, row, mask in ((2, 0, C_TOP), (3, PATCH + 1, C_BOTTOM)):
                for c in range(CH):
                    nc.gpsimd.tensor_scalar(
                        halo[:, :, c, side, :],
                        xw[:, row, 1:IMG + 1, c].rearrange("p (j w) -> p j w", w=PATCH),
                        cst[0:96, mask:mask + 1], None, ALU.mult).then_inc(halo_ok, 1)
            pool.wait_ge(small_sb, 2)
            pool.wait_ge(tails, 8)
            nc.gpsimd.tensor_scalar(H[:, :, 0], sq[:, 0:B], 0.0, vecT[:, V_CLS:V_CLS + 1], ALU.mult, ALU.add).then_inc(h_ok, 1)
            nc.gpsimd.tensor_scalar(Hc[:, :, 0], sq[:, 0:B], 0.0, vecC[:, V_CLS:V_CLS + 1], ALU.mult, ALU.add).then_inc(h_ok, 1)

            def prepare(e, slot):
                nc.gpsimd.tensor_copy(w1s[:, slot, :], w1r[:, bass.ds(e, 1), :].rearrange("p o f -> p (o f)")).then_inc(w1_slot, 1)
                nc.gpsimd.tensor_tensor(w2s[:, slot, :, :], w2r[:, bass.ds(e, 1), :, :].rearrange("p o f d -> p (o f) d"),
                                        w2m[:, bass.ds(e, 1), :].rearrange("p o f -> p (o f)").unsqueeze(2).to_broadcast([128, FT, D]),
                                        ALU.subtract).then_inc(w2_slot, 1)
                nc.gpsimd.tensor_copy(b1s[:, slot, :], vecT[:, bass.ds(e * FT + V_B1, FT)]).then_inc(b1_slot, 1)

            def add(e):
                pool.wait_ge(z_ok, e + 2)
                nc.gpsimd.tensor_tensor(acc[:, :, :], acc[:, :, :], z[:, :, :], ALU.add).then_inc(acc_ok, 1)

            pool.wait_ge(s_w1, 16)
            pool.wait_ge(w2m_ok, 1)
            prepare(0, 0)
            prepare(1, 1)
            pool.wait_ge(z_ok, 1)
            with pool.Fori(0, E // 2 - 1) as i:
                for slot in range(2):
                    pool.wait_ge(mm2_done, i * (2 * FT) + (slot + 1) * FT)
                    prepare(i * 2 + (slot + 2), slot)
                    pool.wait_ge(acc_ok, i * 2 + (slot + 1))
                    add(i * 2 + slot)
            pool.wait_ge(acc_ok, E - 1)
            add(E - 2)

        @block.tensor
        def _(pe):
            pe.wait_ge(s_cst, 16)
            pe.wait_ge(s_vec, 160)
            nc.tensor.transpose(PS[:, 4, 0:NV], vec[0:NV, :], ident[0:NV, 0:NV]).then_inc(small_ps, 1)

            def turn(k, half):
                n = 2 * k + half
                if n >= 4:
                    pe.wait_ge(xt_act if half == 0 else xt_dve, n // 2 - 1)
                for j in range(3):
                    pj = 3 * half + j
                    if k < 6:
                        pix, rows = own_px[:, k, pj, :], 128
                    elif k == 6:
                        pix, rows = halo[:, pj, 0:2, :, :].rearrange("p c s i -> p (c s i)"), 128
                    else:
                        pix, rows = halo[:, pj, 2, :, :].rearrange("p s i -> p (s i)"), 64
                    mm = nc.tensor.transpose(PS[0:rows, n % 4, 96 * j:96 * j + 96], pix, ident[0:96, 0:96])
                mm.then_inc(xt_ps, 1)

            for k in range(6):
                pe.wait_ge(px_act if k % 3 == 0 else px_dve, 1 + k // 3 if k % 3 == 0 else k - k // 3)
                for half in range(2):
                    turn(k, half)
            pe.wait_ge(small_sb, 1)
            nc.tensor.matmul(PS[:, 4, 128:128 + NV], centre, vecT[:, :], start=True, stop=True).then_inc(small_ps, 1)
            pe.wait_ge(halo_ok, 12)
            for k in (6, 7):
                for half in range(2):
                    turn(k, half)
            for k in range(8):
                if k == 2:
                    pe.wait_ge(s_wt, 32)
                    for v in range(4):
                        mm = nc.tensor.transpose(PS[:, 5, 128 * v:128 * v + 128], wt[:, v, :], ident)
                    mm.then_inc(small_ps, 1)
                    pe.wait_ge(s_dw, 16)
                    pe.wait_ge(small_sb, 2)
                    nc.tensor.matmul(PS[:, 4, 200:201], dw[:, :], vecT[:, V_TB:V_TB + 1], start=True, stop=True).then_inc(small_ps, 1)
                    pe.wait_ge(small_sb, 4)
                    nc.tensor.matmul(PS[:, 4, 202:203], centre, c0[:, 0:1], start=True, stop=True).then_inc(small_ps, 1)
                pe.wait_ge(wk_ok, k + 1)
                pe.wait_ge(xt_act, k + 1)
                pe.wait_ge(xt_dve, k + 1)
                rows = 128 if k < 7 else 64
                for n, (a, b) in enumerate(PCUTS):
                    mm = nc.tensor.matmul(PS[:, 6 + n, 0:b - a], wkc[0:rows, k, :], XT[0:rows, k, a:b],
                                          start=(k == 0), stop=(k == 7))
            mm.then_inc(conv_ps, 1)
            def squares(n, bank):
                pe.wait_ge(sq_ok, n)
                for t in range(TILES):
                    mm = nc.tensor.matmul(PS[:, bank, t:t + 1], sq[:, 128 * t:128 * t + 128], ones[:, :], start=True, stop=True)
                mm.then_inc(var_ps, 1)

            def spread(n, bank):
                pe.wait_ge(diag_ok, n)
                for t in range(TILES):
                    mm = nc.tensor.matmul(tile5(bank, t), twos[:, :], diag[:, t, :], start=True, stop=True)
                mm.then_inc(bc_ps, 1)

            pe.wait_ge(y_ok, 1)
            pe.wait_ge(dense_ok, 2)
            for v in range(2):
                for n, (a, b) in enumerate(PCUTS):
                    mm = nc.tensor.matmul(PS[:, 2 * v + n, 0:b - a], dwg[:, v, :], ysb[:, a:b], start=True, stop=True)
                mm.then_inc(t_ps, 1)
            squares(1, 6)
            pe.wait_ge(small_sb, 5)
            spread(1, 4)
            squares(2, 6)
            spread(2, 4)
            pe.wait_ge(wparts_ok, 1)
            pe.wait_ge(xs_ok, 1)
            for which, bank in ((1, 0), (0, 2), (2, 6)):
                for n, (a, b) in enumerate(CUTS):
                    for part in range(3):
                        mm = nc.tensor.matmul(PS[:, bank + n, 0:b - a], wpart[:, part, which, :], xs[:, a:b],
                                              start=(part == 0), stop=(part == 2))
                mm.then_inc(qkv_ps, 1)

            def scores(rnd, banks):
                for p in range(4):
                    pr = 4 * rnd + p
                    for half in range(2):
                        col = NT * (2 * pr + half)
                        for hp in range(4):
                            mm = nc.tensor.matmul(
                                PS[64 * half:64 * half + 64, banks[hp], 2 * NT * p:2 * NT * p + 2 * NT],
                                kvs[32 * hp:32 * hp + 32, 0, col:col + 64], qe[32 * hp:32 * hp + 32, :, col:col + NT],
                                start=True, stop=True)
                mm.then_inc(sc_ps, 1)

            pe.wait_ge(spike_ok, 3)
            pe.wait_ge(pre_ok, 2)
            scores(0, (0, 1, 2, 3))
            pe.wait_ge(spike_ok, 4)
            for pr in range(B // 2):
                for half in range(2):
                    col = NT * (2 * pr + half)
                    mm = nc.tensor.transpose(PS[64 * half:64 * half + 64, 5, 64 * pr:64 * pr + 64].bitcast(BF16),
                                             kvs[:, 1, col:col + 64], identb[:, :])
            mm.then_inc(vt_ps, 1)
            pe.wait_ge(vt_sb, 1)
            pe.wait_ge(pre_ok, 3)
            scores(1, (4, 5, 6, 7))
            for rnd in range(2):
                pe.wait_ge(sc_sb, rnd + 1)
                for p in range(4):
                    pr = 4 * rnd + p
                    for half in range(2):
                        rows = slice(64 * half, 64 * half + NT)
                        for hp in range(4):
                            mm = nc.tensor.matmul(
                                PS[32 * hp:32 * hp + 32, 2 * rnd + half, 2 * NT * p:2 * NT * p + 2 * NT],
                                vtok[rows, pr, 32 * hp:32 * hp + 32], A[rows, hp, pr, :], start=True, stop=True)
                mm.then_inc(av_ps, 1)
            pe.wait_ge(os_ok, 1)
            for which, bank in ((4, 6), (3, 4)):
                for n, (a, b) in enumerate(CUTS):
                    for part in range(3):
                        mm = nc.tensor.matmul(PS[:, bank + n, 0:b - a], wpart[:, part, which, :], os_[:, a:b],
                                              start=(part == 0), stop=(part == 2))
                mm.then_inc(proj_ps, 1)
            squares(3, 0)
            spread(3, 2)
            pe.wait_ge(h2_ok, 2)
            for t in range(TILES):
                n = min(128, TOK - 128 * t)
                mm = nc.tensor.transpose(tile5(6, t, n), H[:, :, :].rearrange("p b n -> p (b n)")[:, 128 * t:128 * t + n], ident)
            mm.then_inc(h2t_ps, 1)
            pe.wait_ge(x3_ok, 1)
            pe.wait_ge(s_rw, 16)
            for t in range(TILES):
                mm = nc.tensor.matmul(PS[:, 0, 16 + E * t:16 + E * t + E], X3[:, 128 * t:128 * t + 128], rw[:, :], start=True, stop=True)
            mm.then_inc(lg_ps, 1)
            pe.wait_ge(lg_sb, 1)
            pe.wait_ge(bc_ps, 3)

            def first(slot, f):
                for n, (a, b) in enumerate(CUTS):
                    mm = nc.tensor.matmul(PS[:, 2 * (f % 2) + n, 0:b - a], w1s[:, slot, 128 * f:128 * f + 128], X3[:, a:b],
                                          start=True, stop=True)
                mm.then_inc(g_ps, 1)

            def second(slot, f):
                for n, (a, b) in enumerate(CUTS):
                    mm = nc.tensor.matmul(PS[:, 4 + n, 0:b - a], w2s[:, slot, f, :], hs[:, f, a:b],
                                          start=(f == 0), stop=(f == FT - 1))
                mm.then_inc(mm2_done, 1)

            def turn_back():
                for t in range(TILES):
                    mm = nc.tensor.transpose(tile5(6, t), ysum[:, 128 * t:128 * t + 128], ident)
                mm.then_inc(turn_ps, 1)

            def window(e, slot, begin=False, end=False):
                for f in range(FT):
                    pe.wait_ge(relu_ok, e * FT + (f + 1))
                    if f < 2:
                        first(slot, f + 2)
                    elif not end:
                        if f == 2:
                            pe.wait_ge(w1_slot, e + 2)
                        first(1 - slot, f - 2)
                    if f == 0:
                        pe.wait_ge(w2_slot, e + 1)
                        if not begin:
                            pe.wait_ge(ysum_ok, e)
                    second(slot, f)
                    if f == 1 and not begin:
                        pe.wait_ge(z_ok, e)
                        turn_back()

            pe.wait_ge(w1_slot, 1)
            first(0, 0)
            first(0, 1)
            window(0, 0, begin=True)
            with pe.Fori(0, E // 2 - 1) as i:
                window(i * 2 + 1, 1)
                window(i * 2 + 2, 0)
            window(E - 1, 1, end=True)
            pe.wait_ge(gate_ok, 1)
            for t in range(TILES):
                mm = nc.tensor.transpose(tile5(0, t, E), W8[:, t, :], ident)
            mm.then_inc(wT_ps, 1)
            pe.wait_ge(ysum_ok, E)
            pe.wait_ge(z_ok, E)
            turn_back()
            pe.wait_ge(s_gb, 32)
            pe.wait_ge(wT_sb, 1)
            for t in range(TILES):
                mm = nc.tensor.matmul(tile5(2, t), wT[:, 128 * t:128 * t + 128], fb[:, :], start=True, stop=True)
            mm.then_inc(beta_ps, 1)

        @block.scalar
        def _(act):
            for m in range(2):
                act.wait_ge(s_x[m], 16)
                gather(nc.scalar.copy, 3 * m).then_inc(px_act, 1)
            act.wait_ge(small_ps, 1)
            nc.scalar.copy(vecT[:, :], PS[:, 4, 0:NV]).then_inc(small_sb, 1)

            def evacuate(k):
                rows = 128 if k < 7 else 64
                act.wait_ge(xt_ps, 2 * k + 1)
                nc.scalar.copy(
                    XT[0:rows, k, :].rearrange("p (q j) -> p j q", j=SIDE)[:, 0:3, :],
                    PS[0:rows, 2 * k % 4, 0:288].rearrange("p (j q) -> p j q", j=3)).then_inc(xt_act, 1)

            for k in range(6):
                evacuate(k)
            act.wait_ge(small_ps, 2)
            nc.scalar.copy(vecC[:, :], PS[:, 4, 128:128 + NV]).then_inc(small_sb, 1)
            evacuate(6)
            evacuate(7)
            act.wait_ge(small_ps, 3)
            nc.scalar.copy(wtT[:, 0:4, :], PS[:, 5, :].rearrange("p (k c) -> p k c", k=4)).then_inc(small_sb, 1)
            act.wait_ge(small_ps, 4)
            nc.scalar.activation(c0[:, 0:1], PS[:, 4, 200:201], ACT.Identity,
                                 bias=vecT[:, V_DENSEB:V_DENSEB + 1]).then_inc(small_sb, 1)
            act.wait_ge(small_ps, 5)
            nc.scalar.copy(c0[:, 1:2], PS[:, 4, 202:203]).then_inc(small_sb, 1)
            act.wait_ge(conv_ps, 1)
            nc.scalar.activation(ysb[:, :], wide(6, PTOK), ACT.Identity, bias=vecC[:, V_CONVB:V_CONVB + 1]).then_inc(y_ok, 1)
            act.wait_ge(tails, 8)
            act.wait_ge(h_ok, 2)
            nc.scalar.activation(sq[:, 0:PTOK], wide(6, PTOK), ACT.Square, bias=vecC[:, V_CONVB:V_CONVB + 1]).then_inc(sq_ok, 1)

            def root(n):
                act.wait_ge(v_ok, n)
                nc.scalar.activation(r_s[:, :], r_v[:, :], ACT.Sqrt).then_inc(root_ok, 1)

            act.wait_ge(t_ps, 1)
            nc.scalar.copy(h0[:, 0, :], wide(0, PTOK)).then_inc(t_sb, 1)
            root(1)
            act.wait_ge(t_ps, 2)
            nc.scalar.copy(h0[:, 1, :], wide(2, PTOK)).then_inc(t_sb, 1)
            act.wait_ge(h0_ok, 1)
            nc.scalar.activation(Hc[:, :, 1:NT], h1[:, :].rearrange("p (b n) -> p b n", b=B), ACT.Identity,
                                 bias=c0[:, 1:2]).then_inc(h_ok, 1)
            act.wait_ge(h_ok, 3)
            nc.scalar.activation(sq[:, 0:TOK], Hc[:, :, :].rearrange("p b n -> p (b n)"), ACT.Square).then_inc(sq_ok, 1)
            root(2)
            act.wait_ge(h0_ok, 2)
            nc.scalar.activation(H[:, :, 1:NT], ysb[:, :].rearrange("p (b n) -> p b n", b=B), ACT.Identity,
                                 bias=c0[:, 0:1]).then_inc(h_ok, 1)
            act.wait_ge(bn_var, 1)
            nc.scalar.activation(bn_s[:, 0, :], bnmv[:, :, 1], ACT.Sqrt, bias=cst[:, C_EPS + 1:C_EPS + 2]).then_inc(bn_root, 1)
            act.wait_ge(bn_ok, 1)
            for which, bank in ((1, 0), (0, 2), (2, 6)):
                nc.scalar.activation(pre[:, which, :], wide(bank, TOK), ACT.Relu, scale=bn_scale[:, which:which + 1],
                                     bias=bn_shift[:, which:which + 1]).then_inc(pre_ok, 1)
            act.wait_ge(vt_ps, 1)
            nc.scalar.copy(vtok[:, :, :].rearrange("p r d -> p (r d)"), PS[:, 5, :].bitcast(BF16)).then_inc(vt_sb, 1)
            act.wait_ge(h2_ok, 1)
            nc.scalar.activation(sq[:, 0:TOK], Hc[:, :, :].rearrange("p b n -> p (b n)"), ACT.Square).then_inc(sq_ok, 1)
            root(3)
            act.wait_ge(h2t_ps, 1)
            nc.scalar.copy(acc[:, 0:4, :], PS[:, 6, :].rearrange("p (t d) -> p t d", d=D)).then_inc(acc_ok, 1)
            nc.scalar.copy(acc[0:TOK - 512, 4, :], PS[0:TOK - 512, 7, 0:D]).then_inc(z_ok, 1)
            act.wait_ge(gap, 1)
            nc.scalar.activation(gs[:, 3, :], gs[:, 2, :], ACT.Exp).then_inc(gexp, 1)
            act.wait_ge(gexp, 1)
            nc.scalar.activation(junk[:, 0, 0:1], cst[:, C_EPS:C_EPS + 1], ACT.Sqrt).then_inc(act_own, 1)

            def relu(e, slot, f, begin=False):
                act.wait_ge(g_ps, e * FT + (f + 1))
                if not begin:
                    act.wait_ge(mm2_done, e * FT + (f + 1 - FT))
                if f == 0:
                    act.wait_ge(b1_slot, e + 1)
                nc.scalar.activation(hs[:, f, :], wide(2 * (f % 2), TOK), ACT.Relu, bias=b1s[:, slot, f:f + 1]).then_inc(relu_ok, 1)

            def statistics(e):
                act.wait_ge(turn_ps, e + 1)
                for t in range(TILES):
                    nc.scalar.activation(junk[:, t, :], tile5(6, t), ACT.Square,
                                         accum_out=ssq[:, t:t + 1]).then_inc(ssq_ok, 1)
                act.wait_ge(ssq_ok, e * TILES + TILES)
                nc.scalar.activation(f_s[:, 0, :], ssq[:, :], ACT.Sqrt, scale=1.0 / D,
                                     bias=cst[:, C_EPS + 2:C_EPS + 3]).then_inc(froot, 1)

            def window(e, slot, begin=False, end=False):
                relu(e, slot, 2, begin)
                relu(e, slot, 3, begin)
                if not begin:
                    statistics(e - 1)
                if not end:
                    relu(e + 1, 1 - slot, 0)
                    relu(e + 1, 1 - slot, 1)

            relu(0, 0, 0, begin=True)
            relu(0, 0, 1, begin=True)
            window(0, 0, begin=True)
            with act.Fori(0, E // 2 - 1) as i:
                window(i * 2 + 1, 1)
                window(i * 2 + 2, 0)
            window(E - 1, 1, end=True)
            act.wait_ge(wT_ps, 1)
            nc.scalar.copy(wT[:, :], wide(0, PAD)[0:E, :]).then_inc(wT_sb, 1)
            statistics(E - 1)

        @block.vector
        def _(dve):
            own = Steps(dve, dve_own)

            for tile_, val in ((ones[:, :], 1.0), (twos[:, :], 2.0), (sq[:, :], 1.0), (kvs[:, :, TOK:PAD], 0.0),
                               (X3[:, TOK:PAD], 0.0), (ysum[:, TOK:PAD], 0.0), (acc[:, TILES - 1, :], 0.0)):
                nc.vector.memset(tile_, val).then_inc(tails, 1)
            dve.wait_ge(s_cst, 16)
            nc.vector.tensor_copy(identb[:, :], ident).then_inc(tails, 1)

            for m in range(2):
                dve.wait_ge(s_x[m], 16)
                for c in (1, 2):
                    gather(nc.vector.tensor_copy, 3 * m + c).then_inc(px_dve, 1)

            def evacuate(k):
                rows = 128 if k < 7 else 64
                dve.wait_ge(xt_ps, 2 * k + 2)
                nc.vector.tensor_copy(
                    XT[0:rows, k, :].rearrange("p (q j) -> p j q", j=SIDE)[:, 3:6, :],
                    PS[0:rows, (2 * k + 1) % 4, 0:288].rearrange("p (j q) -> p j q", j=3)).then_inc(xt_dve, 1)

            for k in range(6):
                evacuate(k)
            flat = [wk[:, 3 * m:3 * m + 3, :].rearrange("p c d -> p (c d)") for m in range(2)]
            dve.wait_ge(s_w[0], 16)
            for s in range(1, 5):
                dve.wait_ge(s_w[s], 32)
                for m in range(2):
                    before = wsh[:, 0, m, :] if s == 1 else flat[m]
                    if s > 1:
                        dve.wait_ge(dve_own, own.n - 1)
                    if s < 3:
                        mask = cst[:, C_NOT_LAST:C_NOT_LAST + 1] if s == 1 else cst[:, C_NOT_FIRST:C_NOT_FIRST + 1]
                        own.mark(nc.vector.scalar_tensor_tensor(flat[m], wsh[:, s, m, :], mask, before, ALU.mult, ALU.add))
                    else:
                        own.mark(nc.vector.tensor_tensor(flat[m], wsh[:, s, m, :], before, ALU.add))
            for lo, hi, rows in ((0, 3, 128), (3, 6, 128), (6, 7, 128), (7, 8, 64)):
                if lo == 6:
                    dve.wait_ge(s_whalo, 128)
                own.wait()
                own.then(nc.vector.tensor_reduce(mean8[0:rows, lo:hi], wk[0:rows, lo:hi, :], AX.X, ALU.add))
                own.then(nc.vector.tensor_scalar(nmean8[0:rows, lo:hi], mean8[0:rows, lo:hi], 1.0 / D, None, ALU.mult))
                nc.vector.tensor_tensor(wkc[0:rows, lo:hi, :], wk[0:rows, lo:hi, :],
                                        nmean8[0:rows, lo:hi].unsqueeze(2).to_broadcast([rows, hi - lo, D]),
                                        ALU.subtract).then_inc(wk_ok, hi - lo)
                if hi == 6:
                    for k in (6, 7):
                        evacuate(k)
            dve.wait_ge(s_dw, 16)
            dve.wait_ge(small_sb, 1)
            own.then(nc.vector.tensor_scalar(dwg[:, 0, :], dw[:, :], vecT[:, V_TG:V_TG + 1], None, ALU.mult))
            own.then(nc.vector.tensor_reduce(mean8[:, 0:1], dwg[:, 0, :], AX.X, ALU.add))
            own.then(nc.vector.tensor_scalar(nmean8[:, 0:1], mean8[:, 0:1], 1.0 / D, None, ALU.mult))
            nc.vector.tensor_scalar(dwg[:, 1, :], dwg[:, 0, :], nmean8[:, 0:1], None, ALU.subtract).then_inc(dense_ok, 2)
            dve.wait_ge(small_sb, 3)
            own.then(nc.vector.tensor_reduce(mean8[:, 1:2], wtT[:, 3, :], AX.X, ALU.add))
            own.then(nc.vector.tensor_scalar(nmean8[:, 1:2], mean8[:, 1:2], 1.0 / D, None, ALU.mult))
            own.then(nc.vector.tensor_scalar(wtT[:, 4, :], wtT[:, 3, :], nmean8[:, 1:2], None, ALU.subtract))
            left = wtT[:, :, :]
            for part in range(3):
                own.then(nc.vector.tensor_copy(wpart[:, part, :, :], left))
                if part < 2:
                    own.then(nc.vector.tensor_tensor(wrem[:, part, :, :], left, wpart[:, part, :, :], ALU.subtract))
                    left = wrem[:, part, :, :]
            dve.sem_inc(wparts_ok, 1)
            dve.wait_ge(s_w2, 16)
            own.then(nc.vector.tensor_reduce(w2m[:, :, :], w2r[:, :, :, :], AX.X, ALU.add))
            nc.vector.tensor_scalar(w2m[:, :, :], w2m[:, :, :], 1.0 / D, None, ALU.mult).then_inc(w2m_ok, 1)

            def factor(n, bank):
                dve.wait_ge(var_ps, n)
                nc.vector.tensor_scalar(r_v[:, :], PS[:, bank, 0:TILES], 1.0 / D, EPS[n - 1], ALU.mult, ALU.add).then_inc(v_ok, 1)
                dve.wait_ge(root_ok, n)
                own.then(nc.vector.reciprocal(r_a[:, :], r_s[:, :]))
                own.then(nc.vector.tensor_tensor(r_b[:, :], r_v[:, :], r_a[:, :], ALU.mult))
                own.then(nc.vector.tensor_tensor(r_c[:, :], r_b[:, :], r_s[:, :], ALU.add))
                own.then(nc.vector.reciprocal(r_h[:, :], r_c[:, :]))
                nc.vector.tensor_tensor(diag[:, :, :], ident.unsqueeze(1).to_broadcast([128, TILES, 128]),
                                        r_h[:, :].unsqueeze(2).to_broadcast([128, TILES, 128]), ALU.mult).then_inc(diag_ok, 1)

            factor(1, 6)
            dve.wait_ge(bc_ps, 1)
            dve.wait_ge(t_sb, 2)
            nc.vector.tensor_tensor(h1[:, :], wide(4, PTOK), h0[:, 1, :], ALU.mult).then_inc(h0_ok, 1)
            nc.vector.tensor_tensor(ysb[:, :], wide(4, PTOK), h0[:, 0, :], ALU.mult).then_inc(h0_ok, 1)
            factor(2, 6)
            flat_c = Hc[:, :, :].rearrange("p b n -> p (b n)")
            flat_h = H[:, :, :].rearrange("p b n -> p (b n)")
            dve.wait_ge(bc_ps, 2)
            own.then(nc.vector.scalar_tensor_tensor(spk[:, :], flat_c, 0.0, wide(4, TOK), ALU.max, ALU.mult))
            own.then(nc.vector.tensor_scalar(spk2[:, :], spk[:, :], TIE, CAP, ALU.add, ALU.min))
            nc.vector.tensor_scalar(xs[:, :], spk2[:, :], RNE, RNE, ALU.add, ALU.subtract).then_inc(xs_ok, 1)
            for n, (which, bank) in enumerate(((1, 0), (0, 2), (2, 6))):
                dve.wait_ge(qkv_ps, n + 1)
                for c, (a, b) in enumerate(CUTS):
                    own.mark(nc.vector.bn_stats(bnst[:, which, c, :], PS[:, bank + c, 0:b - a]))
                own.wait()
                own.mark(nc.vector.bn_aggr(bnmv[:, which, :], bnst[:, which, :, :].rearrange("p c s -> p (c s)")))
            own.wait()
            mean, var = bnmv[:, :, 0], bnmv[:, :, 1]
            bn_v, bn_a, bn_b, bn_c, bn_h, bn_m = (bn_s[:, k, :] for k in range(1, 7))
            nc.vector.tensor_scalar(bn_v, var, EPS[1], None, ALU.add).then_inc(bn_var, 1)
            dve.wait_ge(bn_root, 1)
            dve.wait_ge(bn_var, 1)
            own.then(nc.vector.reciprocal(bn_a, bn_s[:, 0, :]))
            own.then(nc.vector.tensor_tensor(bn_b, bn_v, bn_a, ALU.mult))
            own.then(nc.vector.tensor_tensor(bn_c, bn_b, bn_s[:, 0, :], ALU.add))
            own.then(nc.vector.reciprocal(bn_h, bn_c))
            own.then(nc.vector.scalar_tensor_tensor(bn_scale[:, :], bn_h, 2.0, vecT[:, V_AG:V_AG + 3], ALU.mult, ALU.mult))
            own.then(nc.vector.tensor_tensor(bn_m, mean, bn_scale[:, :], ALU.mult))
            nc.vector.scalar_tensor_tensor(bn_shift[:, :], vecT[:, V_AB:V_AB + 3], TIE, bn_m, ALU.add,
                                           ALU.subtract).then_inc(bn_ok, 1)
            for n, which in enumerate((1, 0, 2)):
                dve.wait_ge(pre_ok, n + 1)
                own.then(nc.vector.tensor_scalar(pre2[:, which, :], pre[:, which, :], CAP, RNE, ALU.min, ALU.add))
                if which == 0:
                    for half, mask in ((0, C_EVEN), (1, C_ODD)):
                        nc.vector.tensor_scalar(qe[:, half, :], pre2[:, 0, :], RNE, cst[:, mask:mask + 1],
                                                ALU.subtract, ALU.mult).then_inc(spike_ok, 1)
                else:
                    nc.vector.tensor_scalar(kvs[:, which // 2, 0:TOK], pre2[:, which, :], RNE, None,
                                            ALU.subtract).then_inc(spike_ok, 1)
            for rnd in range(2):
                dve.wait_ge(sc_ps, rnd + 1)
                nc.vector.tensor_scalar(A[:, :, 4 * rnd:4 * rnd + 4, :].rearrange("p g r n -> p g (r n)"),
                                        PS[:, 4 * rnd:4 * rnd + 4, 0:8 * NT], CAP, None, ALU.min).then_inc(sc_sb, 1)
            for rnd in range(2):
                dve.wait_ge(av_ps, rnd + 1)
                o = [PS[:, 2 * rnd + half, 0:8 * NT].rearrange("p (r e n) -> p r e n", e=2, n=NT) for half in range(2)]
                for half in range(2):
                    own.mark(nc.vector.tensor_scalar(av0[:, 2 * rnd + half, :, :], o[half][:, :, 0, :],
                                                     evens[:, 0:1], TIE, ALU.mult, ALU.add))
                for half in range(2):
                    dve.wait_ge(dve_own, own.n - 1)
                    own.mark(nc.vector.scalar_tensor_tensor(av[:, 8 * rnd + half:8 * rnd + 8:2, :], o[half][:, :, 1, :],
                                                            evens[:, 1:2], av0[:, 2 * rnd + half, :, :], ALU.mult, ALU.add))
            own.wait()
            own.then(nc.vector.tensor_scalar(av2[:, :], av[:, :, :].rearrange("p b n -> p (b n)"), CAP, RNE, ALU.min, ALU.add))
            nc.vector.tensor_scalar(os_[:, :], av2[:, :], RNE, None, ALU.subtract).then_inc(os_ok, 1)
            dve.wait_ge(proj_ps, 1)
            nc.vector.scalar_tensor_tensor(flat_c, wide(6, TOK), vecC[:, V_BPROJ:V_BPROJ + 1], flat_c, ALU.add,
                                           ALU.add).then_inc(h2_ok, 1)
            dve.wait_ge(proj_ps, 2)
            nc.vector.scalar_tensor_tensor(flat_h, wide(4, TOK), vecT[:, V_BPROJ:V_BPROJ + 1], flat_h, ALU.add,
                                           ALU.add).then_inc(h2_ok, 1)
            factor(3, 0)
            dve.wait_ge(bc_ps, 3)
            nc.vector.tensor_tensor(X3[:, 0:TOK], wide(2, TOK), flat_c, ALU.mult).then_inc(x3_ok, 1)

            def bc(col):
                return col.unsqueeze(2).to_broadcast([128, TILES, E])

            dve.wait_ge(lg_ps, 1)
            nc.vector.tensor_copy(L[:, :, :], PS[:, 0, 16:16 + TILES * E].rearrange("p (t e) -> p t e", e=E)).then_inc(lg_sb, 1)
            dve.wait_ge(lg_sb, 1)
            rank = cst[:, C_RANK:C_RANK + E].unsqueeze(1).to_broadcast([128, TILES, E])

            def best(level, values, top, pick):
                own.then(nc.vector.tensor_reduce(top, values, AX.X, ALU.max))
                own.then(nc.vector.tensor_tensor(g[0][:, :, :], values, bc(top), ALU.is_equal))
                own.then(nc.vector.tensor_tensor(g[1][:, :, :], g[0][:, :, :], rank, ALU.mult))
                own.then(nc.vector.tensor_reduce(gs[:, 5, :], g[1][:, :, :], AX.X, ALU.max))
                own.then(nc.vector.tensor_tensor(pick, g[1][:, :, :], bc(gs[:, 5, :]), ALU.is_equal))

            best(0, L[:, :, :], gs[:, 0, :], g[2][:, :, :])
            own.then(nc.vector.scalar_tensor_tensor(g[3][:, :, :], g[2][:, :, :], -3.0e38, L[:, :, :], ALU.mult, ALU.add))
            best(1, g[3][:, :, :], gs[:, 1, :], g[4][:, :, :])
            nc.vector.tensor_tensor(gs[:, 2, :], gs[:, 1, :], gs[:, 0, :], ALU.subtract).then_inc(gap, 1)
            dve.wait_ge(gexp, 1)
            own.then(nc.vector.tensor_scalar(gs[:, 4, :], gs[:, 3, :], 1.0, None, ALU.add))
            own.then(nc.vector.reciprocal(gs[:, 5, :], gs[:, 4, :]))
            own.then(nc.vector.tensor_tensor(gs[:, 4, :], gs[:, 3, :], gs[:, 5, :], ALU.mult))
            own.then(nc.vector.tensor_tensor(g[5][:, :, :], g[2][:, :, :], bc(gs[:, 5, :]), ALU.mult))
            own.then(nc.vector.tensor_tensor(g[6][:, :, :], g[4][:, :, :], bc(gs[:, 4, :]), ALU.mult))
            nc.vector.tensor_tensor(W8[:, :, :], g[5][:, :, :], g[6][:, :, :], ALU.add).then_inc(gate_ok, 1)
            dve.wait_ge(gate_ok, 1)

            def close_sum(e, slot, begin=False):
                dve.wait_ge(mm2_done, e * FT + FT)
                if not begin:
                    dve.wait_ge(turn_ps, e)
                bias = vecC[:, V_B2 + e:V_B2 + e + 1] if isinstance(e, int) else vecC[:, bass.ds(e + V_B2, 1)]
                nc.vector.scalar_tensor_tensor(ysum[:, 0:TOK], wide(4, TOK), bias, X3[:, 0:TOK], ALU.add,
                                               ALU.add).then_inc(ysum_ok, 1)

            def finish(e, last=False):
                dve.wait_ge(ssq_ok, e * TILES + TILES)
                nc.vector.tensor_scalar(f_s[:, 1, :], ssq[:, :], 1.0 / D, EPS[2], ALU.mult, ALU.add).then_inc(fch, 1)
                dve.wait_ge(froot, e + 1)
                nc.vector.reciprocal(f_s[:, 2, :], f_s[:, 0, :]).then_inc(fch, 1)
                dve.wait_ge(fch, e * 5 + 2)
                nc.vector.tensor_tensor(f_s[:, 3, :], f_s[:, 1, :], f_s[:, 2, :], ALU.mult).then_inc(fch, 1)
                dve.wait_ge(fch, e * 5 + 3)
                nc.vector.tensor_tensor(f_s[:, 4, :], f_s[:, 3, :], f_s[:, 0, :], ALU.add).then_inc(fch, 1)
                dve.wait_ge(fch, e * 5 + 4)
                nc.vector.reciprocal(f_s[:, 5, :], f_s[:, 4, :]).then_inc(fch, 1)
                dve.wait_ge(fch, e * 5 + 5)
                gate = W8[:, :, e:e + 1] if isinstance(e, int) else W8[:, :, bass.ds(e, 1)]
                nc.vector.scalar_tensor_tensor(frw[:, :], f_s[:, 5, :], 2.0, gate.rearrange("p t o -> p (t o)"), ALU.mult,
                                               ALU.mult).then_inc(ffac, 1)
                dve.wait_ge(ffac, e + 1)
                dve.wait_ge(acc_ok, e + 1)
                gamma = gbc[:, e, :] if isinstance(e, int) else gbc[:, bass.ds(e, 1), :].rearrange("p o d -> p (o d)")
                for t in range(TILES):
                    zt = nc.vector.scalar_tensor_tensor(z[:, t, :], tile5(6, t), frw[:, t:t + 1], gamma, ALU.mult, ALU.mult)
                    if last:
                        zt.then_inc(z_last, 1)
                if not last:
                    zt.then_inc(z_ok, 1)

            def window(e, slot, begin=False):
                if not begin:
                    finish(e - 1)
                close_sum(e, slot, begin)

            dve.wait_ge(s_gb, 32)
            window(0, 0, begin=True)
            with dve.Fori(0, E // 2 - 1) as i:
                window(i * 2 + 1, 1)
                window(i * 2 + 2, 0)
            window(E - 1, 1)
            dve.wait_ge(beta_ps, 1)
            dve.wait_ge(acc_ok, E)
            nc.vector.tensor_tensor(acc[:, :, :].rearrange("p t d -> p (t d)"), wide(2, PAD),
                                    acc[:, :, :].rearrange("p t d -> p (t d)"), ALU.add).then_inc(beta_sb, 1)
            finish(E - 1, last=True)
            dve.wait_ge(beta_sb, 1)
            for t in range(TILES):
                dve.wait_ge(z_last, t + 1)
                nc.vector.tensor_tensor(acc[:, t, :], acc[:, t, :], z[:, t, :], ALU.add).then_inc(out_ok, 1)


_INS = ['x', 'cls_tok', 'L0_tok_conv_w', 'L0_tok_conv_b', 'L0_tok_gamma', 'L0_tok_beta', 'L0_tok_dense_w',
        'L0_tok_dense_b', 'L0_attn_Wqkv', 'L0_attn_gamma', 'L0_attn_beta', 'L0_attn_Wproj', 'L0_attn_bproj',
        'L0_ffn_router_w', 'L0_ffn_w1', 'L0_ffn_b1', 'L0_ffn_w2', 'L0_ffn_b2', 'L0_ffn_gamma', 'L0_ffn_beta']


def kernel(**inputs):
    import concourse.bacc as _bacc
    from concourse.bass_utils import run_bass_kernel_spmd as _run

    nc = _bacc.Bacc("TRN2", target_bir_lowering=False, num_devices=1)
    arrays = {"consts_dram": constants()}
    for name in _INS:
        arrays[f"in_{name}_dram"] = np.ascontiguousarray(inputs[name])
    args = [nc.dram_tensor(n, a.shape, F32, kind="ExternalInput").ap() for n, a in arrays.items()]
    out = nc.dram_tensor("out_dram", (B, NT, D), F32, kind="ExternalOutput").ap()
    vit_layer(nc, *args, out)
    r = _run(nc, [arrays], core_ids=[0])
    return r.results[0]["out_dram"]
```

```python
from contextlib import ExitStack

import numpy as np

import concourse.bass as bass
from concourse import mybir

F32 = mybir.dt.float32
BF16 = mybir.dt.bfloat16
F32R = mybir.dt.float32r
ALU = mybir.AluOpType
ACT = mybir.ActivationFunctionType
AX = mybir.AxisListType

B, IMG, CH, PATCH, D = 16, 96, 3, 16, 128
SIDE = IMG // PATCH
NP = SIDE * SIDE
NT = NP + 1
TOK = B * NT
PTOK = B * NP
TILES = -(-TOK // 128)
PAD = TILES * 128
HEADS, HD = 8, 16
E, F = 8, 512
FT = F // 128
BANK = 512
CUTS = ((0, BANK), (BANK, TOK))
PCUTS = ((0, BANK), (BANK, PTOK))
XROW = (IMG + 2) * CH
RNE = float(2 ** 23)
TIE = float(2 ** -22)
CAP = 4.0

V_B1, V_B2, V_CONVB, V_TG, V_TB, V_DENSEB, V_AG, V_AB, V_BPROJ, V_CLS, NV = 0, 32, 40, 41, 42, 43, 44, 47, 50, 51, 52

C_ID, C_CENTRE, C_NOT_LAST, C_NOT_FIRST, C_EVEN, C_ODD, C_RANK, C_TOP, C_BOTTOM, C_EPS, C_KEEP, CN = \
    0, 128, 256, 257, 258, 259, 260, 268, 269, 270, 273, 275
EPS = (1e-3, 1e-5, 1e-6)


def constants():
    p = np.arange(128)
    c = np.zeros((128, CN), np.float32)
    c[:, C_ID:C_ID + 128] = np.eye(128)
    c[:, C_CENTRE:C_CENTRE + 128] = np.eye(128) - 1.0 / 128
    c[:, C_NOT_LAST] = p % PATCH != PATCH - 1
    c[:, C_NOT_FIRST] = p % PATCH != 0
    c[:, C_EVEN] = (p // HD) % 2 == 0
    c[:, C_ODD] = (p // HD) % 2 == 1
    c[:, C_RANK:C_RANK + E] = E - np.arange(E)
    c[:, C_TOP] = p % SIDE != 0
    c[:, C_BOTTOM] = p % SIDE != SIDE - 1
    c[:, C_EPS:C_EPS + 3] = EPS
    c[:, C_KEEP] = c[:, C_EVEN] * HD ** -0.5
    c[:, C_KEEP + 1] = c[:, C_ODD] * HD ** -0.5
    return c


class Steps:

    def __init__(self, eng, sem):
        self.eng, self.sem, self.n = eng, sem, 0

    def mark(self, ins):
        self.n += 1
        ins.then_inc(self.sem, 1)

    def wait(self):
        self.eng.wait_ge(self.sem, self.n)

    def then(self, ins):
        self.mark(ins)
        self.wait()


def vit_layer(nc, consts, x, cls_tok, conv_w, conv_b, tok_g, tok_b, dense_w, dense_b, wqkv, attn_g, attn_b,
              wproj, bproj, router_w, w1, b1, w2, b2, ffn_g, ffn_b, out):
    with ExitStack() as ctx:
        def sb(name, shape, dt=F32):
            return ctx.enter_context(nc.sbuf_tensor(name, shape, dt))

        def sem(name):
            return ctx.enter_context(nc.semaphore(name))

        cst = sb("cst", [128, CN])
        ident = cst[:, C_ID:C_ID + 128]
        centre = cst[:, C_CENTRE:C_CENTRE + 128]
        evens = cst[:, C_KEEP:C_KEEP + 2]
        identb = sb("identb", [128, 128], BF16)
        ones = sb("ones", [128, 1])
        twos = sb("twos", [128, 128])
        vec = sb("vec", [64, 128])
        vecT = sb("vecT", [128, NV])
        vecC = sb("vecC", [128, NV])

        dw = sb("dw", [128, D])
        dwg = sb("dwg", [128, 2, D])
        c0 = sb("c0", [128, 2])
        ysb = sb("ysb", [128, PTOK])
        sq = sb("sq", [128, PAD])
        r_s = sb("r_s", [128, TILES])
        r_v = sb("r_v", [128, TILES])
        r_a = sb("r_a", [128, TILES])
        r_b = sb("r_b", [128, TILES])
        r_c = sb("r_c", [128, TILES])
        r_h = sb("r_h", [128, TILES])
        diag = sb("diag", [128, TILES, 128])
        h0 = sb("h0", [128, 2, PTOK])
        h1 = sb("h1", [128, PTOK])
        H = sb("H", [128, B, NT])
        Hc = sb("Hc", [128, B, NT])

        wt = sb("wt", [128, 4, D])
        wtT = sb("wtT", [128, 5, D])
        wrem = sb("wrem", [128, 2, 5, D])
        wpart = sb("wpart", [128, 3, 5, D], BF16)
        xs = sb("xs", [128, TOK], BF16)
        bnst = sb("bnst", [128, 3, 2, 6])
        bnmv = sb("bnmv", [128, 3, 2])
        bn_s = sb("bn_s", [128, 8, 3])
        bn_scale = sb("bn_scale", [128, 3])
        bn_shift = sb("bn_shift", [128, 3])
        qe = sb("qe", [128, 2, TOK], BF16)
        kvs = sb("kvs", [128, 2, PAD], BF16)
        vtok = sb("vtok", [128, B // 2, D], BF16)
        A = sb("A", [128, 4, B // 2, 2 * NT], BF16)
        av2 = sb("av2", [128, TOK])
        os_ = sb("os", [128, TOK], BF16)

        X3 = sb("X3", [128, PAD])
        rw = sb("rw", [128, E])
        L = sb("L", [128, TILES, E])
        g = [sb(f"g{i}", [128, TILES, E]) for i in range(5)]
        gs = sb("gs", [128, 6, TILES])
        W8 = sb("W8", [128, TILES, E])
        wT = sb("wT", [E, PAD])
        fb = sb("fb", [E, D])
        gbc = sb("gbc", [128, E, D])
        ysum = sb("ysum", [128, PAD])
        junk = sb("junk", [128, TILES, 128], BF16)
        b1s = sb("b1s", [128, 2, FT])
        ssq = sb("ssq", [128, TILES])
        f_s = sb("f_s", [128, 6, TILES])
        frw = sb("frw", [128, TILES])
        z = sb("z", [128, TILES, D])
        zg = sb("zg", [128, TILES, D])
        acc = sb("acc", [128, TILES, D])

        with ExitStack() as scope:
            def room(name, shape, dt=F32):
                return scope.enter_context(nc.sbuf_tensor(name, shape, dt))

            xin = room("xin", [96, PATCH + 2, XROW])
            halo = room("halo", [96, SIDE, CH, 4, PATCH])
            own_px = room("own_px", [96, 6, SIDE, 128])
            XT = room("XT", [128, 8, PTOK])
            wsh = room("wsh", [128, 5, 2, CH * D])
            wk = room("wk", [128, 8, D])
            wkc = room("wkc", [128, 8, D])
            mean8 = room("mean8", [128, 8])
            nmean8 = room("nmean8", [128, 8])

        raw = sb("raw", [128, 2, E // 2, F])
        parts = sb("parts", [128, E, 4, F], F32R)
        slot_w = sb("slot_w", [128, 2, 4, F], F32R)
        cen = sb("cen", [128, 2, F])
        w2m = sb("w2m", [128, E, FT])
        w2s = sb("w2s", [128, E, FT])
        rel = sb("rel", [128, FT, TOK])
        with ExitStack() as scope:
            pre = scope.enter_context(nc.sbuf_tensor("pre", [128, 3, TOK], F32))
            pre2 = scope.enter_context(nc.sbuf_tensor("pre2", [128, 3, TOK], F32))
            spk = scope.enter_context(nc.sbuf_tensor("spk", [128, TOK], F32))
            spk2 = scope.enter_context(nc.sbuf_tensor("spk2", [128, TOK], F32))
            av0 = scope.enter_context(nc.sbuf_tensor("av0", [128, 4, 4, NT], F32))
            av = spk[:, :].rearrange("p (b n) -> p b n", n=NT)
        hs = sb("hs", [128, 2, FT, TOK], F32R)
        X3p = sb("X3p", [128, 2, TOK], F32R)

        PS = ctx.enter_context(nc.psum_tensor("PS", [128, 8, BANK], F32))

        def wide(bank, cols):
            return PS[:, bank:bank + 2, :].rearrange("p b n -> p (b n)")[:, 0:cols]

        def halves(bank):
            return PS[:, bank:bank + 2, 0:TOK // 2]

        def in_halves(row):
            return row.rearrange("p (h n) -> p h n", h=2)

        def tile5(bank, t, rows=128):
            return PS[0:rows, bank + t // 4, (t % 4) * 128:(t % 4) * 128 + 128]

        s_cst, s_x, s_vec = sem("s_cst"), [sem("s_x0"), sem("s_x1")], sem("s_vec")
        s_halo_rows = sem("s_halo_rows")
        s_w = [[sem(f"s_shift{i}_half{m}") for i in range(5)] for m in range(2)]
        s_whalo, s_wt, s_dw, s_rw, s_gb = (sem(n) for n in ("s_whalo", "s_wt", "s_dw", "s_rw", "s_gb"))
        four_w1, four_w2 = sem("four_w1"), sem("four_w2")
        s_w1 = [four_w1] * (E // 2) + [sem(f"s_w1_{e}") for e in range(E // 2, E)]
        s_w2 = [four_w2] * (E // 2) + [sem(f"s_w2_{e}") for e in range(E // 2, E)]
        pads = sem("pads")
        wpads = sem("wpads")
        tails = sem("tails")
        halo_ok = sem("halo_ok")
        px_act, px_dve = sem("px_act"), sem("px_dve")
        xt_ps, xt_sb = sem("xt_ps"), sem("xt_sb")
        small_ps, small_sb = sem("small_ps"), sem("small_sb")
        wk_ok, conv_ps, y_ok, sq_ok = sem("wk_ok"), sem("conv_ps"), sem("y_ok"), sem("sq_ok")
        dense_ok = sem("dense_ok")
        var_ps, v_ok, root_ok, diag_ok, bc_ps = sem("var_ps"), sem("v_ok"), sem("root_ok"), sem("diag_ok"), sem("bc_ps")
        t_ps, t_sb = sem("t_ps"), sem("t_sb")
        h0_ok, h_ok = sem("h0_ok"), sem("h_ok")
        wcen_ok, wpart_ok, wrem_ok, xs_ok = sem("wcen_ok"), sem("wpart_ok"), sem("wrem_ok"), sem("xs_ok")
        w1_high, w1_low, w2_cen, w2_high, w2_low = (sem(n) for n in ("w1_high", "w1_low", "w2_cen", "w2_high", "w2_low"))
        x3p_ok, hi_ok, lo_dve, lo_pool, zg_ok = (sem(n) for n in ("x3p_ok", "hi_ok", "lo_dve", "lo_pool", "zg_ok"))
        qkv_ps, bn_var, bn_root, bn_ok, pre_ok, spike_ok = (sem(n) for n in
                                                            ("qkv_ps", "bn_var", "bn_root", "bn_ok", "pre_ok", "spike_ok"))
        vt_ps, vt_sb, sc_ps, sc_sb, av_ps, os_ok = (sem(n) for n in
                                                    ("vt_ps", "vt_sb", "sc_ps", "sc_sb", "av_ps", "os_ok"))
        proj_ps, h2_ok, x3_ok = sem("proj_ps"), sem("h2_ok"), sem("x3_ok")
        h2t_ps, lg_ps, lg_sb, gap, gexp, gate_ok, wT_ps, wT_sb = (sem(n) for n in (
            "h2t_ps", "lg_ps", "lg_sb", "gap", "gexp", "gate_ok", "wT_ps", "wT_sb"))
        w2m_ok, out_ok, z_last = sem("w2m_ok"), sem("out_ok"), sem("z_last")
        w1_slot, w2_slot, b1_slot = ([sem(f"{n}_slot{i}") for i in range(2)] for n in ("w1", "w2", "b1"))
        g_ps, relu_ok, mm2_done, ysum_ok, turn_ps, ssq_ok, froot, z_ok, acc_ok, fch, ffac = (sem(n) for n in (
            "g_ps", "relu_ok", "mm2_done", "ysum_ok", "turn_ps", "ssq_ok", "froot", "z_ok", "acc_ok", "fch", "ffac"))
        beta_ps, beta_sb, s_out = sem("beta_ps"), sem("beta_sb"), sem("s_out")
        dve_own, pool_own, act_own = sem("dve_own"), sem("pool_own"), sem("act_own")

        def gather(copy, k):
            m, c = k // 3, k % 3
            pix = xin[:, 1 + 8 * m:9 + 8 * m, CH:CH + IMG * CH].rearrange("p r (j w c) -> p j r w c", w=PATCH, c=CH)
            return copy(own_px[:, k, :, :].rearrange("p j (r w) -> p j r w", w=PATCH), pix[:, :, :, :, c])

        block = ctx.enter_context(nc.Block())

        @block.sync
        def _(sp):
            bands = x.rearrange("b (i r) w c -> (b i) r (w c)", r=PATCH)
            for m in range(2):
                nc.sync.dma_start(xin[:, 1 + 8 * m:9 + 8 * m, CH:CH + IMG * CH],
                                  bands[:, 8 * m:8 * m + 8, :]).then_inc(s_x[m], 16)
                if m == 0:
                    nc.sync.dma_start(cst[:, :], consts).then_inc(s_cst, 16)
            sp.wait_ge(pads, 2)
            nc.sync.dma_start(xin[1:96, 0, CH:CH + IMG * CH], bands[0:95, PATCH - 1, :]).then_inc(s_halo_rows, 16)
            nc.sync.dma_start(xin[0:95, PATCH + 1, CH:CH + IMG * CH], bands[1:96, 0, :]).then_inc(s_halo_rows, 16)
            wq = conv_w.rearrange("i j c d -> (i j) (c d)")
            sp.wait_ge(wpads, 4)
            for m in range(2):
                for s, step in ((0, 0), (1, 1), (2, -1), (3, PATCH), (4, -PATCH)):
                    lo, hi = max(0, 128 * m + step), min(256, 128 * m + 128 + step)
                    nc.sync.dma_start(wsh[lo - step - 128 * m:hi - step - 128 * m, s, m, :],
                                      wq[lo:hi, 3 * s * D:(3 * s + 3) * D]).then_inc(s_w[m][s], 16)
            nc.sync.dma_start(wt[:, 0:3, :], wqkv.rearrange("(k p) c -> p k c", p=128)).then_inc(s_wt, 16)
            nc.sync.dma_start(wt[:, 3, :], wproj).then_inc(s_wt, 16)
            sides = (conv_w[:, 0, 3:6, :], conv_w[:, PATCH - 1, 6:9, :], conv_w[0, :, 9:12, :], conv_w[PATCH - 1, :, 12:15, :])
            for s, w in enumerate(sides):
                nc.sync.dma_start(wk[16 * s:16 * s + 16, 6:8, :], w[:, 0:3:2, :]).then_inc(s_whalo, 16)
                nc.sync.dma_start(wk[64 + 16 * s:80 + 16 * s, 6, :], w[:, 1, :]).then_inc(s_whalo, 16)
            nc.sync.dma_start(dw[:, :], dense_w).then_inc(s_dw, 16)
            for row, v in ((V_B1, b1.rearrange("e (f p) -> (e f) p", p=128)), (V_B2, b2),
                           (V_CONVB, conv_b.rearrange("(a d) -> a d", a=1)), (V_TG, tok_g.rearrange("(a d) -> a d", a=1)),
                           (V_TB, tok_b.rearrange("(a d) -> a d", a=1)), (V_DENSEB, dense_b.rearrange("(a d) -> a d", a=1)),
                           (V_AG, attn_g.rearrange("(k d) -> k d", d=D)), (V_AB, attn_b.rearrange("(k d) -> k d", d=D)),
                           (V_BPROJ, bproj.rearrange("(a d) -> a d", a=1)), (V_CLS, cls_tok.rearrange("a b d -> (a b) d"))):
                nc.sync.dma_start(vec[row:row + v.shape[0], :], v).then_inc(s_vec, 16)
            nc.sync.dma_start(rw[:, :], router_w).then_inc(s_rw, 16)
            nc.sync.dma_start(gbc[:, :, :].rearrange("p e d -> p (e d)"),
                              ffn_g.rearrange("e d -> (e d)").partition_broadcast(128)).then_inc(s_gb, 16)
            nc.sync.dma_start(fb[:, :], ffn_b).then_inc(s_gb, 16)
            sp.wait_ge(xt_ps, 8)
            four = slice(0, E // 2)
            nc.sync.dma_start(raw[:, 1, :, :].rearrange("p e (f d) -> p e f d", d=D),
                              w2[four].rearrange("e (f p) d -> p e f d", p=128)).then_inc(four_w2, 16)
            nc.sync.dma_start(raw[:, 0, :, :], w1[four].rearrange("e p f -> p e f")).then_inc(four_w1, 16)

            def fill_first(e, slot):
                src = parts[:, e, 0:2, :] if isinstance(e, int) else parts[:, bass.ds(e, 1), 0:2, :].rearrange("p o k f -> p (o k) f")
                nc.sync.dma_start(slot_w[:, slot, 0:2, :].bitcast(F32), src.bitcast(F32)).then_inc(w1_slot[slot], 16)
                nc.sync.dma_start(b1s[:, slot, :], vecT[:, bass.ds(e * FT + V_B1, FT)]).then_inc(b1_slot[slot], 16)

            def fill_second(e, slot):
                src = parts[:, e, 2:4, :] if isinstance(e, int) else parts[:, bass.ds(e, 1), 2:4, :].rearrange("p o k f -> p (o k) f")
                nc.sync.dma_start(slot_w[:, slot, 2:4, :].bitcast(F32), src.bitcast(F32)).then_inc(w2_slot[slot], 16)

            def load(e):
                sp.wait_ge(w2_cen, e + 1)
                nc.sync.dma_start(raw[:, 1, e, :].rearrange("p (f d) -> p f d", d=D),
                                  w2[e + E // 2].rearrange("(f p) d -> p f d", p=128)).then_inc(s_w2[e + E // 2], 16)
                sp.wait_ge(w1_low, e + 1)
                nc.sync.dma_start(raw[:, 0, e, :], w1[e + E // 2]).then_inc(s_w1[e + E // 2], 16)

            for e in range(2):
                sp.wait_ge(w1_low, e + 1)
                sp.wait_ge(w1_high, e + 1)
                fill_first(e, e)
                sp.wait_ge(w2_low, e + 1)
                sp.wait_ge(w2_high, e + 1)
                fill_second(e, e)
                load(e)
            load(2)
            load(3)
            sp.wait_ge(w1_low, E)
            sp.wait_ge(w1_high, E)
            sp.wait_ge(w2_low, E)
            sp.wait_ge(w2_high, E)
            with sp.Fori(0, E // 2 - 1) as i:
                for slot in range(2):
                    sp.wait_ge(relu_ok, i * (2 * FT) + (slot + 1) * FT)
                    fill_first(i * 2 + (slot + 2), slot)
                    sp.wait_ge(mm2_done, i * (2 * FT) + (slot + 1) * FT)
                    fill_second(i * 2 + (slot + 2), slot)

            rows = out.rearrange("b n d -> (b n) d")
            for t in range(TILES):
                sp.wait_ge(out_ok, t + 1)
                n = min(128, TOK - 128 * t)
                nc.sync.dma_start(rows[128 * t:128 * t + n, :], acc[0:n, t, :]).then_inc(s_out, 16)
            sp.wait_ge(s_out, 16 * TILES)

        @block.gpsimd
        def _(pool):
            for s, rows, m in ((2, slice(0, 32), 0), (4, slice(0, 32), 0), (1, slice(96, 128), 1), (3, slice(96, 128), 1)):
                nc.gpsimd.memset(wsh[rows, s, m, :], 0.0).then_inc(wpads, 1)
            xw = xin[:, :, :].rearrange("p r (w c) -> p r w c", c=CH)
            pool.wait_ge(pads, 3)
            pool.wait_ge(s_cst, 16)
            pool.wait_ge(s_x[0], 16)
            pool.wait_ge(s_x[1], 16)
            for side, col in ((0, 0), (1, PATCH + 1)):
                for c in range(CH):
                    nc.gpsimd.tensor_copy(
                        halo[:, :, c, side, :],
                        xw[:, 1:PATCH + 1, col:col + PATCH * (SIDE - 1) + 1:PATCH, c].rearrange("p r j -> p j r")
                    ).then_inc(halo_ok, 1)
            pool.wait_ge(s_halo_rows, 32)
            for side, row, mask in ((2, 0, C_TOP), (3, PATCH + 1, C_BOTTOM)):
                for c in range(CH):
                    nc.gpsimd.tensor_scalar(
                        halo[:, :, c, side, :],
                        xw[:, row, 1:IMG + 1, c].rearrange("p (j w) -> p j w", w=PATCH),
                        cst[0:96, mask:mask + 1], None, ALU.mult).then_inc(halo_ok, 1)
            pool.wait_ge(small_sb, 3)
            pool.wait_ge(tails, 8)
            nc.gpsimd.tensor_scalar(H[:, :, 0], sq[:, 0:B], 0.0, vecT[:, V_CLS:V_CLS + 1], ALU.mult, ALU.add).then_inc(h_ok, 1)
            nc.gpsimd.tensor_scalar(Hc[:, :, 0], sq[:, 0:B], 0.0, vecC[:, V_CLS:V_CLS + 1], ALU.mult, ALU.add).then_inc(h_ok, 1)

            def remainder(part):
                pool.wait_ge(wpart_ok, part + 1)
                left = wrem[:, part - 1, :, :] if part else wtT[:, :, :]
                nc.gpsimd.tensor_tensor(wrem[:, part, :, :], left, wpart[:, part, :, :], ALU.subtract).then_inc(wrem_ok, 1)

            for e in range(E):
                at = e % (E // 2)
                pool.wait_ge(s_w2[e], 16)
                pool.wait_ge(w2m_ok, e + 1)
                if e >= 2:
                    pool.wait_ge(w2_high, e - 1)
                nc.gpsimd.tensor_tensor(cen[:, e % 2, :].rearrange("p (f d) -> p f d", d=D),
                                        raw[:, 1, at, :].rearrange("p (f d) -> p f d", d=D),
                                        w2m[:, e, :].unsqueeze(2).to_broadcast([128, FT, D]), ALU.subtract).then_inc(w2_cen, 1)
                if e < 2:
                    remainder(e)
                pool.wait_ge(s_w1[e], 16)
                pool.wait_ge(w1_high, e + 1)
                nc.gpsimd.tensor_tensor(parts[:, e, 1, :], raw[:, 0, at, :], parts[:, e, 0, :].bitcast(F32),
                                        ALU.subtract).then_inc(w1_low, 1)
                pool.wait_ge(w2_high, e + 1)
                nc.gpsimd.tensor_tensor(parts[:, e, 3, :], cen[:, e % 2, :], parts[:, e, 2, :].bitcast(F32),
                                        ALU.subtract).then_inc(w2_low, 1)

            def low(e, f, begin=False):
                pool.wait_ge(hi_ok, e * FT + (f + 1))
                if not begin:
                    pool.wait_ge(mm2_done, e * FT + (f + 1 - FT))
                nc.gpsimd.tensor_tensor(hs[:, 1, f, :], rel[:, f, :], hs[:, 0, f, :].bitcast(F32),
                                        ALU.subtract).then_inc(lo_pool, 1)

            def gamma(e):
                pool.wait_ge(z_ok, e + 2)
                pool.wait_ge(acc_ok, e + 1)
                row = gbc[:, e:e + 1, :] if isinstance(e, int) else gbc[:, bass.ds(e, 1), :]
                nc.gpsimd.tensor_tensor(zg[:, :, :], z[:, :, :], row.to_broadcast([128, TILES, D]), ALU.mult).then_inc(zg_ok, 1)

            def add(e):
                pool.wait_ge(zg_ok, e + 2)
                nc.gpsimd.tensor_tensor(acc[:, :, :], acc[:, :, :], zg[:, :, :], ALU.add).then_inc(acc_ok, 1)

            def window(e, begin=False, end=False):
                low(e, 3, begin)
                if not end:
                    low(e + 1, 1)
                if not begin:
                    gamma(e - 1)
                    add(e - 1)

            low(0, 1, begin=True)
            pool.wait_ge(s_gb, 32)
            window(0, begin=True)
            with pool.Fori(0, E // 2 - 1) as i:
                window(i * 2 + 1)
                window(i * 2 + 2)
            window(E - 1, end=True)

        @block.tensor
        def _(pe):
            pe.wait_ge(s_cst, 16)
            def stay_awake(n, bank):
                for _ in range(n):
                    nc.tensor.matmul(PS[:, bank, BANK - 128:BANK], ident, ident, start=True, stop=True)

            def turn(k):
                if k >= 2:
                    pe.wait_ge(xt_sb, k - 1)
                for j in range(SIDE):
                    if k < 6:
                        pix, rows = own_px[:, k, j, :], 128
                    elif k == 6:
                        pix, rows = halo[:, j, 0:2, :, :].rearrange("p c s i -> p (c s i)"), 128
                    else:
                        pix, rows = halo[:, j, 2, :, :].rearrange("p s i -> p (s i)"), 64
                    mm = nc.tensor.transpose(PS[0:rows, 2 * (k % 2) + j // 3, 96 * (j % 3):96 * (j % 3) + 96], pix,
                                             ident[0:96, 0:96])
                mm.then_inc(xt_ps, 1)

            for k in range(6):
                stay_awake(1, 5)
                pe.wait_ge(px_dve if k % 3 == 2 else px_act, 1 + k // 3 if k % 3 == 2 else 2 * (k // 3) + k % 3 + 1)
                turn(k)
            stay_awake(2, 5)
            for k in range(8):
                if k == 3:
                    pe.wait_ge(halo_ok, 12)
                    turn(6)
                    turn(7)
                if k == 5:
                    pe.wait_ge(s_wt, 32)
                    for v in range(4):
                        mm = nc.tensor.transpose(PS[:, 5, 128 * v:128 * v + 128], wt[:, v, :], ident)
                    mm.then_inc(small_ps, 1)
                    pe.wait_ge(s_vec, 160)
                    nc.tensor.transpose(PS[:, 4, 0:NV], vec[0:NV, :], ident[0:NV, 0:NV]).then_inc(small_ps, 1)
                if k == 7:
                    pe.wait_ge(small_sb, 2)
                    nc.tensor.matmul(PS[:, 4, 128:128 + NV], centre, vecT[:, :], start=True, stop=True).then_inc(small_ps, 1)
                pe.wait_ge(wk_ok, k + 1)
                pe.wait_ge(xt_sb, k + 1)
                rows = 128 if k < 7 else 64
                for n, (a, b) in enumerate(PCUTS):
                    mm = nc.tensor.matmul(PS[:, 6 + n, 0:b - a], wkc[0:rows, k, :], XT[0:rows, k, a:b],
                                          start=(k == 0), stop=(k == 7))
            mm.then_inc(conv_ps, 1)
            pe.wait_ge(s_dw, 16)
            pe.wait_ge(small_sb, 3)
            nc.tensor.matmul(PS[:, 4, 200:201], dw[:, :], vecT[:, V_TB:V_TB + 1], start=True, stop=True).then_inc(small_ps, 1)

            def squares(n, bank):
                pe.wait_ge(sq_ok, n)
                for t in range(TILES):
                    mm = nc.tensor.matmul(PS[:, bank, t:t + 1], sq[:, 128 * t:128 * t + 128], ones[:, :], start=True, stop=True)
                mm.then_inc(var_ps, 1)

            def spread(n, bank):
                for t in range(TILES):
                    pe.wait_ge(diag_ok, TILES * (n - 1) + t + 1)
                    mm = nc.tensor.matmul(tile5(bank, t), twos[:, :], diag[:, t, :], start=True, stop=True)
                mm.then_inc(bc_ps, 1)

            pe.wait_ge(y_ok, 1)
            pe.wait_ge(dense_ok, 2)
            for v in (1, 0):
                for n, (a, b) in enumerate(PCUTS):
                    mm = nc.tensor.matmul(PS[:, 2 * v + n, 0:b - a], dwg[:, v, :], ysb[:, a:b], start=True, stop=True)
                mm.then_inc(t_ps, 1)
                if v == 1:
                    squares(1, 6)
            stay_awake(2, 7)
            pe.wait_ge(small_sb, 4)
            nc.tensor.matmul(PS[:, 4, 202:203], centre, c0[:, 0:1], start=True, stop=True).then_inc(small_ps, 1)
            pe.wait_ge(small_sb, 5)
            stay_awake(3, 7)
            spread(1, 4)
            stay_awake(12, 7)
            squares(2, 6)
            stay_awake(8, 7)
            spread(2, 4)
            stay_awake(8, 7)
            pe.wait_ge(wpart_ok, 3)
            pe.wait_ge(xs_ok, 1)
            for which, bank in ((1, 0), (0, 2), (2, 6)):
                for n, (a, b) in enumerate(CUTS):
                    for part in range(3):
                        mm = nc.tensor.matmul(PS[:, bank + n, 0:b - a], wpart[:, part, which, :], xs[:, a:b],
                                              start=(part == 0), stop=(part == 2))
                mm.then_inc(qkv_ps, 1)

            def scores(rnd, banks):
                for p in range(4):
                    pr = 4 * rnd + p
                    for half in range(2):
                        col = NT * (2 * pr + half)
                        for hp in range(4):
                            mm = nc.tensor.matmul(
                                PS[64 * half:64 * half + 64, banks[hp], 2 * NT * p:2 * NT * p + 2 * NT],
                                kvs[32 * hp:32 * hp + 32, 0, col:col + 64], qe[32 * hp:32 * hp + 32, :, col:col + NT],
                                start=True, stop=True)
                mm.then_inc(sc_ps, 1)

            stay_awake(28, 4)
            pe.wait_ge(spike_ok, 3)
            pe.wait_ge(pre_ok, 2)
            scores(0, (0, 1, 2, 3))
            pe.wait_ge(spike_ok, 4)
            for pr in range(B // 2):
                for half in range(2):
                    col = NT * (2 * pr + half)
                    mm = nc.tensor.transpose(PS[64 * half:64 * half + 64, 5, 64 * pr:64 * pr + 64].bitcast(BF16),
                                             kvs[:, 1, col:col + 64], identb[:, :])
            mm.then_inc(vt_ps, 1)
            stay_awake(4, 4)
            pe.wait_ge(vt_sb, 1)
            pe.wait_ge(pre_ok, 3)
            scores(1, (4, 5, 6, 7))
            for rnd in range(2):
                pe.wait_ge(sc_sb, 2)
                stay_awake(2, 3)
                for p in range(4):
                    pr = 4 * rnd + p
                    if rnd:
                        pe.wait_ge(sc_sb, 3 + p // 2)
                    for half in range(2):
                        rows = slice(64 * half, 64 * half + NT)
                        for hp in range(4):
                            mm = nc.tensor.matmul(
                                PS[32 * hp:32 * hp + 32, 2 * rnd + half, 2 * NT * p:2 * NT * p + 2 * NT],
                                vtok[rows, pr, 32 * hp:32 * hp + 32], A[rows, hp, pr, :], start=True, stop=True)
                mm.then_inc(av_ps, 1)
            stay_awake(9, 4)
            pe.wait_ge(os_ok, 1)
            for which, bank in ((4, 6), (3, 4)):
                for n, (a, b) in enumerate(CUTS):
                    for part in range(3):
                        mm = nc.tensor.matmul(PS[:, bank + n, 0:b - a], wpart[:, part, which, :], os_[:, a:b],
                                              start=(part == 0), stop=(part == 2))
                mm.then_inc(proj_ps, 1)
            stay_awake(4, 1)
            squares(3, 0)
            stay_awake(8, 1)
            spread(3, 2)
            pe.wait_ge(h2_ok, 2)
            for t in range(TILES):
                n = min(128, TOK - 128 * t)
                mm = nc.tensor.transpose(tile5(6, t, n), H[:, :, :].rearrange("p b n -> p (b n)")[:, 128 * t:128 * t + n], ident)
            mm.then_inc(h2t_ps, 1)
            pe.wait_ge(x3_ok, 1)
            pe.wait_ge(s_rw, 16)
            for t in range(TILES):
                mm = nc.tensor.matmul(PS[:, 0, 16 + E * t:16 + E * t + E], X3[:, 128 * t:128 * t + 128], rw[:, :], start=True, stop=True)
            mm.then_inc(lg_ps, 1)
            stay_awake(2, 1)
            pe.wait_ge(lg_sb, 1)
            pe.wait_ge(bc_ps, 3)

            def exact(bank, w, x, start, stop, closed=None):
                for n in range(2):
                    if closed is not None:
                        pe.wait_ge(ysum_ok, closed * 2 + (n - 1))
                    for k, (i, j) in enumerate(((0, 0), (0, 1), (1, 0))):
                        mm = nc.tensor.matmul(PS[:, bank + n, 0:TOK // 2], w[i], x[j][:, n * TOK // 2:(n + 1) * TOK // 2],
                                              start=start and k == 0, stop=stop and k == 2)
                return mm

            def first(slot, f):
                exact(2 * (f % 2), [slot_w[:, slot, k, 128 * f:128 * f + 128] for k in (0, 1)],
                      [X3p[:, k, :] for k in (0, 1)], True, True).then_inc(g_ps, 1)

            def second(slot, f, closed):
                exact(4, [slot_w[:, slot, k, 128 * f:128 * f + 128] for k in (2, 3)],
                      [hs[:, k, f, :] for k in (0, 1)], f == 0, f == FT - 1, closed).then_inc(mm2_done, 1)

            def turn_back():
                for t in range(TILES):
                    mm = nc.tensor.transpose(tile5(6, t), ysum[:, 128 * t:128 * t + 128], ident)
                mm.then_inc(turn_ps, 1)

            def window(pair, slot, begin=False, end=False):
                e = pair * 2 + slot
                for f in range(FT):
                    if f == 0 or not end:
                        pe.wait_ge(relu_ok, e * FT + (f + 2))
                    if f == 0:
                        first(slot, FT - 1)
                        pe.wait_ge(w2_slot[slot], pair * 16 + 16)
                    elif not end:
                        if f == 1:
                            pe.wait_ge(w1_slot[1 - slot], pair * 16 + 16 * (1 + slot))
                        first(1 - slot, f - 1)
                    pe.wait_ge(hi_ok, e * FT + (f + 1))
                    if f % 2:
                        pe.wait_ge(lo_pool, e * 2 + (f // 2 + 1))
                    else:
                        pe.wait_ge(lo_dve, e * 2 + (f // 2 + 1))
                    second(slot, f, None if begin or f else e)
                    if f == 0 and not begin:
                        pe.wait_ge(z_ok, e)
                        turn_back()

            pe.wait_ge(w1_slot[0], 16)
            pe.wait_ge(x3p_ok, 2)
            first(0, 0)
            first(0, 1)
            pe.wait_ge(relu_ok, 1)
            first(0, 2)
            window(0, 0, begin=True)
            with pe.Fori(0, E // 2 - 1) as i:
                window(i, 1)
                window(i + 1, 0)
            window(E // 2 - 1, 1, end=True)
            pe.wait_ge(gate_ok, 1)
            for t in range(TILES):
                mm = nc.tensor.transpose(tile5(0, t, E), W8[:, t, :], ident)
            mm.then_inc(wT_ps, 1)
            pe.wait_ge(ysum_ok, 2 * E)
            pe.wait_ge(z_ok, E)
            turn_back()
            pe.wait_ge(s_gb, 32)
            pe.wait_ge(wT_sb, 1)
            for t in range(TILES):
                mm = nc.tensor.matmul(tile5(2, t), wT[:, 128 * t:128 * t + 128], fb[:, :], start=True, stop=True)
            mm.then_inc(beta_ps, 1)

        @block.scalar
        def _(act):
            def own_pixels(m):
                act.wait_ge(s_x[m], 16)
                for c in (0, 1):
                    gather(nc.scalar.copy, 3 * m + c).then_inc(px_act, 1)

            def evacuate(k):
                rows = 128 if k < 7 else 64
                act.wait_ge(xt_ps, k + 1)
                at = 2 * (k % 2)
                nc.scalar.copy(
                    XT[0:rows, k, :].rearrange("p (q b j) -> p b j q", j=3, b=2),
                    PS[0:rows, at:at + 2, 0:288].rearrange("p b (j q) -> p b j q", j=3)).then_inc(xt_sb, 1)

            own_pixels(0)
            evacuate(0)
            evacuate(1)
            own_pixels(1)
            for k in range(2, 6):
                evacuate(k)
            act.wait_ge(s_cst, 16)
            nc.scalar.activation(junk[:, 0, 0:1], cst[:, C_EPS:C_EPS + 1], ACT.Sqrt).then_inc(act_own, 1)
            evacuate(6)
            evacuate(7)
            act.wait_ge(small_ps, 1)
            nc.scalar.copy(wtT[:, 0:4, :], PS[:, 5, :].rearrange("p (k c) -> p k c", k=4)).then_inc(small_sb, 1)
            act.wait_ge(small_ps, 2)
            nc.scalar.copy(vecT[:, :], PS[:, 4, 0:NV]).then_inc(small_sb, 1)
            act.wait_ge(small_ps, 3)
            nc.scalar.copy(vecC[:, :], PS[:, 4, 128:128 + NV]).then_inc(small_sb, 1)
            def bf16_part(part):
                if part:
                    act.wait_ge(wrem_ok, part)
                src = wrem[:, part - 1, :, :] if part else wtT[:, :, :]
                nc.scalar.copy(wpart[:, part, :, :], src).then_inc(wpart_ok, 1)

            def means(e):
                act.wait_ge(s_w2[e], 16)
                for f in range(FT):
                    m = nc.scalar.activation(junk[:, f, :], raw[:, 1, e % (E // 2), 128 * f:128 * f + 128], ACT.Identity,
                                             scale=1.0 / D, accum_out=w2m[:, e, f:f + 1])
                m.then_inc(w2m_ok, 1)

            def high_first(e):
                act.wait_ge(s_w1[e], 16)
                nc.scalar.copy(parts[:, e, 0, :], raw[:, 0, e % (E // 2), :]).then_inc(w1_high, 1)

            def high_second(e):
                act.wait_ge(w2_cen, e + 1)
                nc.scalar.copy(parts[:, e, 2, :], cen[:, e % 2, :]).then_inc(w2_high, 1)

            act.wait_ge(conv_ps, 1)
            act.wait_ge(small_sb, 3)
            nc.scalar.activation(ysb[:, :], wide(6, PTOK), ACT.Identity, bias=vecC[:, V_CONVB:V_CONVB + 1]).then_inc(y_ok, 1)
            act.wait_ge(tails, 8)
            act.wait_ge(h_ok, 2)
            nc.scalar.activation(sq[:, 0:PTOK], wide(6, PTOK), ACT.Square, bias=vecC[:, V_CONVB:V_CONVB + 1]).then_inc(sq_ok, 1)
            act.wait_ge(wcen_ok, 1)
            bf16_part(0)
            act.wait_ge(small_ps, 4)
            nc.scalar.activation(c0[:, 0:1], PS[:, 4, 200:201], ACT.Identity,
                                 bias=vecT[:, V_DENSEB:V_DENSEB + 1]).then_inc(small_sb, 1)

            def root(n):
                act.wait_ge(v_ok, n)
                nc.scalar.activation(r_s[:, :], r_v[:, :], ACT.Sqrt).then_inc(root_ok, 1)

            act.wait_ge(t_ps, 1)
            nc.scalar.copy(h0[:, 1, :], wide(2, PTOK)).then_inc(t_sb, 1)
            high_first(0)
            root(1)
            act.wait_ge(t_ps, 2)
            nc.scalar.copy(h0[:, 0, :], wide(0, PTOK)).then_inc(t_sb, 1)
            act.wait_ge(small_ps, 5)
            nc.scalar.copy(c0[:, 1:2], PS[:, 4, 202:203]).then_inc(small_sb, 1)
            high_second(0)
            high_first(1)
            bf16_part(1)
            high_second(1)
            act.wait_ge(h0_ok, 1)
            act.wait_ge(small_sb, 5)
            nc.scalar.activation(Hc[:, :, 1:NT], h1[:, :].rearrange("p (b n) -> p b n", b=B), ACT.Identity,
                                 bias=c0[:, 1:2]).then_inc(h_ok, 1)
            act.wait_ge(h_ok, 3)
            nc.scalar.activation(sq[:, 0:TOK], Hc[:, :, :].rearrange("p b n -> p (b n)"), ACT.Square).then_inc(sq_ok, 1)
            root(2)
            act.wait_ge(h0_ok, 2)
            nc.scalar.activation(H[:, :, 1:NT], ysb[:, :].rearrange("p (b n) -> p b n", b=B), ACT.Identity,
                                 bias=c0[:, 0:1]).then_inc(h_ok, 1)
            bf16_part(2)
            high_first(2)
            means(4)
            high_second(2)
            high_first(3)
            high_first(4)
            high_second(3)
            means(5)
            high_first(5)
            act.wait_ge(bn_var, 1)
            nc.scalar.activation(bn_s[:, 0, :], bnmv[:, :, 1], ACT.Sqrt, bias=cst[:, C_EPS + 1:C_EPS + 2]).then_inc(bn_root, 1)
            high_second(4)
            act.wait_ge(bn_ok, 1)
            for which, bank in ((1, 0), (0, 2), (2, 6)):
                nc.scalar.activation(pre[:, which, :], wide(bank, TOK), ACT.Relu, scale=bn_scale[:, which:which + 1],
                                     bias=bn_shift[:, which:which + 1]).then_inc(pre_ok, 1)
            high_second(5)
            means(6)
            high_first(6)
            act.wait_ge(vt_ps, 1)
            nc.scalar.copy(vtok[:, :, :].rearrange("p r d -> p (r d)"), PS[:, 5, :].bitcast(BF16)).then_inc(vt_sb, 1)
            high_second(6)
            means(7)
            high_first(7)
            high_second(7)
            act.wait_ge(h2_ok, 1)
            nc.scalar.activation(sq[:, 0:TOK], Hc[:, :, :].rearrange("p b n -> p (b n)"), ACT.Square).then_inc(sq_ok, 1)
            root(3)
            act.wait_ge(h2t_ps, 1)
            nc.scalar.copy(acc[:, 0:4, :], PS[:, 6, :].rearrange("p (t d) -> p t d", d=D)).then_inc(acc_ok, 1)
            nc.scalar.copy(acc[0:TOK - 512, 4, :], PS[0:TOK - 512, 7, 0:D]).then_inc(z_ok, 1)
            def relu(e, slot, f, pair, begin=False):
                act.wait_ge(g_ps, e * FT + (f + 1))
                if f == 0:
                    act.wait_ge(b1_slot[slot], pair * 16 + 16)
                if not begin:
                    act.wait_ge(hi_ok, e * FT + (f + 1 - FT))
                    act.wait_ge(lo_pool if f % 2 else lo_dve, e * 2 + (f // 2 - 1))
                nc.scalar.activation(in_halves(rel[:, f, :]), halves(2 * (f % 2)), ACT.Relu, bias=b1s[:, slot, f:f + 1]).then_inc(relu_ok, 1)

            def statistics(e):
                act.wait_ge(turn_ps, e + 1)
                for t in range(TILES):
                    nc.scalar.activation(junk[:, t, :], tile5(6, t), ACT.Square,
                                         accum_out=ssq[:, t:t + 1]).then_inc(ssq_ok, 1)
                act.wait_ge(ssq_ok, e * TILES + TILES)
                nc.scalar.activation(f_s[:, 0, :], ssq[:, :], ACT.Sqrt, scale=1.0 / D,
                                     bias=cst[:, C_EPS + 2:C_EPS + 3]).then_inc(froot, 1)

            def scale(e):
                act.wait_ge(ffac, e + 1)
                act.wait_ge(zg_ok, e + 1)
                for t in range(TILES):
                    zt = nc.scalar.activation(z[:, t, :], tile5(6, t), ACT.Copy, scale=frw[:, t:t + 1])
                zt.then_inc(z_ok, 1)

            def window(pair, slot, begin=False, end=False):
                e = pair * 2 + slot
                relu(e, slot, 3, pair, begin)
                if not begin:
                    statistics(e - 1)
                if not end:
                    relu(e + 1, 1 - slot, 0, pair + slot)
                    relu(e + 1, 1 - slot, 1, pair + slot)
                if not begin:
                    scale(e - 1)
                if not end:
                    relu(e + 1, 1 - slot, 2, pair + slot)

            relu(0, 0, 0, 0, begin=True)
            relu(0, 0, 1, 0, begin=True)
            relu(0, 0, 2, 0, begin=True)
            window(0, 0, begin=True)
            act.wait_ge(gap, 1)
            nc.scalar.activation(gs[:, 3, :], gs[:, 2, :], ACT.Exp).then_inc(gexp, 1)
            act.wait_ge(gexp, 1)
            nc.scalar.activation(junk[:, 0, 0:1], cst[:, C_EPS:C_EPS + 1], ACT.Sqrt).then_inc(zg_ok, 1)
            act.wait_ge(zg_ok, 1)
            with act.Fori(0, E // 2 - 1) as i:
                window(i, 1)
                window(i + 1, 0)
            window(E // 2 - 1, 1, end=True)
            act.wait_ge(wT_ps, 1)
            nc.scalar.copy(wT[:, :], wide(0, PAD)[0:E, :]).then_inc(wT_sb, 1)
            statistics(E - 1)

        @block.vector
        def _(dve):
            own = Steps(dve, dve_own)

            for row in (0, PATCH + 1):
                nc.vector.memset(xin[:, row, :], 0.0).then_inc(pads, 1)
            nc.vector.memset(xin[:, 1:PATCH + 1, :].rearrange("p r (w c) -> p r w c", c=CH)[:, :, 0:IMG + 2:IMG + 1, :],
                             0.0).then_inc(pads, 1)
            for tile_, val in ((ones[:, :], 1.0), (twos[:, :], 2.0), (sq[:, :], 1.0), (kvs[:, :, TOK:PAD], 0.0),
                               (X3[:, TOK:PAD], 0.0), (ysum[:, TOK:PAD], 0.0), (acc[:, TILES - 1, :], 0.0)):
                nc.vector.memset(tile_, val).then_inc(tails, 1)
            def own_pixels(m):
                dve.wait_ge(s_x[m], 16)
                gather(nc.vector.tensor_copy, 3 * m + 2).then_inc(px_dve, 1)

            def centred(lo, hi, rows):
                own.then(nc.vector.tensor_reduce(mean8[0:rows, lo:hi], wk[0:rows, lo:hi, :], AX.X, ALU.add))
                own.then(nc.vector.tensor_scalar(nmean8[0:rows, lo:hi], mean8[0:rows, lo:hi], 1.0 / D, None, ALU.mult))
                nc.vector.tensor_tensor(wkc[0:rows, lo:hi, :], wk[0:rows, lo:hi, :],
                                        nmean8[0:rows, lo:hi].unsqueeze(2).to_broadcast([rows, hi - lo, D]),
                                        ALU.subtract).then_inc(wk_ok, hi - lo)

            own_pixels(0)
            own_pixels(1)
            dve.wait_ge(s_cst, 16)
            for m in range(2):
                flat = wk[:, 3 * m:3 * m + 3, :].rearrange("p c d -> p (c d)")
                dve.wait_ge(s_w[m][0], 16)
                for s in range(1, 5):
                    dve.wait_ge(s_w[m][s], 16)
                    if s < 3:
                        mask = cst[:, C_NOT_LAST:C_NOT_LAST + 1] if s == 1 else cst[:, C_NOT_FIRST:C_NOT_FIRST + 1]
                        own.then(nc.vector.scalar_tensor_tensor(flat, wsh[:, s, m, :], mask,
                                                                wsh[:, 0, m, :] if s == 1 else flat, ALU.mult, ALU.add))
                    else:
                        own.then(nc.vector.tensor_tensor(flat, wsh[:, s, m, :], flat, ALU.add))
                centred(3 * m, 3 * m + 3, 128)
            dve.wait_ge(s_whalo, 128)
            centred(6, 7, 128)
            centred(7, 8, 64)
            nc.vector.tensor_copy(identb[:, :], ident).then_inc(tails, 1)
            dve.wait_ge(s_dw, 16)
            dve.wait_ge(small_sb, 2)
            own.then(nc.vector.tensor_scalar(dwg[:, 0, :], dw[:, :], vecT[:, V_TG:V_TG + 1], None, ALU.mult))
            own.then(nc.vector.tensor_reduce(mean8[:, 0:1], dwg[:, 0, :], AX.X, ALU.add))
            own.then(nc.vector.tensor_scalar(nmean8[:, 0:1], mean8[:, 0:1], 1.0 / D, None, ALU.mult))
            nc.vector.tensor_scalar(dwg[:, 1, :], dwg[:, 0, :], nmean8[:, 0:1], None, ALU.subtract).then_inc(dense_ok, 2)
            dve.wait_ge(small_sb, 1)
            own.then(nc.vector.tensor_reduce(mean8[:, 1:2], wtT[:, 3, :], AX.X, ALU.add))
            own.then(nc.vector.tensor_scalar(nmean8[:, 1:2], mean8[:, 1:2], 1.0 / D, None, ALU.mult))
            nc.vector.tensor_scalar(wtT[:, 4, :], wtT[:, 3, :], nmean8[:, 1:2], None, ALU.subtract).then_inc(wcen_ok, 1)
            def row_means(e):
                dve.wait_ge(s_w2[e], 16)
                own.then(nc.vector.tensor_reduce(w2s[:, e, :], raw[:, 1, e % (E // 2), :].rearrange("p (f d) -> p f d", d=D),
                                                 AX.X, ALU.add))
                nc.vector.tensor_scalar(w2m[:, e, :], w2s[:, e, :], 1.0 / D, None, ALU.mult).then_inc(w2m_ok, 1)

            row_means(0)
            row_means(1)

            def factor(n, bank):
                dve.wait_ge(var_ps, n)
                nc.vector.tensor_scalar(r_v[:, :], PS[:, bank, 0:TILES], 1.0 / D, EPS[n - 1], ALU.mult, ALU.add).then_inc(v_ok, 1)
                dve.wait_ge(root_ok, n)
                own.then(nc.vector.reciprocal(r_a[:, :], r_s[:, :]))
                own.then(nc.vector.tensor_tensor(r_b[:, :], r_v[:, :], r_a[:, :], ALU.mult))
                own.then(nc.vector.tensor_tensor(r_c[:, :], r_b[:, :], r_s[:, :], ALU.add))
                own.then(nc.vector.reciprocal(r_h[:, :], r_c[:, :]))
                for t in range(TILES):
                    nc.vector.tensor_scalar(diag[:, t, :], ident, r_h[:, t:t + 1], None, ALU.mult).then_inc(diag_ok, 1)

            factor(1, 6)
            row_means(2)
            row_means(3)
            dve.wait_ge(bc_ps, 1)
            dve.wait_ge(t_sb, 1)
            nc.vector.tensor_tensor(h1[:, :], wide(4, PTOK), h0[:, 1, :], ALU.mult).then_inc(h0_ok, 1)
            dve.wait_ge(t_sb, 2)
            nc.vector.tensor_tensor(ysb[:, :], wide(4, PTOK), h0[:, 0, :], ALU.mult).then_inc(h0_ok, 1)
            factor(2, 6)
            flat_c = Hc[:, :, :].rearrange("p b n -> p (b n)")
            flat_h = H[:, :, :].rearrange("p b n -> p (b n)")
            dve.wait_ge(bc_ps, 2)
            own.then(nc.vector.scalar_tensor_tensor(spk[:, :], flat_c, 0.0, wide(4, TOK), ALU.max, ALU.mult))
            own.then(nc.vector.tensor_scalar(spk2[:, :], spk[:, :], TIE, CAP, ALU.add, ALU.min))
            nc.vector.tensor_scalar(xs[:, :], spk2[:, :], RNE, RNE, ALU.add, ALU.subtract).then_inc(xs_ok, 1)
            for n, (which, bank) in enumerate(((1, 0), (0, 2), (2, 6))):
                dve.wait_ge(qkv_ps, n + 1)
                for c, (a, b) in enumerate(CUTS):
                    own.mark(nc.vector.bn_stats(bnst[:, which, c, :], PS[:, bank + c, 0:b - a]))
                own.wait()
                own.mark(nc.vector.bn_aggr(bnmv[:, which, :], bnst[:, which, :, :].rearrange("p c s -> p (c s)")))
            own.wait()
            mean, var = bnmv[:, :, 0], bnmv[:, :, 1]
            bn_v, bn_a, bn_b, bn_c, bn_h, bn_m = (bn_s[:, k, :] for k in range(1, 7))
            nc.vector.tensor_scalar(bn_v, var, EPS[1], None, ALU.add).then_inc(bn_var, 1)
            dve.wait_ge(bn_root, 1)
            dve.wait_ge(bn_var, 1)
            own.then(nc.vector.reciprocal(bn_a, bn_s[:, 0, :]))
            own.then(nc.vector.tensor_tensor(bn_b, bn_v, bn_a, ALU.mult))
            own.then(nc.vector.tensor_tensor(bn_c, bn_b, bn_s[:, 0, :], ALU.add))
            own.then(nc.vector.reciprocal(bn_h, bn_c))
            own.then(nc.vector.scalar_tensor_tensor(bn_scale[:, :], bn_h, 2.0, vecT[:, V_AG:V_AG + 3], ALU.mult, ALU.mult))
            own.then(nc.vector.tensor_tensor(bn_m, mean, bn_scale[:, :], ALU.mult))
            nc.vector.scalar_tensor_tensor(bn_shift[:, :], vecT[:, V_AB:V_AB + 3], TIE, bn_m, ALU.add,
                                           ALU.subtract).then_inc(bn_ok, 1)
            for n, which in enumerate((1, 0, 2)):
                dve.wait_ge(pre_ok, n + 1)
                own.then(nc.vector.tensor_scalar(pre2[:, which, :], pre[:, which, :], CAP, RNE, ALU.min, ALU.add))
                if which == 0:
                    for half, mask in ((0, C_EVEN), (1, C_ODD)):
                        nc.vector.tensor_scalar(qe[:, half, :], pre2[:, 0, :], RNE, cst[:, mask:mask + 1],
                                                ALU.subtract, ALU.mult).then_inc(spike_ok, 1)
                else:
                    nc.vector.tensor_scalar(kvs[:, which // 2, 0:TOK], pre2[:, which, :], RNE, None,
                                            ALU.subtract).then_inc(spike_ok, 1)
            for rnd in range(2):
                dve.wait_ge(sc_ps, rnd + 1)
                for two in range(2):
                    pr = 4 * rnd + 2 * two
                    nc.vector.tensor_scalar(A[:, :, pr:pr + 2, :].rearrange("p g r n -> p g (r n)"),
                                            PS[:, 4 * rnd:4 * rnd + 4, 4 * NT * two:4 * NT * two + 4 * NT], CAP, None,
                                            ALU.min).then_inc(sc_sb, 1)
            for rnd in range(2):
                dve.wait_ge(av_ps, rnd + 1)
                o = [PS[:, 2 * rnd + half, 0:8 * NT].rearrange("p (r e n) -> p r e n", e=2, n=NT) for half in range(2)]
                for half in range(2):
                    own.mark(nc.vector.tensor_scalar(av0[:, 2 * rnd + half, :, :], o[half][:, :, 0, :],
                                                     evens[:, 0:1], TIE, ALU.mult, ALU.add))
                for half in range(2):
                    dve.wait_ge(dve_own, own.n - 1)
                    own.mark(nc.vector.scalar_tensor_tensor(av[:, 8 * rnd + half:8 * rnd + 8:2, :], o[half][:, :, 1, :],
                                                            evens[:, 1:2], av0[:, 2 * rnd + half, :, :], ALU.mult, ALU.add))
            own.wait()
            own.then(nc.vector.tensor_scalar(av2[:, :], av[:, :, :].rearrange("p b n -> p (b n)"), CAP, RNE, ALU.min, ALU.add))
            nc.vector.tensor_scalar(os_[:, :], av2[:, :], RNE, None, ALU.subtract).then_inc(os_ok, 1)
            dve.wait_ge(proj_ps, 1)
            nc.vector.scalar_tensor_tensor(flat_c, wide(6, TOK), vecC[:, V_BPROJ:V_BPROJ + 1], flat_c, ALU.add,
                                           ALU.add).then_inc(h2_ok, 1)
            dve.wait_ge(proj_ps, 2)
            nc.vector.scalar_tensor_tensor(flat_h, wide(4, TOK), vecT[:, V_BPROJ:V_BPROJ + 1], flat_h, ALU.add,
                                           ALU.add).then_inc(h2_ok, 1)
            factor(3, 0)
            dve.wait_ge(bc_ps, 3)
            nc.vector.tensor_tensor(X3[:, 0:TOK], wide(2, TOK), flat_c, ALU.mult).then_inc(x3_ok, 1)
            dve.wait_ge(x3_ok, 1)
            nc.vector.tensor_copy(X3p[:, 0, :], X3[:, 0:TOK]).then_inc(x3p_ok, 1)
            dve.wait_ge(x3p_ok, 1)
            nc.vector.tensor_tensor(X3p[:, 1, :], X3[:, 0:TOK], X3p[:, 0, :].bitcast(F32), ALU.subtract).then_inc(x3p_ok, 1)

            def split(e, f, begin=False):
                dve.wait_ge(relu_ok, e * FT + (f + 1))
                if not begin:
                    dve.wait_ge(mm2_done, e * FT + (f + 1 - FT))
                nc.vector.tensor_copy(hs[:, 0, f, :], rel[:, f, :]).then_inc(hi_ok, 1)
                if f % 2 == 0:
                    dve.wait_ge(hi_ok, e * FT + (f + 1))
                    nc.vector.tensor_tensor(hs[:, 1, f, :], rel[:, f, :], hs[:, 0, f, :].bitcast(F32),
                                            ALU.subtract).then_inc(lo_dve, 1)

            def bc(col):
                return col.unsqueeze(2).to_broadcast([128, TILES, E])

            dve.wait_ge(lg_ps, 1)
            nc.vector.tensor_copy(L[:, :, :], PS[:, 0, 16:16 + TILES * E].rearrange("p (t e) -> p t e", e=E)).then_inc(lg_sb, 1)
            dve.wait_ge(lg_sb, 1)
            rank = cst[:, C_RANK:C_RANK + E].unsqueeze(1).to_broadcast([128, TILES, E])

            def best(level, values, top, pick):
                own.then(nc.vector.tensor_reduce(top, values, AX.X, ALU.max))
                own.then(nc.vector.tensor_tensor(g[0][:, :, :], values, bc(top), ALU.is_equal))
                own.then(nc.vector.tensor_tensor(g[1][:, :, :], g[0][:, :, :], rank, ALU.mult))
                own.then(nc.vector.tensor_reduce(gs[:, 5, :], g[1][:, :, :], AX.X, ALU.max))
                own.then(nc.vector.tensor_tensor(pick, g[1][:, :, :], bc(gs[:, 5, :]), ALU.is_equal))

            best(0, L[:, :, :], gs[:, 0, :], g[2][:, :, :])
            split(0, 0, begin=True)
            split(0, 1, begin=True)
            own.then(nc.vector.scalar_tensor_tensor(g[3][:, :, :], g[2][:, :, :], -3.0e38, L[:, :, :], ALU.mult, ALU.add))
            best(1, g[3][:, :, :], gs[:, 1, :], g[4][:, :, :])
            nc.vector.tensor_tensor(gs[:, 2, :], gs[:, 1, :], gs[:, 0, :], ALU.subtract).then_inc(gap, 1)
            def close_sum(e):
                dve.wait_ge(mm2_done, e * FT + FT)
                if not (isinstance(e, int) and e == 0):
                    dve.wait_ge(turn_ps, e)
                bias = vecC[:, V_B2 + e:V_B2 + e + 1] if isinstance(e, int) else vecC[:, bass.ds(e + V_B2, 1)]
                for half in range(2):
                    cols = slice(half * TOK // 2, (half + 1) * TOK // 2)
                    nc.vector.scalar_tensor_tensor(ysum[:, cols], PS[:, 4 + half, 0:TOK // 2], bias, X3[:, cols], ALU.add,
                                                   ALU.add).then_inc(ysum_ok, 1)

            def finish(e):
                dve.wait_ge(ssq_ok, e * TILES + TILES)
                nc.vector.tensor_scalar(f_s[:, 1, :], ssq[:, :], 1.0 / D, EPS[2], ALU.mult, ALU.add).then_inc(fch, 1)
                dve.wait_ge(froot, e + 1)
                nc.vector.reciprocal(f_s[:, 2, :], f_s[:, 0, :]).then_inc(fch, 1)
                dve.wait_ge(fch, e * 5 + 2)
                nc.vector.tensor_tensor(f_s[:, 3, :], f_s[:, 1, :], f_s[:, 2, :], ALU.mult).then_inc(fch, 1)
                dve.wait_ge(fch, e * 5 + 3)
                nc.vector.tensor_tensor(f_s[:, 4, :], f_s[:, 3, :], f_s[:, 0, :], ALU.add).then_inc(fch, 1)
                dve.wait_ge(fch, e * 5 + 4)
                nc.vector.reciprocal(f_s[:, 5, :], f_s[:, 4, :]).then_inc(fch, 1)
                dve.wait_ge(fch, e * 5 + 5)
                dve.wait_ge(z_ok, e + 1)
                gate = W8[:, :, e:e + 1] if isinstance(e, int) else W8[:, :, bass.ds(e, 1)]
                nc.vector.scalar_tensor_tensor(frw[:, :], f_s[:, 5, :], 2.0, gate.rearrange("p t o -> p (t o)"), ALU.mult,
                                               ALU.mult).then_inc(ffac, 1)

            def window(e, end=False):
                split(e, 3)
                finish(e - 1)
                if not end:
                    split(e + 1, 0)
                    split(e + 1, 1)
                close_sum(e)
                if not end:
                    split(e + 1, 2)

            split(0, 2, begin=True)
            split(0, 3, begin=True)
            split(1, 0)
            split(1, 1)
            close_sum(0)
            split(1, 2)
            dve.wait_ge(gexp, 1)
            own.then(nc.vector.tensor_scalar(gs[:, 4, :], gs[:, 3, :], 1.0, None, ALU.add))
            own.then(nc.vector.reciprocal(gs[:, 5, :], gs[:, 4, :]))
            own.then(nc.vector.tensor_tensor(gs[:, 4, :], gs[:, 3, :], gs[:, 5, :], ALU.mult))
            own.then(nc.vector.tensor_tensor(g[0][:, :, :], g[2][:, :, :], bc(gs[:, 5, :]), ALU.mult))
            own.then(nc.vector.tensor_tensor(g[1][:, :, :], g[4][:, :, :], bc(gs[:, 4, :]), ALU.mult))
            nc.vector.tensor_tensor(W8[:, :, :], g[0][:, :, :], g[1][:, :, :], ALU.add).then_inc(gate_ok, 1)
            dve.wait_ge(gate_ok, 1)
            with dve.Fori(0, E // 2 - 1) as i:
                window(i * 2 + 1)
                window(i * 2 + 2)
            window(E - 1, end=True)
            dve.wait_ge(beta_ps, 1)
            dve.wait_ge(acc_ok, E)
            nc.vector.tensor_tensor(acc[:, :, :].rearrange("p t d -> p (t d)"), wide(2, PAD),
                                    acc[:, :, :].rearrange("p t d -> p (t d)"), ALU.add).then_inc(beta_sb, 1)
            finish(E - 1)
            dve.wait_ge(ffac, E)
            for t in range(TILES):
                nc.vector.scalar_tensor_tensor(zg[:, t, :], tile5(6, t), frw[:, t:t + 1], gbc[:, E - 1, :], ALU.mult,
                                               ALU.mult).then_inc(z_last, 1)
            dve.wait_ge(beta_sb, 1)
            for t in range(TILES):
                dve.wait_ge(z_last, t + 1)
                nc.vector.tensor_tensor(acc[:, t, :], acc[:, t, :], zg[:, t, :], ALU.add).then_inc(out_ok, 1)


_INS = ['x', 'cls_tok', 'L0_tok_conv_w', 'L0_tok_conv_b', 'L0_tok_gamma', 'L0_tok_beta', 'L0_tok_dense_w',
        'L0_tok_dense_b', 'L0_attn_Wqkv', 'L0_attn_gamma', 'L0_attn_beta', 'L0_attn_Wproj', 'L0_attn_bproj',
        'L0_ffn_router_w', 'L0_ffn_w1', 'L0_ffn_b1', 'L0_ffn_w2', 'L0_ffn_b2', 'L0_ffn_gamma', 'L0_ffn_beta']


def kernel(**inputs):
    import concourse.bacc as _bacc
    from concourse.bass_utils import run_bass_kernel_spmd as _run

    nc = _bacc.Bacc("TRN2", target_bir_lowering=False, num_devices=1)
    arrays = {"consts_dram": constants()}
    for name in _INS:
        arrays[f"in_{name}_dram"] = np.ascontiguousarray(inputs[name])
    args = [nc.dram_tensor(n, a.shape, F32, kind="ExternalInput").ap() for n, a in arrays.items()]
    out = nc.dram_tensor("out_dram", (B, NT, D), F32, kind="ExternalOutput").ap()
    vit_layer(nc, *args, out)
    r = _run(nc, [arrays], core_ids=[0])
    return r.results[0]["out_dram"]
```

```python
from contextlib import ExitStack

import numpy as np

import concourse.bass as bass
from concourse import mybir

F32 = mybir.dt.float32
BF16 = mybir.dt.bfloat16
F32R = mybir.dt.float32r
ALU = mybir.AluOpType
ACT = mybir.ActivationFunctionType
AX = mybir.AxisListType

B, IMG, CH, PATCH, D = 16, 96, 3, 16, 128
SIDE = IMG // PATCH
NP = SIDE * SIDE
NT = NP + 1
TOK = B * NT
PTOK = B * NP
TILES = -(-TOK // 128)
PAD = TILES * 128
HEADS, HD = 8, 16
E, F = 8, 512
FT = F // 128
BANK = 512
HALVES = (slice(0, TOK // 2), slice(TOK // 2, TOK))
ORDER = (0, 1, 2, 6, 7, 3, 4, 5)
PCUTS = ((0, BANK), (BANK, PTOK))
XROW = (IMG + 2) * CH
PAIRS = B // 2
EARLY = 5
LATE_BANKS = (4, 6, 7, 4)
K_FIRST = (2 * EARLY - 1) * NT + 64
RNE = float(2 ** 23)
TIE = float(2 ** -22)
CAP = 4.0

V_B1, V_B2, V_CONVB, V_TG, V_TB, V_DENSEB, V_AG, V_AB, V_BPROJ, V_CLS, NV = 0, 32, 40, 41, 42, 43, 44, 47, 50, 51, 52

C_ID, C_CENTRE, C_NOT_LAST, C_NOT_FIRST, C_EVEN, C_ODD, C_RANK, C_TOP, C_BOTTOM, C_EPS, C_KEEP, C_TIE, CN = \
    0, 128, 256, 257, 258, 259, 260, 268, 269, 270, 273, 275, 276
EPS = (1e-3, 1e-5, 1e-6)


def constants():
    p = np.arange(128)
    c = np.zeros((128, CN), np.float32)
    c[:, C_ID:C_ID + 128] = np.eye(128)
    c[:, C_CENTRE:C_CENTRE + 128] = np.eye(128) - 1.0 / 128
    c[:, C_NOT_LAST] = p % PATCH != PATCH - 1
    c[:, C_NOT_FIRST] = p % PATCH != 0
    c[:, C_EVEN] = (p // HD) % 2 == 0
    c[:, C_ODD] = (p // HD) % 2 == 1
    c[:, C_RANK:C_RANK + E] = E - np.arange(E)
    c[:, C_TOP] = p % SIDE != 0
    c[:, C_BOTTOM] = p % SIDE != SIDE - 1
    c[:, C_EPS:C_EPS + 3] = EPS
    c[:, C_KEEP] = c[:, C_EVEN] * HD ** -0.5
    c[:, C_KEEP + 1] = c[:, C_ODD] * HD ** -0.5
    c[:, C_TIE] = TIE
    return c


class Steps:

    def __init__(self, eng, sem):
        self.eng, self.sem, self.n = eng, sem, 0

    def mark(self, ins):
        self.n += 1
        ins.then_inc(self.sem, 1)

    def wait(self):
        self.eng.wait_ge(self.sem, self.n)

    def then(self, ins):
        self.mark(ins)
        self.wait()


def vit_layer(nc, consts, x, cls_tok, conv_w, conv_b, tok_g, tok_b, dense_w, dense_b, wqkv, attn_g, attn_b,
              wproj, bproj, router_w, w1, b1, w2, b2, ffn_g, ffn_b, out):
    with ExitStack() as ctx:
        def sb(name, shape, dt=F32):
            return ctx.enter_context(nc.sbuf_tensor(name, shape, dt))

        def sem(name):
            return ctx.enter_context(nc.semaphore(name))

        cst = sb("cst", [128, CN])
        ident = cst[:, C_ID:C_ID + 128]
        centre = cst[:, C_CENTRE:C_CENTRE + 128]
        evens = cst[:, C_KEEP:C_KEEP + 2]
        identb = sb("identb", [128, 128], BF16)
        ones = sb("ones", [128, 1])
        twos = sb("twos", [128, 128])
        vec = sb("vec", [64, 128])
        vecT = sb("vecT", [128, NV])
        vecC = sb("vecC", [128, NV])

        dw = sb("dw", [128, D])
        dwg = sb("dwg", [128, 2, D])
        c0 = sb("c0", [128, 2])
        ysb = sb("ysb", [128, PTOK])
        sq = sb("sq", [128, PAD])
        last_g = sq[:, :].rearrange("p (t d) -> p t d", d=D)
        r_s = sb("r_s", [128, TILES])
        r_v = sb("r_v", [128, TILES])
        r_a = sb("r_a", [128, TILES])
        r_b = sb("r_b", [128, TILES])
        r_c = sb("r_c", [128, TILES])
        r_h = sb("r_h", [128, TILES])
        diag = sb("diag", [128, TILES, 128])
        h0 = sb("h0", [128, 2, PTOK])
        h1 = sb("h1", [128, PTOK])
        H = sb("H", [128, B, NT])
        Hc = sb("Hc", [128, B, NT])

        wt = sb("wt", [128, 4, D])
        wtT = sb("wtT", [128, 5, D])
        wrem = sb("wrem", [128, 2, 5, D])
        wpart = sb("wpart", [128, 3, 5, D], BF16)
        xs = sb("xs", [128, TOK], BF16)
        bnst = sb("bnst", [128, 3, 2, 6])
        bnmv = sb("bnmv", [128, 3, 2])
        bn_s = sb("bn_s", [128, 8, 3])
        bn_scale = sb("bn_scale", [128, 3])
        bn_shift = sb("bn_shift", [128, 3])
        qe = sb("qe", [128, 2, TOK], BF16)
        kvs = sb("kvs", [128, 2, PAD], BF16)
        vtok = sb("vtok", [128, B // 2, D], BF16)
        A = sb("A", [128, 4, B // 2, 2 * NT], BF16)
        av2 = sb("av2", [128, TOK])
        os_ = sb("os", [128, TOK], BF16)

        X3 = sb("X3", [128, PAD])
        rw = sb("rw", [128, E])
        L = sb("L", [128, TILES, E])
        g = [sb(f"g{i}", [128, TILES, E]) for i in range(5)]
        gs = sb("gs", [128, 6, TILES])
        W8 = sb("W8", [128, TILES, E])
        wT = sb("wT", [E, PAD])
        fb = sb("fb", [E, D])
        gbc = sb("gbc", [128, E, D])
        ysum = sb("ysum", [128, PAD])
        junk = sb("junk", [128, TILES, 128], BF16)
        b1s = sb("b1s", [128, 2, FT])
        ssq = sb("ssq", [128, TILES])
        f_s = sb("f_s", [128, 6, TILES])
        frw = sb("frw", [128, TILES])
        z = sb("z", [128, TILES, D])
        zg = sb("zg", [128, TILES, D])
        acc = sb("acc", [128, TILES, D])

        with ExitStack() as scope:
            def room(name, shape, dt=F32):
                return scope.enter_context(nc.sbuf_tensor(name, shape, dt))

            xin = room("xin", [96, PATCH + 2, XROW])
            halo = room("halo", [96, SIDE, CH, 4, PATCH])
            own_px = room("own_px", [96, 6, SIDE, 128])
            XT = room("XT", [128, 8, PTOK])
            wsh = room("wsh", [128, 5, 2, CH * D])
            wk = room("wk", [128, 8, D])
            wkc = room("wkc", [128, 8, D])
            mean8 = room("mean8", [128, 8])
            nmean8 = room("nmean8", [128, 8])

        raw = sb("raw", [128, 2, E // 2, F])
        parts = sb("parts", [128, E, 4, F], F32R)
        slot_w = sb("slot_w", [128, 2, 4, F], F32R)
        cen = sb("cen", [128, 2, F])
        w2m = sb("w2m", [128, E, FT])
        w2s = sb("w2s", [128, E, FT])
        rel = sb("rel", [128, FT, TOK])
        with ExitStack() as scope:
            pre = scope.enter_context(nc.sbuf_tensor("pre", [128, 3, TOK], F32))
            pre2 = scope.enter_context(nc.sbuf_tensor("pre2", [128, 3, TOK], F32))
            spk = scope.enter_context(nc.sbuf_tensor("spk", [128, TOK], F32))
            spk2 = scope.enter_context(nc.sbuf_tensor("spk2", [128, TOK], F32))
            av0 = scope.enter_context(nc.sbuf_tensor("av0", [128, 4, 4, NT], F32))
            av = spk[:, :].rearrange("p (b n) -> p b n", n=NT)
        hs = sb("hs", [128, 2, FT, TOK], F32R)
        X3p = sb("X3p", [128, 2, TOK], F32R)

        PS = ctx.enter_context(nc.psum_tensor("PS", [128, 8, BANK], F32))

        def wide(bank, cols):
            return PS[:, bank:bank + 2, :].rearrange("p b n -> p (b n)")[:, 0:cols]

        def halves(bank):
            return PS[:, bank:bank + 2, 0:TOK // 2]

        def in_halves(row):
            return row.rearrange("p (h n) -> p h n", h=2)

        def tile5(bank, t, rows=128):
            return PS[0:rows, bank + t // 4, (t % 4) * 128:(t % 4) * 128 + 128]

        s_cst, s_x, s_vec = sem("s_cst"), [sem("s_x0"), sem("s_x1")], sem("s_vec")
        s_halo_rows, s_vec_pool = sem("s_halo_rows"), sem("s_vec_pool")
        s_w = [[sem(f"s_shift{i}_half{m}") for i in range(5)] for m in range(2)]
        s_whalo, s_wt, s_dw, s_rw, s_gb = (sem(n) for n in ("s_whalo", "s_wt", "s_dw", "s_rw", "s_gb"))
        four_w1, four_w2 = sem("four_w1"), sem("four_w2")
        s_w1 = [four_w1] * (E // 2) + [sem(f"s_w1_{e}") for e in range(E // 2, E)]
        s_w2 = [four_w2] * (E // 2) + [sem(f"s_w2_{e}") for e in range(E // 2, E)]
        pads = sem("pads")
        wpads = sem("wpads")
        tails = sem("tails")
        halo_ok = sem("halo_ok")
        px_act, px_dve = sem("px_act"), sem("px_dve")
        xt_ps, xt_sb = sem("xt_ps"), sem("xt_sb")
        small_ps, small_sb = sem("small_ps"), sem("small_sb")
        wk_ok, conv_ps, y_ok, sq_ok = sem("wk_ok"), sem("conv_ps"), sem("y_ok"), sem("sq_ok")
        dense_ok = sem("dense_ok")
        var_ps, v_ok, root_ok, diag_ok, bc_ps = sem("var_ps"), sem("v_ok"), sem("root_ok"), sem("diag_ok"), sem("bc_ps")
        t_ps, t_sb = sem("t_ps"), sem("t_sb")
        h0_ok, h_ok = sem("h0_ok"), sem("h_ok")
        r_ok, diag_act, out_pool = sem("r_ok"), sem("diag_act"), sem("out_pool")
        wcen_ok, wpart_ok, wrem_ok, xs_ok = sem("wcen_ok"), sem("wpart_ok"), sem("wrem_ok"), sem("xs_ok")
        w1_high, w1_low, w2_cen, w2_high, w2_low = (sem(n) for n in ("w1_high", "w1_low", "w2_cen", "w2_high", "w2_low"))
        x3_high, x3_low, hi_ok, lo_dve, lo_pool, zg_ok = (sem(n) for n in ("x3_high", "x3_low", "hi_ok", "lo_dve", "lo_pool", "zg_ok"))
        qkv_ps, bn_var, bn_root, bn_ok, pre_ok, spike_ok = (sem(n) for n in
                                                            ("qkv_ps", "bn_var", "bn_root", "bn_ok", "pre_ok", "spike_ok"))
        vt_ps, vt_sb, sc_first, sc_ps, sc_sb, av_ps, av_even, os_ok = (sem(n) for n in
                                                    ("vt_ps", "vt_sb", "sc_first", "sc_ps", "sc_sb", "av_ps", "av_even", "os_ok"))
        proj_ps, h2_ok, x3_ok = sem("proj_ps"), sem("h2_ok"), sem("x3_ok")
        h2t_ps, lg_ps, lg_sb, gap, gexp, gate_ok, wT_ps, wT_sb = (sem(n) for n in (
            "h2t_ps", "lg_ps", "lg_sb", "gap", "gexp", "gate_ok", "wT_ps", "wT_sb"))
        w2m_ok, out_ok, z_last = sem("w2m_ok"), sem("out_ok"), sem("z_last")
        w1_slot, w2_slot, b1_slot = ([sem(f"{n}_slot{i}") for i in range(2)] for n in ("w1", "w2", "b1"))
        g_ps, relu_ok, mm2_done, ysum_ok, turn_ps, ssq_ok, froot, z_ok, acc_ok, fch, ffac = (sem(n) for n in (
            "g_ps", "relu_ok", "mm2_done", "ysum_ok", "turn_ps", "ssq_ok", "froot", "z_ok", "acc_ok", "fch", "ffac"))
        beta_ps, beta_sb, s_out = sem("beta_ps"), sem("beta_sb"), sem("s_out")
        dve_own, act_own = sem("dve_own"), sem("act_own")

        def gather(copy, k):
            m, c = k // 3, k % 3
            pix = xin[:, 1 + 8 * m:9 + 8 * m, CH:CH + IMG * CH].rearrange("p r (j w c) -> p j r w c", w=PATCH, c=CH)
            return copy(own_px[:, k, :, :].rearrange("p j (r w) -> p j r w", w=PATCH), pix[:, :, :, :, c])

        block = ctx.enter_context(nc.Block())

        @block.sync
        def _(sp):
            bands = x.rearrange("b (i r) w c -> (b i) r (w c)", r=PATCH)
            wq = conv_w.rearrange("i j c d -> (i j) (c d)")
            for m in range(2):
                nc.sync.dma_start(xin[:, 1 + 8 * m:9 + 8 * m, CH:CH + IMG * CH],
                                  bands[:, 8 * m:8 * m + 8, :]).then_inc(s_x[m], 16)
                if m == 0:
                    nc.sync.dma_start(cst[:, :], consts).then_inc(s_cst, 16)
                else:
                    sides = (conv_w[:, 0, 3:6, :], conv_w[:, PATCH - 1, 6:9, :], conv_w[0, :, 9:12, :],
                             conv_w[PATCH - 1, :, 12:15, :])
                    for s, w in enumerate(sides):
                        nc.sync.dma_start(wk[16 * s:16 * s + 16, 6:8, :], w[:, 0:3:2, :]).then_inc(s_whalo, 16)
                        nc.sync.dma_start(wk[64 + 16 * s:80 + 16 * s, 6, :], w[:, 1, :]).then_inc(s_whalo, 16)
                sp.wait_ge(wpads, 2 * m + 2)
                for s, step in ((0, 0), (1, 1), (2, -1), (3, PATCH), (4, -PATCH)):
                    lo, hi = max(0, 128 * m + step), min(256, 128 * m + 128 + step)
                    nc.sync.dma_start(wsh[lo - step - 128 * m:hi - step - 128 * m, s, m, :],
                                      wq[lo:hi, 3 * s * D:(3 * s + 3) * D]).then_inc(s_w[m][s], 16)
                if m == 0:
                    sp.wait_ge(pads, 2)
                    nc.sync.dma_start(xin[1:96, 0, CH:CH + IMG * CH], bands[0:95, PATCH - 1, :]).then_inc(s_halo_rows, 16)
                    nc.sync.dma_start(xin[0:95, PATCH + 1, CH:CH + IMG * CH], bands[1:96, 0, :]).then_inc(s_halo_rows, 16)
            nc.sync.dma_start(wt[:, 0:3, :], wqkv.rearrange("(k p) c -> p k c", p=128)).then_inc(s_wt, 16)
            nc.sync.dma_start(wt[:, 3, :], wproj).then_inc(s_wt, 16)
            for row, v in ((V_CONVB, conv_b.rearrange("(a d) -> a d", a=1)), (V_TG, tok_g.rearrange("(a d) -> a d", a=1)),
                           (V_TB, tok_b.rearrange("(a d) -> a d", a=1)), (V_DENSEB, dense_b.rearrange("(a d) -> a d", a=1)),
                           (V_AG, attn_g.rearrange("(k d) -> k d", d=D)), (V_AB, attn_b.rearrange("(k d) -> k d", d=D)),
                           (V_BPROJ, bproj.rearrange("(a d) -> a d", a=1))):
                nc.sync.dma_start(vec[row:row + v.shape[0], :], v).then_inc(s_vec, 16)
            nc.sync.dma_start(dw[:, :], dense_w).then_inc(s_dw, 16)
            sp.wait_ge(xt_ps, 8)
            four = slice(0, E // 2)
            nc.sync.dma_start(raw[:, 1, :, :].rearrange("p e (f d) -> p e f d", d=D),
                              w2[four].rearrange("e (f p) d -> p e f d", p=128)).then_inc(four_w2, 16)
            nc.sync.dma_start(raw[:, 0, :, :], w1[four].rearrange("e p f -> p e f")).then_inc(four_w1, 16)

            nc.sync.dma_start(rw[:, :], router_w).then_inc(s_rw, 16)
            nc.sync.dma_start(gbc[:, :, :].rearrange("p e d -> p (e d)"),
                              ffn_g.rearrange("e d -> (e d)").partition_broadcast(128)).then_inc(s_gb, 16)
            nc.sync.dma_start(fb[:, :], ffn_b).then_inc(s_gb, 16)

            def fill_first(e, slot):
                src = parts[:, e, 0:2, :] if isinstance(e, int) else parts[:, bass.ds(e, 1), 0:2, :].rearrange("p o k f -> p (o k) f")
                nc.sync.dma_start(slot_w[:, slot, 0:2, :].bitcast(F32), src.bitcast(F32)).then_inc(w1_slot[slot], 16)
                nc.sync.dma_start(b1s[:, slot, :], vecT[:, bass.ds(e * FT + V_B1, FT)]).then_inc(b1_slot[slot], 16)

            def fill_second(e, slot):
                src = parts[:, e, 2:4, :] if isinstance(e, int) else parts[:, bass.ds(e, 1), 2:4, :].rearrange("p o k f -> p (o k) f")
                nc.sync.dma_start(slot_w[:, slot, 2:4, :].bitcast(F32), src.bitcast(F32)).then_inc(w2_slot[slot], 16)

            def load(e):
                sp.wait_ge(w2_cen, e + 1)
                nc.sync.dma_start(raw[:, 1, e, :].rearrange("p (f d) -> p f d", d=D),
                                  w2[e + E // 2].rearrange("(f p) d -> p f d", p=128)).then_inc(s_w2[e + E // 2], 16)
                sp.wait_ge(w1_low, e + 1)
                nc.sync.dma_start(raw[:, 0, e, :], w1[e + E // 2]).then_inc(s_w1[e + E // 2], 16)

            for e in range(2):
                sp.wait_ge(w1_low, e + 1)
                sp.wait_ge(w1_high, e + 1)
                fill_first(e, e)
                sp.wait_ge(w2_low, e + 1)
                sp.wait_ge(w2_high, e + 1)
                fill_second(e, e)
                load(e)
            load(2)
            load(3)
            sp.wait_ge(w1_low, E)
            sp.wait_ge(w1_high, E)
            sp.wait_ge(w2_low, E)
            sp.wait_ge(w2_high, E)
            with sp.Fori(0, E // 2 - 1) as i:
                for slot in range(2):
                    sp.wait_ge(relu_ok, i * (2 * FT) + (slot + 1) * FT)
                    fill_first(i * 2 + (slot + 2), slot)
                    sp.wait_ge(mm2_done, i * (2 * FT) + (slot + 1) * FT)
                    fill_second(i * 2 + (slot + 2), slot)

            rows = out.rearrange("b n d -> (b n) d")
            sp.wait_ge(out_ok, 1)
            nc.sync.dma_start(rows[512:TOK, :], acc[0:TOK - 512, 4, :]).then_inc(s_out, 16)
            sp.wait_ge(out_pool, 1)
            sp.wait_ge(out_ok, 2)
            nc.sync.dma_start(rows[0:256, :].rearrange("(t p) d -> p t d", p=128), acc[:, 0:2, :]).then_inc(s_out, 16)
            sp.wait_ge(out_ok, 4)
            nc.sync.dma_start(rows[256:512, :].rearrange("(t p) d -> p t d", p=128), acc[:, 2:4, :]).then_inc(s_out, 16)
            sp.wait_ge(s_out, 16 * 3)

        @block.gpsimd
        def _(pool):
            for s, rows, m in ((2, slice(0, 32), 0), (4, slice(0, 32), 0), (1, slice(96, 128), 1), (3, slice(96, 128), 1)):
                nc.gpsimd.memset(wsh[rows, s, m, :], 0.0).then_inc(wpads, 1)
            for row, v in ((V_B1, b1.rearrange("e (f p) -> (e f) p", p=128)), (V_B2, b2),
                           (V_CLS, cls_tok.rearrange("a b d -> (a b) d"))):
                nc.gpsimd.dma_start(vec[row:row + v.shape[0], :], v).then_inc(s_vec_pool, 16)
            xw = xin[:, :, :].rearrange("p r (w c) -> p r w c", c=CH)
            pool.wait_ge(pads, 3)
            pool.wait_ge(s_cst, 16)
            pool.wait_ge(s_halo_rows, 32)
            for side, row, mask in ((2, 0, C_TOP), (3, PATCH + 1, C_BOTTOM)):
                for c in range(CH):
                    nc.gpsimd.tensor_scalar(
                        halo[:, :, c, side, :],
                        xw[:, row, 1:IMG + 1, c].rearrange("p (j w) -> p j w", w=PATCH),
                        cst[0:96, mask:mask + 1], None, ALU.mult).then_inc(halo_ok, 1)
            pool.wait_ge(s_x[0], 16)
            pool.wait_ge(s_x[1], 16)
            for side, col in ((0, 0), (1, PATCH + 1)):
                for c in range(CH):
                    nc.gpsimd.tensor_copy(
                        halo[:, :, c, side, :],
                        xw[:, 1:PATCH + 1, col:col + PATCH * (SIDE - 1) + 1:PATCH, c].rearrange("p r j -> p j r")
                    ).then_inc(halo_ok, 1)
            pool.wait_ge(small_sb, 3)
            pool.wait_ge(tails, 8)
            nc.gpsimd.tensor_scalar(H[:, :, 0], sq[:, 0:B], 0.0, vecT[:, V_CLS:V_CLS + 1], ALU.mult, ALU.add).then_inc(h_ok, 1)
            nc.gpsimd.tensor_scalar(Hc[:, :, 0], sq[:, 0:B], 0.0, vecC[:, V_CLS:V_CLS + 1], ALU.mult, ALU.add).then_inc(h_ok, 1)

            def remainder(part):
                pool.wait_ge(wpart_ok, part + 1)
                left = wrem[:, part - 1, :, :] if part else wtT[:, :, :]
                nc.gpsimd.tensor_tensor(wrem[:, part, :, :], left, wpart[:, part, :, :], ALU.subtract).then_inc(wrem_ok, 1)

            for e in range(E):
                at = e % (E // 2)
                pool.wait_ge(s_w2[e], 16)
                pool.wait_ge(w2m_ok, e + 1)
                if e >= 2:
                    pool.wait_ge(w2_high, e - 1)
                nc.gpsimd.tensor_tensor(cen[:, e % 2, :].rearrange("p (f d) -> p f d", d=D),
                                        raw[:, 1, at, :].rearrange("p (f d) -> p f d", d=D),
                                        w2m[:, e, :].unsqueeze(2).to_broadcast([128, FT, D]), ALU.subtract).then_inc(w2_cen, 1)
                if e < 2:
                    remainder(e)
                pool.wait_ge(s_w1[e], 16)
                pool.wait_ge(w1_high, e + 1)
                nc.gpsimd.tensor_tensor(parts[:, e, 1, :], raw[:, 0, at, :], parts[:, e, 0, :].bitcast(F32),
                                        ALU.subtract).then_inc(w1_low, 1)
                pool.wait_ge(w2_high, e + 1)
                nc.gpsimd.tensor_tensor(parts[:, e, 3, :], cen[:, e % 2, :], parts[:, e, 2, :].bitcast(F32),
                                        ALU.subtract).then_inc(w2_low, 1)

            def low(e, f, begin=False):
                pool.wait_ge(hi_ok, e * FT + (f + 1))
                if not begin:
                    pool.wait_ge(mm2_done, e * FT + (f + 1 - FT))
                nc.gpsimd.tensor_tensor(hs[:, 1, f, :], rel[:, f, :], hs[:, 0, f, :].bitcast(F32),
                                        ALU.subtract).then_inc(lo_pool, 1)

            def gamma(e):
                pool.wait_ge(z_ok, e + 2)
                pool.wait_ge(acc_ok, e + 1)
                row = gbc[:, e:e + 1, :] if isinstance(e, int) else gbc[:, bass.ds(e, 1), :]
                nc.gpsimd.tensor_tensor(zg[:, :, :], z[:, :, :], row.to_broadcast([128, TILES, D]), ALU.mult).then_inc(zg_ok, 1)

            def add(e):
                pool.wait_ge(zg_ok, e + 2)
                nc.gpsimd.tensor_tensor(acc[:, :, :], acc[:, :, :], zg[:, :, :], ALU.add).then_inc(acc_ok, 1)

            low(0, 1, begin=True)
            low(0, 3, begin=True)
            low(1, 1)
            low(1, 3)
            pool.wait_ge(s_gb, 32)
            with pool.Fori(0, E - 3) as e:
                low(e + 2, 1)
                gamma(e)
                low(e + 2, 3)
                add(e)
            low(E - 1, 1)
            gamma(E - 3)
            add(E - 3)
            gamma(E - 2)
            pool.wait_ge(beta_sb, 1)
            add(E - 2)
            pool.wait_ge(acc_ok, E)
            pool.wait_ge(z_last, 1)
            nc.gpsimd.tensor_tensor(acc[:, 0, :], acc[:, 0, :], z[:, 0, :], ALU.add).then_inc(out_pool, 1)

        @block.tensor
        def _(pe):
            pe.wait_ge(s_cst, 16)

            def stay_awake(n, bank):
                for _ in range(n):
                    nc.tensor.matmul(PS[:, bank, BANK - 128:BANK], ident, ident, start=True, stop=True)

            def turn(k):
                if k >= 2:
                    pe.wait_ge(xt_sb, k - 1)
                for j in range(SIDE):
                    if k < 6:
                        pix, rows = own_px[:, k, j, :], 128
                    elif k == 6:
                        pix, rows = halo[:, j, 0:2, :, :].rearrange("p c s i -> p (c s i)"), 128
                    else:
                        pix, rows = halo[:, j, 2, :, :].rearrange("p s i -> p (s i)"), 64
                    mm = nc.tensor.transpose(PS[0:rows, 2 * (k % 2) + j // 3, 96 * (j % 3):96 * (j % 3) + 96], pix,
                                             ident[0:96, 0:96])
                mm.then_inc(xt_ps, 1)

            def turn_own(k):
                pe.wait_ge(px_dve if k % 3 == 2 else px_act, 1 + k // 3 if k % 3 == 2 else 2 * (k // 3) + k % 3 + 1)
                turn(k)

            for k in range(3):
                turn_own(k)
            stay_awake(3, 5)
            for at, k in enumerate(ORDER):
                if at == 2:
                    turn_own(3)
                    turn_own(4)
                if at == 3:
                    turn_own(5)
                    pe.wait_ge(halo_ok, 12)
                    turn(6)
                    turn(7)
                if at == 5:
                    pe.wait_ge(s_wt, 32)
                    for v in range(4):
                        mm = nc.tensor.transpose(PS[:, 5, 128 * v:128 * v + 128], wt[:, v, :], ident)
                    mm.then_inc(small_ps, 1)
                    pe.wait_ge(s_vec, 112)
                    pe.wait_ge(s_vec_pool, 48)
                    nc.tensor.transpose(PS[:, 4, 0:NV], vec[0:NV, :], ident[0:NV, 0:NV]).then_inc(small_ps, 1)
                if at == 7:
                    pe.wait_ge(small_sb, 2)
                    nc.tensor.matmul(PS[:, 4, 128:128 + NV], centre, vecT[:, :], start=True, stop=True).then_inc(small_ps, 1)
                pe.wait_ge(wk_ok, at + 1)
                pe.wait_ge(xt_sb, k + 1)
                rows = 128 if k < 7 else 64
                for n, (a, b) in enumerate(PCUTS):
                    mm = nc.tensor.matmul(PS[:, 6 + n, 0:b - a], wkc[0:rows, k, :], XT[0:rows, k, a:b],
                                          start=(at == 0), stop=(at == 7))
            mm.then_inc(conv_ps, 1)
            pe.wait_ge(s_dw, 16)
            pe.wait_ge(small_sb, 3)
            nc.tensor.matmul(PS[:, 4, 200:201], dw[:, :], vecT[:, V_TB:V_TB + 1], start=True, stop=True).then_inc(small_ps, 1)

            def squares(n, bank):
                for t in range(TILES):
                    if t in (0, 2):
                        pe.wait_ge(sq_ok, 2 * n - 1 + t // 2)
                    mm = nc.tensor.matmul(PS[:, bank, t:t + 1], sq[:, 128 * t:128 * t + 128], ones[:, :], start=True, stop=True)
                mm.then_inc(var_ps, 1)

            def spread(n, bank):
                for t in range(TILES):
                    if t < 3:
                        pe.wait_ge(diag_ok, 3 * (n - 1) + t + 1)
                    else:
                        pe.wait_ge(diag_act, (TILES - 3) * (n - 1) + t - 2)
                    mm = nc.tensor.matmul(tile5(bank, t), twos[:, :], diag[:, t, :], start=True, stop=True)
                mm.then_inc(bc_ps, 1)

            stay_awake(3, 1)
            squares(1, 5)
            pe.wait_ge(y_ok, 1)
            pe.wait_ge(dense_ok, 2)
            for v in (1, 0):
                for n, (a, b) in enumerate(PCUTS):
                    mm = nc.tensor.matmul(PS[:, 2 * v + n, 0:b - a], dwg[:, v, :], ysb[:, a:b], start=True, stop=True)
                mm.then_inc(t_ps, 1)
                if v == 1:
                    pe.wait_ge(small_sb, 4)
                    nc.tensor.matmul(PS[:, 4, 202:203], centre, c0[:, 0:1], start=True, stop=True).then_inc(small_ps, 1)
            pe.wait_ge(small_sb, 5)
            stay_awake(3, 7)
            spread(1, 4)
            stay_awake(9, 7)
            squares(2, 6)
            stay_awake(6, 7)
            spread(2, 4)
            stay_awake(8, 7)
            pe.wait_ge(wpart_ok, 3)
            for which, bank in ((1, 0), (0, 2), (2, 6)):
                for n in range(2):
                    pe.wait_ge(xs_ok, n + 1)
                    for part in range(3):
                        mm = nc.tensor.matmul(PS[:, bank + n, 0:TOK // 2], wpart[:, part, which, :], xs[:, HALVES[n]],
                                              start=(part == 0), stop=(part == 2))
                    mm.then_inc(qkv_ps, 1)

            def scores(pr, bank, at, hps=range(4)):
                for half in range(2):
                    col = NT * (2 * pr + half)
                    for hp in hps:
                        mm = nc.tensor.matmul(PS[64 * half:64 * half + 64, bank[hp], at:at + 2 * NT],
                                              kvs[32 * hp:32 * hp + 32, 0, col:col + 64],
                                              qe[32 * hp:32 * hp + 32, :, col:col + NT], start=True, stop=True)
                return mm

            stay_awake(26, 4)
            pe.wait_ge(spike_ok, 3)
            pe.wait_ge(pre_ok, 2)
            for pr in range(EARLY):
                mm = scores(pr, range(4), 2 * NT * pr)
            mm.then_inc(sc_ps, 1)
            pe.wait_ge(pre_ok, 3)
            pe.wait_ge(spike_ok, 6)
            for n in range(PAIRS - EARLY):
                mm = scores(EARLY + n, LATE_BANKS, 2 * NT * n, (0,))
            mm.then_inc(sc_first, 1)
            for n in range(PAIRS - EARLY):
                mm = scores(EARLY + n, LATE_BANKS, 2 * NT * n, (1, 2))
            mm.then_inc(sc_ps, 1)
            pe.wait_ge(sc_first, 1)
            for n in range(PAIRS - EARLY):
                mm = scores(EARLY + n, LATE_BANKS, 2 * NT * (PAIRS - EARLY + n), (3,))
            mm.then_inc(sc_ps, 1)
            stay_awake(4, 5)
            pe.wait_ge(spike_ok, 7)
            for pr in range(PAIRS):
                for half in range(2):
                    col = NT * (2 * pr + half)
                    mm = nc.tensor.transpose(PS[64 * half:64 * half + 64, 5, 64 * pr:64 * pr + 64].bitcast(BF16),
                                             kvs[:, 1, col:col + 64], identb[:, :])
            mm.then_inc(vt_ps, 1)
            pe.wait_ge(sc_sb, 2)
            stay_awake(2, 3)
            for rnd in range(2):
                if rnd:
                    stay_awake(2, 3)
                pe.wait_ge(vt_sb, rnd + 1)
                for p in range(4):
                    pr = 4 * rnd + p
                    if rnd:
                        pe.wait_ge(sc_sb, 2 if pr < EARLY else 4)
                    for half in range(2):
                        rows = slice(64 * half, 64 * half + NT)
                        for hp in range(4):
                            mm = nc.tensor.matmul(
                                PS[32 * hp:32 * hp + 32, 2 * rnd + half, 2 * NT * p:2 * NT * p + 2 * NT],
                                vtok[rows, pr, 32 * hp:32 * hp + 32], A[rows, hp, pr, :], start=True, stop=True)
                mm.then_inc(av_ps, 1)
            stay_awake(8, 4)
            for which, bank in ((4, 6), (3, 4)):
                for n in range(2):
                    pe.wait_ge(os_ok, n + 1)
                    for part in range(3):
                        mm = nc.tensor.matmul(PS[:, bank + n, 0:TOK // 2], wpart[:, part, which, :],
                                              os_[:, HALVES[n]], start=(part == 0), stop=(part == 2))
                    mm.then_inc(proj_ps, 1)
            stay_awake(2, 1)
            squares(3, 0)
            stay_awake(6, 1)
            spread(3, 2)
            pe.wait_ge(h2_ok, 3)
            for t in range(TILES):
                n = min(128, TOK - 128 * t)
                mm = nc.tensor.transpose(tile5(6, t, n), H[:, :, :].rearrange("p b n -> p (b n)")[:, 128 * t:128 * t + n], ident)
            mm.then_inc(h2t_ps, 1)
            def exact(bank, w, x, start, stop, closed=None, begin=False):
                for n in range(2):
                    if closed is not None:
                        pe.wait_ge(ysum_ok, closed * 2 + (n - 1))
                    for k, (i, j) in enumerate(((0, 0), (1, 0), (0, 1))):
                        if begin and k != 1:
                            pe.wait_ge(x3_low if k else x3_high, n + 1)
                        mm = nc.tensor.matmul(PS[:, bank + n, 0:TOK // 2], w[i], x[j][:, n * TOK // 2:(n + 1) * TOK // 2],
                                              start=start and k == 0, stop=stop and k == 2)
                return mm

            def first(slot, f, begin=False):
                exact(2 * (f % 2), [slot_w[:, slot, k, 128 * f:128 * f + 128] for k in (0, 1)],
                      [X3p[:, k, :] for k in (0, 1)], True, True, begin=begin).then_inc(g_ps, 1)

            def second(slot, f, closed):
                exact(4, [slot_w[:, slot, k, 128 * f:128 * f + 128] for k in (2, 3)],
                      [hs[:, k, f, :] for k in (0, 1)], f == 0, f == FT - 1, closed).then_inc(mm2_done, 1)

            def turn_back(bank=6):
                for t in range(TILES):
                    mm = nc.tensor.transpose(tile5(bank, t), ysum[:, 128 * t:128 * t + 128], ident)
                mm.then_inc(turn_ps, 1)

            def window(pair, slot, begin=False, end=False):
                e = pair * 2 + slot
                for f in range(FT):
                    if f == 0:
                        pe.wait_ge(relu_ok, e * FT + 2)
                        first(slot, FT - 1)
                        if not end:
                            pe.wait_ge(w1_slot[1 - slot], pair * 16 + 16 * (1 + slot))
                    if f < 3 and not end:
                        pe.wait_ge(relu_ok, e * FT + (f + 3))
                        first(1 - slot, f)
                    if end and f == 0:
                        pe.wait_ge(gate_ok, 1)
                        pe.wait_ge(relu_ok, E * FT - 1)
                        for t in range(TILES):
                            mm = nc.tensor.transpose(tile5(0, t, E), W8[:, t, :], ident)
                        mm.then_inc(wT_ps, 1)
                    if f == 0:
                        pe.wait_ge(w2_slot[slot], pair * 16 + 16)
                    pe.wait_ge(hi_ok, e * FT + (f + 1))
                    if end and f == FT - 1:
                        pe.wait_ge(lo_dve, E * 2 + 1)
                    elif f % 2:
                        pe.wait_ge(lo_pool, e * 2 + (f // 2 + 1))
                    else:
                        pe.wait_ge(lo_dve, e * 2 + (f // 2 + 1))
                    second(slot, f, None if begin or f else e)
                    if f == 0 and not begin:
                        pe.wait_ge(z_ok, e)
                        turn_back()

            pe.wait_ge(w1_slot[0], 16)
            pe.wait_ge(bc_ps, 3)
            first(0, 0, begin=True)
            first(0, 1)
            pe.wait_ge(x3_ok, 2)
            pe.wait_ge(s_rw, 16)
            for t in range(TILES):
                mm = nc.tensor.matmul(PS[:, 5, E * t:E * t + E], X3[:, 128 * t:128 * t + 128], rw[:, :], start=True, stop=True)
            mm.then_inc(lg_ps, 1)
            pe.wait_ge(relu_ok, 1)
            first(0, 2)
            pe.wait_ge(lg_sb, 1)
            window(0, 0, begin=True)
            with pe.Fori(0, E // 2 - 1) as i:
                window(i, 1)
                window(i + 1, 0)
            window(E // 2 - 1, 1, end=True)
            pe.wait_ge(relu_ok, E * FT)
            pe.wait_ge(s_gb, 32)
            pe.wait_ge(wT_sb, 1)
            for t in range(TILES):
                mm = nc.tensor.matmul(tile5(2, t), wT[:, 128 * t:128 * t + 128], fb[:, :], start=True, stop=True)
            mm.then_inc(beta_ps, 1)
            pe.wait_ge(ysum_ok, 2 * E)
            turn_back(0)
            pe.wait_ge(z_ok, E)
            turn_back(6)

        @block.scalar
        def _(act):
            def own_pixels(m):
                act.wait_ge(s_x[m], 16)
                for c in (0, 1):
                    gather(nc.scalar.copy, 3 * m + c).then_inc(px_act, 1)

            def evacuate(k):
                rows = 128 if k < 7 else 64
                act.wait_ge(xt_ps, k + 1)
                at = 2 * (k % 2)
                nc.scalar.copy(
                    XT[0:rows, k, :].rearrange("p (q b j) -> p b j q", j=3, b=2),
                    PS[0:rows, at:at + 2, 0:288].rearrange("p b (j q) -> p b j q", j=3)).then_inc(xt_sb, 1)

            act.wait_ge(tails, 1)
            nc.scalar.activation(junk[:, 0, 0:1], ones[:, :], ACT.Sqrt).then_inc(act_own, 1)
            own_pixels(0)
            evacuate(0)
            evacuate(1)
            evacuate(2)
            own_pixels(1)
            for k in range(3, 6):
                evacuate(k)
            evacuate(6)
            evacuate(7)
            act.wait_ge(small_ps, 1)
            nc.scalar.copy(wtT[:, 0:4, :], PS[:, 5, :].rearrange("p (k c) -> p k c", k=4)).then_inc(small_sb, 1)
            act.wait_ge(small_ps, 2)
            nc.scalar.copy(vecT[:, :], PS[:, 4, 0:NV]).then_inc(small_sb, 1)
            act.wait_ge(small_ps, 3)
            nc.scalar.copy(vecC[:, :], PS[:, 4, 128:128 + NV]).then_inc(small_sb, 1)

            def bf16_part(part):
                if part:
                    act.wait_ge(wrem_ok, part)
                src = wrem[:, part - 1, :, :] if part else wtT[:, :, :]
                nc.scalar.copy(wpart[:, part, :, :], src).then_inc(wpart_ok, 1)

            def means(e):
                act.wait_ge(s_w2[e], 16)
                for f in range(FT):
                    m = nc.scalar.activation(junk[:, f, :], raw[:, 1, e % (E // 2), 128 * f:128 * f + 128], ACT.Identity,
                                             scale=1.0 / D, accum_out=w2m[:, e, f:f + 1])
                m.then_inc(w2m_ok, 1)

            def high_first(e):
                act.wait_ge(s_w1[e], 16)
                nc.scalar.copy(parts[:, e, 0, :], raw[:, 0, e % (E // 2), :]).then_inc(w1_high, 1)

            def high_second(e):
                act.wait_ge(w2_cen, e + 1)
                nc.scalar.copy(parts[:, e, 2, :], cen[:, e % 2, :]).then_inc(w2_high, 1)

            act.wait_ge(conv_ps, 1)
            act.wait_ge(small_sb, 3)
            act.wait_ge(tails, 8)
            act.wait_ge(h_ok, 2)
            for half in range(2):
                cols = slice(half * PTOK // 2, (half + 1) * PTOK // 2)
                nc.scalar.activation(sq[:, cols], wide(6, PTOK)[:, cols], ACT.Square,
                                     bias=vecC[:, V_CONVB:V_CONVB + 1]).then_inc(sq_ok, 1)
            nc.scalar.activation(ysb[:, :], wide(6, PTOK), ACT.Identity, bias=vecC[:, V_CONVB:V_CONVB + 1]).then_inc(y_ok, 1)
            act.wait_ge(wcen_ok, 1)
            bf16_part(0)
            act.wait_ge(small_ps, 4)
            nc.scalar.activation(c0[:, 0:1], PS[:, 4, 200:201], ACT.Identity,
                                 bias=vecT[:, V_DENSEB:V_DENSEB + 1]).then_inc(small_sb, 1)

            def root(n):
                act.wait_ge(v_ok, n)
                nc.scalar.activation(r_s[:, :], r_v[:, :], ACT.Sqrt).then_inc(root_ok, 1)

            def last_diagonals(n):
                act.wait_ge(r_ok, n)
                for t in range(3, TILES):
                    nc.scalar.activation(diag[:, t, :], ident, ACT.Copy, scale=r_h[:, t:t + 1]).then_inc(diag_act, 1)

            root(1)
            act.wait_ge(t_ps, 1)
            nc.scalar.copy(h0[:, 1, :], wide(2, PTOK)).then_inc(t_sb, 1)
            act.wait_ge(small_ps, 5)
            nc.scalar.copy(c0[:, 1:2], PS[:, 4, 202:203]).then_inc(small_sb, 1)
            last_diagonals(1)
            tokens = sq[:, 0:TOK].rearrange("p (b n) -> p b n", b=B)
            nc.scalar.activation(tokens[:, :, 0], Hc[:, :, 0], ACT.Square)
            act.wait_ge(t_ps, 2)
            nc.scalar.copy(h0[:, 0, :], wide(0, PTOK)).then_inc(t_sb, 1)
            high_first(0)
            high_second(0)
            high_first(1)
            bf16_part(1)
            act.wait_ge(small_sb, 5)
            h1b = h1[:, :].rearrange("p (b n) -> p b n", b=B)
            for half in range(2):
                act.wait_ge(h0_ok, half + 1)
                b = slice(half * B // 2, (half + 1) * B // 2)
                nc.scalar.activation(tokens[:, b, 1:NT], h1b[:, b, :], ACT.Square, bias=c0[:, 1:2]).then_inc(sq_ok, 1)
            nc.scalar.activation(Hc[:, :, 1:NT], h1b, ACT.Identity, bias=c0[:, 1:2]).then_inc(h_ok, 1)
            root(2)
            high_second(1)
            act.wait_ge(h0_ok, 3)
            nc.scalar.activation(H[:, :, 1:NT], ysb[:, :].rearrange("p (b n) -> p b n", b=B), ACT.Identity,
                                 bias=c0[:, 0:1]).then_inc(h_ok, 1)
            last_diagonals(2)
            bf16_part(2)
            high_first(2)
            means(4)
            high_second(2)
            high_first(3)
            high_first(4)
            def bn_roots(lo, hi, n):
                act.wait_ge(bn_var, n)
                nc.scalar.activation(bn_s[:, 0, lo:hi], bnmv[:, lo:hi, 1], ACT.Sqrt,
                                     bias=cst[:, C_EPS + 1:C_EPS + 2]).then_inc(bn_root, 1)

            bn_roots(0, 2, 1)
            high_second(3)
            for which, bank in ((1, 0), (0, 2), (2, 6)):
                act.wait_ge(bn_ok, 2 if which == 2 else 1)
                nc.scalar.activation(in_halves(pre[:, which, :]), halves(bank), ACT.Relu, scale=bn_scale[:, which:which + 1],
                                     bias=bn_shift[:, which:which + 1]).then_inc(pre_ok, 1)
                if which == 1:
                    bn_roots(2, 3, 2)
            high_second(4)
            means(5)
            act.wait_ge(vt_ps, 1)
            for n in range(2):
                nc.scalar.copy(vtok[:, PAIRS // 2 * n:PAIRS // 2 * (n + 1), :].rearrange("p r d -> p (r d)"),
                               PS[:, 5, BANK // 2 * n:BANK // 2 * (n + 1)].bitcast(BF16)).then_inc(vt_sb, 1)
            high_first(5)

            def weighted_even(rnd):
                act.wait_ge(av_ps, rnd + 1)
                o = PS[:, 2 * rnd, 0:8 * NT].rearrange("p (r e n) -> p r e n", e=2, n=NT)
                nc.scalar.activation(av0[:, 2 * rnd, :, :], o[:, :, 0, :], ACT.Identity, scale=evens[:, 0:1],
                                     bias=cst[:, C_TIE:C_TIE + 1]).then_inc(av_even, 1)

            weighted_even(0)
            high_second(5)
            weighted_even(1)
            means(6)
            high_first(6)
            for half in range(2):
                act.wait_ge(h2_ok, half + 1)
                cols = slice(half * TOK // 2, (half + 1) * TOK // 2)
                nc.scalar.activation(sq[:, cols], Hc[:, :, :].rearrange("p b n -> p (b n)")[:, cols],
                                     ACT.Square).then_inc(sq_ok, 1)
            high_second(6)
            root(3)
            high_first(7)
            last_diagonals(3)
            means(7)
            for half in range(2):
                act.wait_ge(x3_ok, half + 1)
                nc.scalar.copy(X3p[:, 0, HALVES[half]], X3[:, HALVES[half]]).then_inc(x3_high, 1)
            act.wait_ge(h2t_ps, 1)
            nc.scalar.copy(acc[:, 0:4, :], PS[:, 6, :].rearrange("p (t d) -> p t d", d=D)).then_inc(acc_ok, 1)
            nc.scalar.copy(acc[0:TOK - 512, 4, :], PS[0:TOK - 512, 7, 0:D]).then_inc(z_ok, 1)
            high_second(7)

            def relu(e, slot, f, pair, begin=False):
                act.wait_ge(g_ps, e * FT + (f + 1))
                if f == 0:
                    act.wait_ge(b1_slot[slot], pair * 16 + 16)
                if not begin:
                    act.wait_ge(hi_ok, e * FT + (f + 1 - FT))
                    act.wait_ge(lo_pool if f % 2 else lo_dve, e * 2 + (f // 2 - 1))
                nc.scalar.activation(in_halves(rel[:, f, :]), halves(2 * (f % 2)), ACT.Relu, bias=b1s[:, slot, f:f + 1]).then_inc(relu_ok, 1)

            def statistics(e, bank=6):
                act.wait_ge(turn_ps, e + 1)
                for t in range(TILES):
                    nc.scalar.activation(junk[:, t, :], tile5(bank, t), ACT.Square,
                                         accum_out=ssq[:, t:t + 1]).then_inc(ssq_ok, 1)
                act.wait_ge(ssq_ok, e * TILES + TILES)
                nc.scalar.activation(f_s[:, 0, :], ssq[:, :], ACT.Sqrt, scale=1.0 / D,
                                     bias=cst[:, C_EPS + 2:C_EPS + 3]).then_inc(froot, 1)

            def scale(e):
                act.wait_ge(ffac, e + 1)
                act.wait_ge(zg_ok, e + 1)
                for t in range(TILES):
                    zt = nc.scalar.activation(z[:, t, :], tile5(6, t), ACT.Copy, scale=frw[:, t:t + 1])
                zt.then_inc(z_ok, 1)

            def window(pair, slot, begin=False, end=False):
                e = pair * 2 + slot
                relu(e, slot, 3, pair, begin)
                if not end:
                    relu(e + 1, 1 - slot, 0, pair + slot)
                if not begin:
                    statistics(e - 1)
                if end:
                    act.wait_ge(wT_ps, 1)
                    nc.scalar.copy(wT[:, :], wide(0, PAD)[0:E, :]).then_inc(wT_sb, 1)
                else:
                    relu(e + 1, 1 - slot, 1, pair + slot)
                    relu(e + 1, 1 - slot, 2, pair + slot)
                if not begin:
                    scale(e - 1)

            relu(0, 0, 0, 0, begin=True)
            relu(0, 0, 1, 0, begin=True)
            relu(0, 0, 2, 0, begin=True)
            window(0, 0, begin=True)
            act.wait_ge(gap, 1)
            nc.scalar.activation(gs[:, 3, :], gs[:, 2, :], ACT.Exp).then_inc(gexp, 1)
            act.wait_ge(gexp, 1)
            nc.scalar.activation(junk[:, 0, 0:1], cst[:, C_EPS:C_EPS + 1], ACT.Sqrt).then_inc(zg_ok, 1)
            act.wait_ge(zg_ok, 1)
            with act.Fori(0, E // 2 - 1) as i:
                window(i, 1)
                window(i + 1, 0)
            window(E // 2 - 1, 1, end=True)
            statistics(E - 1, 0)
            act.wait_ge(ffac, E)
            act.wait_ge(zg_ok, E)
            nc.scalar.activation(z[:, 0, :], last_g[:, 0, :], ACT.Copy, scale=frw[:, 0:1]).then_inc(z_last, 1)

        @block.vector
        def _(dve):
            own = Steps(dve, dve_own)

            for row in (0, PATCH + 1):
                nc.vector.memset(xin[:, row, :], 0.0).then_inc(pads, 1)
            nc.vector.memset(xin[:, 1:PATCH + 1, :].rearrange("p r (w c) -> p r w c", c=CH)[:, :, 0:IMG + 2:IMG + 1, :],
                             0.0).then_inc(pads, 1)
            for tile_, val in ((ones[:, :], 1.0), (twos[:, :], 2.0), (sq[:, :], 1.0), (kvs[:, :, TOK:PAD], 0.0),
                               (X3[:, TOK:PAD], 0.0), (ysum[:, TOK:PAD], 0.0), (acc[:, TILES - 1, :], 0.0)):
                nc.vector.memset(tile_, val).then_inc(tails, 1)
            def own_pixels(m):
                dve.wait_ge(s_x[m], 16)
                gather(nc.vector.tensor_copy, 3 * m + 2).then_inc(px_dve, 1)

            def centred(lo, hi, rows):
                own.then(nc.vector.tensor_reduce(mean8[0:rows, lo:hi], wk[0:rows, lo:hi, :], AX.X, ALU.add))
                own.then(nc.vector.tensor_scalar(nmean8[0:rows, lo:hi], mean8[0:rows, lo:hi], 1.0 / D, None, ALU.mult))
                nc.vector.tensor_tensor(wkc[0:rows, lo:hi, :], wk[0:rows, lo:hi, :],
                                        nmean8[0:rows, lo:hi].unsqueeze(2).to_broadcast([rows, hi - lo, D]),
                                        ALU.subtract).then_inc(wk_ok, hi - lo)

            own_pixels(0)
            dve.wait_ge(s_cst, 16)
            for m in range(2):
                flat = wk[:, 3 * m:3 * m + 3, :].rearrange("p c d -> p (c d)")
                dve.wait_ge(s_w[m][0], 16)
                for s in range(1, 5):
                    dve.wait_ge(s_w[m][s], 16)
                    if s < 3:
                        mask = cst[:, C_NOT_LAST:C_NOT_LAST + 1] if s == 1 else cst[:, C_NOT_FIRST:C_NOT_FIRST + 1]
                        own.then(nc.vector.scalar_tensor_tensor(flat, wsh[:, s, m, :], mask,
                                                                wsh[:, 0, m, :] if s == 1 else flat, ALU.mult, ALU.add))
                    else:
                        own.then(nc.vector.tensor_tensor(flat, wsh[:, s, m, :], flat, ALU.add))
                centred(3 * m, 3 * m + 3, 128)
                if m == 0:
                    own_pixels(1)
                    dve.wait_ge(s_whalo, 128)
                    centred(6, 7, 128)
                    centred(7, 8, 64)
            nc.vector.tensor_copy(identb[:, :], ident).then_inc(tails, 1)
            dve.wait_ge(s_dw, 16)
            dve.wait_ge(small_sb, 2)
            own.then(nc.vector.tensor_scalar(dwg[:, 0, :], dw[:, :], vecT[:, V_TG:V_TG + 1], None, ALU.mult))
            own.then(nc.vector.tensor_reduce(mean8[:, 0:1], dwg[:, 0, :], AX.X, ALU.add))
            own.then(nc.vector.tensor_scalar(nmean8[:, 0:1], mean8[:, 0:1], 1.0 / D, None, ALU.mult))
            nc.vector.tensor_scalar(dwg[:, 1, :], dwg[:, 0, :], nmean8[:, 0:1], None, ALU.subtract).then_inc(dense_ok, 2)
            dve.wait_ge(small_sb, 1)
            own.then(nc.vector.tensor_reduce(mean8[:, 1:2], wtT[:, 3, :], AX.X, ALU.add))
            own.then(nc.vector.tensor_scalar(nmean8[:, 1:2], mean8[:, 1:2], 1.0 / D, None, ALU.mult))
            nc.vector.tensor_scalar(wtT[:, 4, :], wtT[:, 3, :], nmean8[:, 1:2], None, ALU.subtract).then_inc(wcen_ok, 1)

            def row_means(e):
                dve.wait_ge(s_w2[e], 16)
                own.then(nc.vector.tensor_reduce(w2s[:, e, :], raw[:, 1, e % (E // 2), :].rearrange("p (f d) -> p f d", d=D),
                                                 AX.X, ALU.add))
                nc.vector.tensor_scalar(w2m[:, e, :], w2s[:, e, :], 1.0 / D, None, ALU.mult).then_inc(w2m_ok, 1)

            row_means(0)
            row_means(1)

            def factor(n, bank):
                dve.wait_ge(var_ps, n)
                nc.vector.tensor_scalar(r_v[:, :], PS[:, bank, 0:TILES], 1.0 / D, EPS[n - 1], ALU.mult, ALU.add).then_inc(v_ok, 1)
                dve.wait_ge(root_ok, n)
                own.then(nc.vector.reciprocal(r_a[:, :], r_s[:, :]))
                own.then(nc.vector.tensor_tensor(r_b[:, :], r_v[:, :], r_a[:, :], ALU.mult))
                own.then(nc.vector.tensor_tensor(r_c[:, :], r_b[:, :], r_s[:, :], ALU.add))
                nc.vector.reciprocal(r_h[:, :], r_c[:, :]).then_inc(r_ok, 1)
                dve.wait_ge(r_ok, n)
                for t in range(3):
                    nc.vector.tensor_scalar(diag[:, t, :], ident, r_h[:, t:t + 1], None, ALU.mult).then_inc(diag_ok, 1)

            factor(1, 5)
            row_means(2)
            row_means(3)
            dve.wait_ge(bc_ps, 1)
            dve.wait_ge(t_sb, 1)
            for half in range(2):
                cols = slice(half * PTOK // 2, (half + 1) * PTOK // 2)
                nc.vector.tensor_tensor(h1[:, cols], wide(4, PTOK)[:, cols], h0[:, 1, cols], ALU.mult).then_inc(h0_ok, 1)
            dve.wait_ge(t_sb, 2)
            nc.vector.tensor_tensor(ysb[:, :], wide(4, PTOK), h0[:, 0, :], ALU.mult).then_inc(h0_ok, 1)
            factor(2, 6)
            flat_c = Hc[:, :, :].rearrange("p b n -> p (b n)")
            flat_h = H[:, :, :].rearrange("p b n -> p (b n)")
            dve.wait_ge(bc_ps, 2)
            dve.wait_ge(h_ok, 3)
            for half in range(2):
                own.mark(nc.vector.scalar_tensor_tensor(spk[:, HALVES[half]], flat_c[:, HALVES[half]], 0.0,
                                                        wide(4, TOK)[:, HALVES[half]], ALU.max, ALU.mult))
            for half in range(2):
                dve.wait_ge(dve_own, own.n - 1)
                own.mark(nc.vector.tensor_scalar(spk2[:, HALVES[half]], spk[:, HALVES[half]], TIE, CAP, ALU.add, ALU.min))
            for half in range(2):
                dve.wait_ge(dve_own, own.n - 1 + half)
                nc.vector.tensor_scalar(xs[:, HALVES[half]], spk2[:, HALVES[half]], RNE, RNE, ALU.add,
                                        ALU.subtract).then_inc(xs_ok, 1)
            def stats(which, c, n, bank):
                dve.wait_ge(qkv_ps, 2 * n + c + 1)
                own.mark(nc.vector.bn_stats(bnst[:, which, c, :], PS[:, bank + c, 0:TOK // 2]))

            def moments(which):
                own.mark(nc.vector.bn_aggr(bnmv[:, which, :], bnst[:, which, :, :].rearrange("p c s -> p (c s)")))

            def norm_step(step, lo, hi):
                n = 2 if lo else 1
                mean, var = bnmv[:, lo:hi, 0], bnmv[:, lo:hi, 1]
                root, bn_v, bn_a, bn_b, bn_c, bn_h, bn_m = (bn_s[:, k, lo:hi] for k in range(7))
                if step == 1:
                    dve.wait_ge(bn_root, n)
                    dve.wait_ge(bn_var, n)
                else:
                    own.wait()
                if step == 0:
                    nc.vector.tensor_scalar(bn_v, var, EPS[1], None, ALU.add).then_inc(bn_var, 1)
                elif step == 1:
                    own.mark(nc.vector.reciprocal(bn_a, root))
                elif step == 2:
                    own.mark(nc.vector.tensor_tensor(bn_b, bn_v, bn_a, ALU.mult))
                elif step == 3:
                    own.mark(nc.vector.tensor_tensor(bn_c, bn_b, root, ALU.add))
                elif step == 4:
                    own.mark(nc.vector.reciprocal(bn_h, bn_c))
                elif step == 5:
                    own.mark(nc.vector.scalar_tensor_tensor(bn_scale[:, lo:hi], bn_h, 2.0, vecT[:, V_AG + lo:V_AG + hi],
                                                            ALU.mult, ALU.mult))
                elif step == 6:
                    own.mark(nc.vector.tensor_tensor(bn_m, mean, bn_scale[:, lo:hi], ALU.mult))
                else:
                    nc.vector.scalar_tensor_tensor(bn_shift[:, lo:hi], vecT[:, V_AB + lo:V_AB + hi], TIE, bn_m, ALU.add,
                                                   ALU.subtract).then_inc(bn_ok, 1)

            stats(1, 0, 0, 0)
            stats(1, 1, 0, 0)
            stats(0, 0, 1, 2)
            dve.wait_ge(dve_own, own.n - 1)
            moments(1)
            stats(0, 1, 1, 2)
            own.wait()
            moments(0)
            norm_step(0, 0, 2)
            stats(2, 0, 2, 6)
            for step in range(1, 8):
                norm_step(step, 0, 2)
            stats(2, 1, 2, 6)
            own.wait()
            moments(2)
            norm_step(0, 2, 3)
            def clip(which, cols):
                own.mark(nc.vector.tensor_scalar(pre2[:, which, cols], pre[:, which, cols], CAP, RNE, ALU.min, ALU.add))

            def round_kv(which, cols, back):
                dve.wait_ge(dve_own, own.n - back)
                nc.vector.tensor_scalar(kvs[:, which // 2, cols], pre2[:, which, cols], RNE, None,
                                        ALU.subtract).then_inc(spike_ok, 1)

            def round_q(odd, cols, back):
                dve.wait_ge(dve_own, own.n - back)
                mask = C_ODD if odd else C_EVEN
                nc.vector.tensor_scalar(qe[:, odd, cols], pre2[:, 0, cols], RNE, cst[:, mask:mask + 1],
                                        ALU.subtract, ALU.mult).then_inc(spike_ok, 1)

            k_first, k_rest = slice(0, K_FIRST), slice(K_FIRST, TOK)
            q_first, q_rest = slice(0, 2 * EARLY * NT), slice(2 * EARLY * NT, TOK)
            dve.wait_ge(pre_ok, 1)
            clip(1, k_first)
            norm_step(1, 2, 3)
            clip(1, k_rest)
            norm_step(2, 2, 3)
            round_kv(1, k_first, 3)
            norm_step(3, 2, 3)
            dve.wait_ge(pre_ok, 2)
            clip(0, q_first)
            norm_step(4, 2, 3)
            clip(0, q_rest)
            norm_step(5, 2, 3)
            round_q(0, q_first, 3)
            norm_step(6, 2, 3)
            round_q(1, q_first, 4)
            norm_step(7, 2, 3)
            round_kv(1, k_rest, 6)
            round_q(0, q_rest, 2)
            round_q(1, q_rest, 2)
            dve.wait_ge(pre_ok, 3)
            clip(2, slice(0, TOK))
            round_kv(2, slice(0, TOK), 0)
            dve.wait_ge(sc_ps, 1)
            for lo, hi in ((0, EARLY // 2), (EARLY // 2, EARLY)):
                nc.vector.tensor_scalar(A[:, :, lo:hi, :].rearrange("p g r n -> p g (r n)"),
                                        PS[:, 0:4, 2 * NT * lo:2 * NT * hi], CAP, None, ALU.min).then_inc(sc_sb, 1)
            late = 2 * NT * (PAIRS - EARLY)
            dve.wait_ge(sc_ps, 2)
            nc.vector.tensor_scalar(A[:, 1:3, EARLY:PAIRS, :].rearrange("p g r n -> p g (r n)"), PS[:, 6:8, 0:late],
                                    CAP, None, ALU.min).then_inc(sc_sb, 1)
            dve.wait_ge(sc_ps, 3)
            nc.vector.tensor_scalar(A[:, 0:4:3, EARLY:PAIRS, :].rearrange("p g r n -> p g (r n)"),
                                    PS[:, 4, 0:2 * late].rearrange("p (g n) -> p g n", g=2), CAP, None,
                                    ALU.min).then_inc(sc_sb, 1)
            for rnd in range(2):
                o = [PS[:, 2 * rnd + half, 0:8 * NT].rearrange("p (r e n) -> p r e n", e=2, n=NT) for half in range(2)]
                dve.wait_ge(av_ps, rnd + 1)
                own.mark(nc.vector.tensor_scalar(av0[:, 2 * rnd + 1, :, :], o[1][:, :, 0, :], evens[:, 0:1], TIE,
                                                 ALU.mult, ALU.add))
                for half in (1, 0):
                    if half:
                        own.wait()
                    else:
                        dve.wait_ge(av_even, rnd + 1)
                    own.mark(nc.vector.scalar_tensor_tensor(av[:, 8 * rnd + half:8 * rnd + 8:2, :], o[half][:, :, 1, :],
                                                            evens[:, 1:2], av0[:, 2 * rnd + half, :, :], ALU.mult, ALU.add))
            for half in range(2):
                dve.wait_ge(dve_own, own.n - (1 if half else 2))
                own.mark(nc.vector.tensor_scalar(av2[:, HALVES[half]], spk[:, HALVES[half]], CAP, RNE, ALU.min, ALU.add))
            for half in range(2):
                dve.wait_ge(dve_own, own.n - 1 + half)
                nc.vector.tensor_scalar(os_[:, HALVES[half]], av2[:, HALVES[half]], RNE, None, ALU.subtract).then_inc(os_ok, 1)
            for half in range(2):
                dve.wait_ge(proj_ps, half + 1)
                cols = slice(half * TOK // 2, (half + 1) * TOK // 2)
                nc.vector.scalar_tensor_tensor(flat_c[:, cols], PS[:, 6 + half, 0:TOK // 2], vecC[:, V_BPROJ:V_BPROJ + 1],
                                               flat_c[:, cols], ALU.add, ALU.add).then_inc(h2_ok, 1)
            dve.wait_ge(proj_ps, 4)
            nc.vector.scalar_tensor_tensor(in_halves(flat_h), halves(4), vecT[:, V_BPROJ:V_BPROJ + 1], in_halves(flat_h),
                                           ALU.add, ALU.add).then_inc(h2_ok, 1)
            factor(3, 0)
            dve.wait_ge(bc_ps, 3)
            for half in range(2):
                nc.vector.tensor_tensor(X3[:, HALVES[half]], wide(2, TOK)[:, HALVES[half]], flat_c[:, HALVES[half]],
                                        ALU.mult).then_inc(x3_ok, 1)
            for half in range(2):
                dve.wait_ge(x3_high, half + 1)
                nc.vector.tensor_tensor(X3p[:, 1, HALVES[half]], X3[:, HALVES[half]], X3p[:, 0, HALVES[half]].bitcast(F32),
                                        ALU.subtract).then_inc(x3_low, 1)

            def split(e, f, begin=False, end=False):
                dve.wait_ge(relu_ok, e * FT + (f + 1))
                if not begin:
                    dve.wait_ge(mm2_done, e * FT + (f + 1 - FT))
                nc.vector.tensor_copy(hs[:, 0, f, :], rel[:, f, :]).then_inc(hi_ok, 1)
                if f % 2 == 0 or end:
                    dve.wait_ge(hi_ok, e * FT + (f + 1))
                    nc.vector.tensor_tensor(hs[:, 1, f, :], rel[:, f, :], hs[:, 0, f, :].bitcast(F32),
                                            ALU.subtract).then_inc(lo_dve, 1)

            def bc(col):
                return col.unsqueeze(2).to_broadcast([128, TILES, E])

            split(0, 0, begin=True)
            split(0, 1, begin=True)
            dve.wait_ge(lg_ps, 1)
            nc.vector.tensor_copy(L[:, :, :], PS[:, 5, 0:TILES * E].rearrange("p (t e) -> p t e", e=E)).then_inc(lg_sb, 1)
            dve.wait_ge(lg_sb, 1)
            rank = cst[:, C_RANK:C_RANK + E].unsqueeze(1).to_broadcast([128, TILES, E])

            def best(level, values, top, pick):
                own.then(nc.vector.tensor_reduce(top, values, AX.X, ALU.max))
                own.then(nc.vector.tensor_tensor(g[0][:, :, :], values, bc(top), ALU.is_equal))
                own.then(nc.vector.tensor_tensor(g[1][:, :, :], g[0][:, :, :], rank, ALU.mult))
                own.then(nc.vector.tensor_reduce(gs[:, 5, :], g[1][:, :, :], AX.X, ALU.max))
                own.then(nc.vector.tensor_tensor(pick, g[1][:, :, :], bc(gs[:, 5, :]), ALU.is_equal))

            best(0, L[:, :, :], gs[:, 0, :], g[2][:, :, :])
            split(0, 2, begin=True)
            split(0, 3, begin=True)
            own.then(nc.vector.scalar_tensor_tensor(g[3][:, :, :], g[2][:, :, :], -3.0e38, L[:, :, :], ALU.mult, ALU.add))
            best(1, g[3][:, :, :], gs[:, 1, :], g[4][:, :, :])
            nc.vector.tensor_tensor(gs[:, 2, :], gs[:, 1, :], gs[:, 0, :], ALU.subtract).then_inc(gap, 1)
            def close_sum(e):
                dve.wait_ge(mm2_done, e * FT + FT)
                if not (isinstance(e, int) and e == 0):
                    dve.wait_ge(turn_ps, e)
                bias = vecC[:, V_B2 + e:V_B2 + e + 1] if isinstance(e, int) else vecC[:, bass.ds(e + V_B2, 1)]
                for half in range(2):
                    cols = slice(half * TOK // 2, (half + 1) * TOK // 2)
                    nc.vector.scalar_tensor_tensor(ysum[:, cols], PS[:, 4 + half, 0:TOK // 2], bias, X3[:, cols], ALU.add,
                                                   ALU.add).then_inc(ysum_ok, 1)

            def finish(e):
                dve.wait_ge(ssq_ok, e * TILES + TILES)
                nc.vector.tensor_scalar(f_s[:, 1, :], ssq[:, :], 1.0 / D, EPS[2], ALU.mult, ALU.add).then_inc(fch, 1)
                dve.wait_ge(froot, e + 1)
                nc.vector.reciprocal(f_s[:, 2, :], f_s[:, 0, :]).then_inc(fch, 1)
                dve.wait_ge(fch, e * 5 + 2)
                nc.vector.tensor_tensor(f_s[:, 3, :], f_s[:, 1, :], f_s[:, 2, :], ALU.mult).then_inc(fch, 1)
                dve.wait_ge(fch, e * 5 + 3)
                nc.vector.tensor_tensor(f_s[:, 4, :], f_s[:, 3, :], f_s[:, 0, :], ALU.add).then_inc(fch, 1)
                dve.wait_ge(fch, e * 5 + 4)
                nc.vector.reciprocal(f_s[:, 5, :], f_s[:, 4, :]).then_inc(fch, 1)
                dve.wait_ge(fch, e * 5 + 5)
                dve.wait_ge(z_ok, e + 1)
                gate = W8[:, :, e:e + 1] if isinstance(e, int) else W8[:, :, bass.ds(e, 1)]
                nc.vector.scalar_tensor_tensor(frw[:, :], f_s[:, 5, :], 2.0, gate.rearrange("p t o -> p (t o)"), ALU.mult,
                                               ALU.mult).then_inc(ffac, 1)

            def window(e, end=False):
                split(e, 3, end=end)
                finish(e - 1)
                if not end:
                    split(e + 1, 0)
                    split(e + 1, 1)
                close_sum(e)
                if not end:
                    split(e + 1, 2)

            split(1, 0)
            split(1, 1)
            close_sum(0)
            split(1, 2)
            dve.wait_ge(gexp, 1)
            own.then(nc.vector.tensor_scalar(gs[:, 4, :], gs[:, 3, :], 1.0, None, ALU.add))
            own.then(nc.vector.reciprocal(gs[:, 5, :], gs[:, 4, :]))
            own.then(nc.vector.tensor_tensor(gs[:, 4, :], gs[:, 3, :], gs[:, 5, :], ALU.mult))
            own.then(nc.vector.tensor_tensor(g[0][:, :, :], g[2][:, :, :], bc(gs[:, 5, :]), ALU.mult))
            own.then(nc.vector.tensor_tensor(g[1][:, :, :], g[4][:, :, :], bc(gs[:, 4, :]), ALU.mult))
            nc.vector.tensor_tensor(W8[:, :, :], g[0][:, :, :], g[1][:, :, :], ALU.add).then_inc(gate_ok, 1)
            dve.wait_ge(gate_ok, 1)
            with dve.Fori(0, E // 2 - 1) as i:
                window(i * 2 + 1)
                window(i * 2 + 2)
            window(E - 1, end=True)
            dve.wait_ge(beta_ps, 1)
            dve.wait_ge(acc_ok, E - 1)
            nc.vector.tensor_tensor(acc[:, :, :].rearrange("p t d -> p (t d)"), wide(2, PAD),
                                    acc[:, :, :].rearrange("p t d -> p (t d)"), ALU.add).then_inc(beta_sb, 1)
            dve.wait_ge(turn_ps, E + 1)
            own.then(nc.vector.tensor_tensor(last_g[:, 0:4, :], PS[:, 6, :].rearrange("p (t d) -> p t d", d=D),
                                             gbc[:, E - 1:E, :].to_broadcast([128, 4, D]), ALU.mult))
            own.then(nc.vector.tensor_tensor(last_g[:, 4, :], PS[:, 7, 0:D], gbc[:, E - 1, :], ALU.mult))
            finish(E - 1)
            dve.wait_ge(ffac, E)
            dve.wait_ge(acc_ok, E)
            for t in (4, 1, 2, 3):
                nc.vector.scalar_tensor_tensor(acc[:, t, :], last_g[:, t, :], frw[:, t:t + 1], acc[:, t, :], ALU.mult,
                                               ALU.add).then_inc(out_ok, 1)


_INS = ['x', 'cls_tok', 'L0_tok_conv_w', 'L0_tok_conv_b', 'L0_tok_gamma', 'L0_tok_beta', 'L0_tok_dense_w',
        'L0_tok_dense_b', 'L0_attn_Wqkv', 'L0_attn_gamma', 'L0_attn_beta', 'L0_attn_Wproj', 'L0_attn_bproj',
        'L0_ffn_router_w', 'L0_ffn_w1', 'L0_ffn_b1', 'L0_ffn_w2', 'L0_ffn_b2', 'L0_ffn_gamma', 'L0_ffn_beta']


def kernel(**inputs):
    import concourse.bacc as _bacc
    from concourse.bass_utils import run_bass_kernel_spmd as _run

    nc = _bacc.Bacc("TRN2", target_bir_lowering=False, num_devices=1)
    arrays = {"consts_dram": constants()}
    for name in _INS:
        arrays[f"in_{name}_dram"] = np.ascontiguousarray(inputs[name])
    args = [nc.dram_tensor(n, a.shape, F32, kind="ExternalInput").ap() for n, a in arrays.items()]
    out = nc.dram_tensor("out_dram", (B, NT, D), F32, kind="ExternalOutput").ap()
    vit_layer(nc, *args, out)
    r = _run(nc, [arrays], core_ids=[0])
    return r.results[0]["out_dram"]
```
